# Optimizing a Trainium2 kernel written in Bass

```python
import numpy as np
import jax
import jax.numpy as jnp

def _softmax(x, axis=-1):
    return jax.nn.softmax(x, axis=axis)

def _gelu(x):
    return jax.nn.gelu(x, approximate=True)

def _silu(x):
    return jax.nn.silu(x)

def _sigmoid(x):
    return jax.nn.sigmoid(x)

def _layernorm(x, axis=-1, eps=1e-05):
    m = jnp.mean(x, axis=axis, keepdims=True)
    v = jnp.var(x, axis=axis, keepdims=True)
    return (x - m) / jnp.sqrt(v + eps)

def _scatter_add(tgt, idx, src, axis=0):
    return tgt.at[idx].add(src)

def _segment_sum(src, seg, n):
    return jax.ops.segment_sum(src, seg, n)
kernel_name = 'mk_flamingo_gated_d2_seqx_r8_327a75'

def setup_inputs(seed: int=0):
    np.random.seed(seed)
    _w = jnp.asarray

    def _rec_inputs():
        import jax
        import jax.numpy as jnp
        _rk = jax.random.key(seed)
        x = 0.002226 + 0.9996 * jax.random.normal(jax.random.fold_in(_rk, 1), (16, 128, 128), jnp.float32)
        _lenS = 128 - jax.random.randint(jax.random.fold_in(_rk, 7), (16,), 0, max(1, 128 // 4) + 1, jnp.int32)
        _lenS2 = 77 - jax.random.randint(jax.random.fold_in(_rk, 8), (16,), 0, max(1, 77 // 4) + 1, jnp.int32)
        _ctx_1024P = jax.random.normal(jax.random.fold_in(_rk, 11), (16, 16, 128), jnp.float32)
        _ctx_1024c = jax.random.dirichlet(jax.random.fold_in(_rk, 511), 0.3 * jnp.ones((16,), jnp.float32), (16, 77))
        _ctx_1024t = jnp.einsum('bsk,bkd->bsd', _ctx_1024c, _ctx_1024P)
        _ctx_1024t = _ctx_1024t * jax.lax.rsqrt(jnp.mean(jnp.square(_ctx_1024t)) + 1e-12) * 0.953939
        ctx_1024 = -0.000125008 + 0.999885 * (_ctx_1024t + 0.3 * jax.random.normal(jax.random.fold_in(_rk, 611), (16, 77, 128), jnp.float32))
        _validS = jnp.arange(128)[None, :] < _lenS[:, None]
        _validS2 = jnp.arange(77)[None, :] < _lenS2[:, None]
        _causal = jnp.tril(jnp.ones((128, 128), dtype=bool))
        mask_BxS2_bk0 = jnp.logical_not(jnp.broadcast_to(_validS2[:, :], (16, 77)))
        _g = jax.random.normal(jax.random.fold_in(_rk, 9001), (2, 2), jnp.float32)
        _g = jnp.sign(_g) * jnp.maximum(jnp.abs(_g), 1.0) + (_g == 0) * 1.0
        g_xattn = _g[0]
        g_ffn = _g[1]
        return (x, ctx_1024, mask_BxS2_bk0, g_xattn, g_ffn)
    x, ctx_1024, mask_BxS2_bk0, g_xattn, g_ffn = _rec_inputs()

    def _L0_xattn_setup():
        import jax, jax.numpy as jnp
        import numpy as np
        EPS = 1e-05

        def layer_norm(x, g, b):
            mu = jnp.mean(x, axis=-1, keepdims=True)
            var = jnp.mean((x - mu) ** 2, axis=-1, keepdims=True)
            return (x - mu) * jax.lax.rsqrt(var + EPS) * g + b
        key = jax.random.key(seed)
        ks = jax.random.split(key, 8)
        b, n, l, D = (8, 512, 64, 128)
        heads, dim_head = (16, 64)
        inner = heads * dim_head
        x = jax.random.normal(ks[0], (b, n, D), dtype=jnp.float32)
        latents = jax.random.normal(ks[1], (b, l, D), dtype=jnp.float32)
        mask = jax.random.randint(ks[2], (b, n), 0, 2) > 0
        Wq = jax.random.normal(ks[3], (D, inner), dtype=jnp.float32) * D ** (-0.5)
        Wkv = jax.random.normal(ks[4], (D, 2 * inner), dtype=jnp.float32) * D ** (-0.5)
        Wout = jax.random.normal(ks[5], (inner, D), dtype=jnp.float32) * inner ** (-0.5)
        g1 = jnp.ones((D,), jnp.float32)
        b1 = jnp.zeros((D,), jnp.float32)
        g2 = jnp.ones((D,), jnp.float32)
        b2 = jnp.zeros((D,), jnp.float32)
        return {'x': x, 'latents': latents, 'mask': mask, 'g1': g1, 'b1': b1, 'g2': g2, 'b2': b2, 'Wq': Wq, 'Wkv': Wkv, 'Wout': Wout}
    _L0_xattn_all = _L0_xattn_setup()
    _L0_xattn_in = {k: v for k, v in _L0_xattn_all.items() if k in ('g1', 'b1', 'g2', 'b2', 'Wq', 'Wkv', 'Wout')}
    del _L0_xattn_all

    def _L0_ffn_setup():
        import jax, jax.numpy as jnp
        import numpy as np
        D_MODEL = 128
        EXPANSION = 4
        D_HIDDEN = D_MODEL * EXPANSION
        NUM_STAGES = int(np.log2(D_HIDDEN))

        def butterfly(y, weights, dim):
            lead = y.shape[:-1]
            for stage in range(weights.shape[0]):
                s = 2 ** stage
                nb = dim // (2 * s)
                yr = y.reshape(*lead, nb, 2, s)
                a = yr[..., 0, :]
                b = yr[..., 1, :]
                w = weights[stage].reshape(nb, s, 2, 2)
                na = w[..., 0, 0] * a + w[..., 0, 1] * b
                nb2 = w[..., 1, 0] * a + w[..., 1, 1] * b
                y = jnp.stack([na, nb2], axis=-2).reshape(*lead, dim)
            return y
        key = jax.random.key(seed)
        ks = jax.random.split(key, 6)
        B, S = (4, 256)
        x = jax.random.normal(ks[0], (B, S, D_MODEL), jnp.float32)
        W_exp = jax.random.normal(ks[1], (D_MODEL, D_HIDDEN), jnp.float32) * 0.02
        b_exp = jnp.zeros((D_HIDDEN,), jnp.float32)
        up_weights = jax.random.normal(ks[2], (NUM_STAGES, D_HIDDEN // 2, 2, 2), jnp.float32) * 0.02
        up_bias = jnp.zeros((D_HIDDEN,), jnp.float32)
        down_weights = jax.random.normal(ks[3], (NUM_STAGES, D_HIDDEN // 2, 2, 2), jnp.float32) * 0.02
        W_con = jax.random.normal(ks[4], (D_HIDDEN, D_MODEL), jnp.float32) * 0.02
        b_con = jnp.zeros((D_MODEL,), jnp.float32)
        down_bias = jnp.zeros((D_MODEL,), jnp.float32)
        return dict(x=x, W_exp=W_exp, b_exp=b_exp, up_weights=up_weights, up_bias=up_bias, down_weights=down_weights, W_con=W_con, b_con=b_con, down_bias=down_bias)
    _L0_ffn_all = _L0_ffn_setup()
    _L0_ffn_in = {k: v for k, v in _L0_ffn_all.items() if k in ('W_exp', 'b_exp', 'up_weights', 'up_bias', 'down_weights', 'W_con', 'b_con', 'down_bias')}
    del _L0_ffn_all

    def _L1_xattn_setup():
        import jax, jax.numpy as jnp
        import numpy as np
        import math
        D_MODEL = 128
        N_HEADS = 16
        HEAD_DIM = D_MODEL // N_HEADS
        TOP_K = 32
        SCALE = math.sqrt(HEAD_DIM)

        def _split_heads(t, n):
            B, L, _ = t.shape
            return t.reshape(B, L, N_HEADS, HEAD_DIM).transpose(0, 2, 1, 3)
        key = jax.random.key(seed)
        ks = jax.random.split(key, 12)
        B, S, N = (2, 256, 256)
        std = 1.0 / math.sqrt(D_MODEL)
        inp = {'x': jax.random.normal(ks[0], (B, S, D_MODEL), dtype=jnp.float32), 'knowledge_embeddings': jax.random.normal(ks[1], (B, N, D_MODEL), dtype=jnp.float32), 'Wq': jax.random.normal(ks[2], (D_MODEL, D_MODEL), dtype=jnp.float32) * std, 'bq': jnp.zeros((D_MODEL,), dtype=jnp.float32), 'Wk': jax.random.normal(ks[3], (D_MODEL, D_MODEL), dtype=jnp.float32) * std, 'bk': jnp.zeros((D_MODEL,), dtype=jnp.float32), 'Wv': jax.random.normal(ks[4], (D_MODEL, D_MODEL), dtype=jnp.float32) * std, 'bv': jnp.zeros((D_MODEL,), dtype=jnp.float32), 'Wo': jax.random.normal(ks[5], (D_MODEL, D_MODEL), dtype=jnp.float32) * std, 'bo': jnp.zeros((D_MODEL,), dtype=jnp.float32)}
        return inp
    _L1_xattn_all = _L1_xattn_setup()
    _L1_xattn_in = {k: v for k, v in _L1_xattn_all.items() if k in ('Wq', 'bq', 'Wk', 'bk', 'Wv', 'bv', 'Wo', 'bo')}
    del _L1_xattn_all

    def _L1_ffn_setup():
        import jax, jax.numpy as jnp
        import numpy as np
        B, S, H, FFN, E = (2, 256, 128, 512, 8)
        key = jax.random.key(seed)
        k0, k1, k2, k3 = jax.random.split(key, 4)
        return {'hidden_states': jax.random.normal(k0, (B, S, H), dtype=jnp.float32), 'Wr': jax.random.normal(k1, (H, E), dtype=jnp.float32) * 0.02, 'br': jnp.zeros((E,), dtype=jnp.float32), 'W1': jax.random.normal(k2, (E, H, FFN), dtype=jnp.float32) * 0.02, 'W2': jax.random.normal(k3, (E, FFN, H), dtype=jnp.float32) * 0.02}
    _L1_ffn_all = _L1_ffn_setup()
    _L1_ffn_in = {k: v for k, v in _L1_ffn_all.items() if k in ('Wr', 'br', 'W1', 'W2')}
    del _L1_ffn_all
    return {'x': x, 'ctx_1024': ctx_1024, 'mask_BxS2_bk0': mask_BxS2_bk0, 'g_xattn': g_xattn, 'g_ffn': g_ffn, 'L0_xattn_g1': _L0_xattn_in['g1'], 'L0_xattn_b1': _L0_xattn_in['b1'], 'L0_xattn_g2': _L0_xattn_in['g2'], 'L0_xattn_b2': _L0_xattn_in['b2'], 'L0_xattn_Wq': _L0_xattn_in['Wq'], 'L0_xattn_Wkv': _L0_xattn_in['Wkv'], 'L0_xattn_Wout': _L0_xattn_in['Wout'], 'L0_ffn_W_exp': _L0_ffn_in['W_exp'], 'L0_ffn_b_exp': _L0_ffn_in['b_exp'], 'L0_ffn_up_weights': _L0_ffn_in['up_weights'], 'L0_ffn_up_bias': _L0_ffn_in['up_bias'], 'L0_ffn_down_weights': _L0_ffn_in['down_weights'], 'L0_ffn_W_con': _L0_ffn_in['W_con'], 'L0_ffn_b_con': _L0_ffn_in['b_con'], 'L0_ffn_down_bias': _L0_ffn_in['down_bias'], 'L1_xattn_Wq': _L1_xattn_in['Wq'], 'L1_xattn_bq': _L1_xattn_in['bq'], 'L1_xattn_Wk': _L1_xattn_in['Wk'], 'L1_xattn_bk': _L1_xattn_in['bk'], 'L1_xattn_Wv': _L1_xattn_in['Wv'], 'L1_xattn_bv': _L1_xattn_in['bv'], 'L1_xattn_Wo': _L1_xattn_in['Wo'], 'L1_xattn_bo': _L1_xattn_in['bo'], 'L1_ffn_Wr': _L1_ffn_in['Wr'], 'L1_ffn_br': _L1_ffn_in['br'], 'L1_ffn_W1': _L1_ffn_in['W1'], 'L1_ffn_W2': _L1_ffn_in['W2']}

def reference(x, ctx_1024, mask_BxS2_bk0, g_xattn, g_ffn, L0_xattn_g1, L0_xattn_b1, L0_xattn_g2, L0_xattn_b2, L0_xattn_Wq, L0_xattn_Wkv, L0_xattn_Wout, L0_ffn_W_exp, L0_ffn_b_exp, L0_ffn_up_weights, L0_ffn_up_bias, L0_ffn_down_weights, L0_ffn_W_con, L0_ffn_b_con, L0_ffn_down_bias, L1_xattn_Wq, L1_xattn_bq, L1_xattn_Wk, L1_xattn_bk, L1_xattn_Wv, L1_xattn_bv, L1_xattn_Wo, L1_xattn_bo, L1_ffn_Wr, L1_ffn_br, L1_ffn_W1, L1_ffn_W2):
    import jax
    import jax.numpy as jnp

    def _L0_xattn_ref(x, latents, mask, g1, b1, g2, b2, Wq, Wkv, Wout):
        import jax, jax.numpy as jnp
        import numpy as np
        EPS = 1e-05

        def layer_norm(x, g, b):
            mu = jnp.mean(x, axis=-1, keepdims=True)
            var = jnp.mean((x - mu) ** 2, axis=-1, keepdims=True)
            return (x - mu) * jax.lax.rsqrt(var + EPS) * g + b
        heads, dim_head = (16, 64)
        b, n, D = x.shape
        l = latents.shape[1]
        xn = layer_norm(x, g1, b1)
        ln_lat = layer_norm(latents, g2, b2)
        q = ln_lat @ Wq
        kv = jnp.concatenate([xn, ln_lat], axis=1) @ Wkv
        k, v = jnp.split(kv, 2, axis=-1)

        def to_heads(t):
            return t.reshape(t.shape[0], t.shape[1], heads, dim_head).transpose(0, 2, 1, 3)
        q, k, v = (to_heads(q), to_heads(k), to_heads(v))
        scale = 1.0 / np.sqrt(np.sqrt(dim_head)).astype(np.float32)
        weight = jnp.einsum('bhld,bhnd->bhln', q * scale, k * scale)
        full_mask = jnp.concatenate([mask, jnp.ones((b, l), dtype=bool)], axis=1)
        neg = -jnp.finfo(weight.dtype).max
        weight = jnp.where(full_mask[:, None, None, :], weight, neg)
        weight = jax.nn.softmax(weight.astype(jnp.float32), axis=-1).astype(q.dtype)
        out = jnp.einsum('bhln,bhnd->bhld', weight, v)
        out = out.transpose(0, 2, 1, 3).reshape(b, l, heads * dim_head)
        return out @ Wout

    def _L0_ffn_ref(x, W_exp, b_exp, up_weights, up_bias, down_weights, W_con, b_con, down_bias):
        import jax, jax.numpy as jnp
        import numpy as np
        D_MODEL = 128
        EXPANSION = 4
        D_HIDDEN = D_MODEL * EXPANSION
        NUM_STAGES = int(np.log2(D_HIDDEN))

        def butterfly(y, weights, dim):
            lead = y.shape[:-1]
            for stage in range(weights.shape[0]):
                s = 2 ** stage
                nb = dim // (2 * s)
                yr = y.reshape(*lead, nb, 2, s)
                a = yr[..., 0, :]
                b = yr[..., 1, :]
                w = weights[stage].reshape(nb, s, 2, 2)
                na = w[..., 0, 0] * a + w[..., 0, 1] * b
                nb2 = w[..., 1, 0] * a + w[..., 1, 1] * b
                y = jnp.stack([na, nb2], axis=-2).reshape(*lead, dim)
            return y
        h = jnp.einsum('bsd,dh->bsh', x, W_exp) + b_exp
        h = butterfly(h, up_weights, D_HIDDEN)
        h = jax.nn.gelu(h + up_bias, approximate=False)
        h = butterfly(h, down_weights, D_HIDDEN)
        y = jnp.einsum('bsh,hd->bsd', h, W_con) + b_con
        return y + down_bias

    def _L1_xattn_ref(x, knowledge_embeddings, Wq, bq, Wk, bk, Wv, bv, Wo, bo):
        import jax, jax.numpy as jnp
        import numpy as np
        import math
        D_MODEL = 128
        N_HEADS = 16
        HEAD_DIM = D_MODEL // N_HEADS
        TOP_K = 32
        SCALE = math.sqrt(HEAD_DIM)

        def _split_heads(t, n):
            B, L, _ = t.shape
            return t.reshape(B, L, N_HEADS, HEAD_DIM).transpose(0, 2, 1, 3)
        B, S, _ = x.shape
        N = knowledge_embeddings.shape[1]
        Q = _split_heads(x @ Wq.T + bq, N_HEADS)
        K = _split_heads(knowledge_embeddings @ Wk.T + bk, N_HEADS)
        V = _split_heads(knowledge_embeddings @ Wv.T + bv, N_HEADS)
        scores = jnp.einsum('bhsd,bhnd->bhsn', Q, K) / SCALE
        k = min(TOP_K, N)
        topk_scores, topk_indices = jax.lax.top_k(scores, k)
        sparse_weights = jax.nn.softmax(topk_scores, axis=-1)
        sel_V = jnp.take_along_axis(V[:, :, None, :, :], topk_indices[..., None], axis=3)
        context = jnp.einsum('bhsk,bhskd->bhsd', sparse_weights, sel_V)
        context = context.transpose(0, 2, 1, 3).reshape(B, S, D_MODEL)
        return context @ Wo.T + bo

    def _L1_ffn_ref(hidden_states, Wr, br, W1, W2):
        import jax, jax.numpy as jnp
        import numpy as np
        B, S, H, FFN, E = (2, 256, 128, 512, 8)
        b, s, h = hidden_states.shape
        x = hidden_states.reshape(-1, h)
        route = jax.nn.sigmoid(x @ Wr + br)
        max_prob = jnp.max(route, axis=1, keepdims=True)
        max_ind = jnp.argmax(route, axis=1)
        out = jnp.zeros_like(x)
        n_experts = Wr.shape[1]
        for e in range(n_experts):
            mask = (max_ind == e)[:, None].astype(x.dtype)
            y = jax.nn.gelu(x @ W1[e], approximate=False) @ W2[e]
            out = out + mask * y
        out = out * max_prob
        return out.reshape(b, s, h)
    x = x + jnp.tanh(g_xattn[0]) * _L0_xattn_ref(ctx_1024, _layernorm(x, axis=-1), mask_BxS2_bk0, L0_xattn_g1, L0_xattn_b1, L0_xattn_g2, L0_xattn_b2, L0_xattn_Wq, L0_xattn_Wkv, L0_xattn_Wout)
    x = x + jnp.tanh(g_ffn[0]) * _L0_ffn_ref(_layernorm(x, axis=-1), L0_ffn_W_exp, L0_ffn_b_exp, L0_ffn_up_weights, L0_ffn_up_bias, L0_ffn_down_weights, L0_ffn_W_con, L0_ffn_b_con, L0_ffn_down_bias)
    x = x + jnp.tanh(g_xattn[1]) * _L1_xattn_ref(_layernorm(x, axis=-1), ctx_1024, L1_xattn_Wq, L1_xattn_bq, L1_xattn_Wk, L1_xattn_bk, L1_xattn_Wv, L1_xattn_bv, L1_xattn_Wo, L1_xattn_bo)
    x = x + jnp.tanh(g_ffn[1]) * _L1_ffn_ref(_layernorm(x, axis=-1), L1_ffn_Wr, L1_ffn_br, L1_ffn_W1, L1_ffn_W2)
    return x

_drawn_inputs = setup_inputs


def setup_inputs(seed=0):
    import zlib

    import numpy as np

    out = dict(_drawn_inputs(seed))
    spreads = {'g_ffn': (-1.0, 0.6),
     'L0_xattn_g1': (1.0, 0.6),
     'L0_xattn_b1': (0.0, 0.8),
     'L0_xattn_g2': (1.0, 0.2),
     'L0_xattn_b2': (0.0, 0.1),
     'L0_ffn_b_exp': (0.0, 0.1),
     'L0_ffn_up_bias': (0.0, 0.1),
     'L0_ffn_b_con': (0.0, 0.1),
     'L0_ffn_down_bias': (0.0, 0.1),
     'L1_xattn_bq': (0.0, 0.1),
     'L1_xattn_bk': (0.0, 0.8),
     'L1_xattn_bv': (0.0, 0.1),
     'L1_xattn_bo': (0.0, 0.1),
     'L1_ffn_br': (0.0, 0.524)}
    factors = {'L1_ffn_Wr': 2.826, 'L1_ffn_W1': 2.668}
    for name, (base, spread) in spreads.items():
        noise = np.random.default_rng([zlib.crc32(name.encode()), seed]).standard_normal(out[name].shape)
        drawn = base * np.exp(spread * noise) if base else spread * noise
        out[name] = jnp.asarray(drawn.astype(out[name].dtype))
    for name, factor in factors.items():
        out[name] = (out[name] * factor).astype(out[name].dtype)
    return out
```

```python
from contextlib import ExitStack

import numpy as np

import concourse.bass as bass
from concourse import mybir

ALU = mybir.AluOpType
ACT = mybir.ActivationFunctionType
F32 = mybir.dt.float32
BF16 = mybir.dt.bfloat16
U8 = mybir.dt.uint8
AX_X = mybir.AxisListType.X

EPS = 1e-5
MASKED = -3.0e38
TAKEN = -3.0e38
SLOTS = 8
LAGS = 6


def flamingo_kernel(nc, t, out):
    NB, S, D = t["x"].shape
    NK = t["ctx_1024"].shape[1]
    H = 16
    INNER = t["L0_xattn_Wq"].shape[1]
    DH = INNER // H
    NC = INNER // 128
    KV = NK + S
    QUADS = H // 4
    HID = t["L0_ffn_W_exp"].shape[1]
    HC = HID // 128
    NST = t["L0_ffn_up_weights"].shape[0]
    D1 = D // H
    SC1 = 1.0 / float(np.sqrt(D1))
    NE = t["L1_ffn_W1"].shape[0]
    ROUNDS = 4
    TILES = NB // 4
    assert S == 128 and D == 128 and DH == 64 and HID == 512 and NK * 4 <= 512

    with ExitStack() as ctx:
        def sb(name, shape, dt=F32):
            return ctx.enter_context(nc.sbuf_tensor(name, shape, dt))

        def sem(name):
            return ctx.enter_context(nc.semaphore(name))

        xs = sb("xs", [128, NB, D])
        cx = sb("cx", [NK, NB, D])
        ident = sb("ident", [128, 128])
        head_mask = sb("head_mask", [128, H])
        half = sb("half", [128, NB])
        ones_row = sb("ones_row", [1, 128], BF16)
        one_f = sb("one_f", [1, 128])
        mask_u8 = sb("mask_u8", [1, NB, NK], U8)
        mask_row = sb("mask_row", [1, NB, NK], BF16)
        g1 = sb("g1", [128, D])
        b1 = sb("b1", [128, D])
        g2 = sb("g2", [128, D])
        b2 = sb("b2", [128, D])
        gates = sb("gates", [128, 4])
        tg = sb("tg", [128, 4])
        a_w = sb("a_w", [128, H, D])
        b_w = sb("b_w", [128, H, D])
        w_up = sb("w_up", [128, HID])
        bias_up = sb("bias_up", [1, HID])
        up_bias = sb("up_bias", [1, HID])
        bias_cols = sb("bias_cols", [128, HC])
        w_dnT = sb("w_dnT", [128, HID])
        w_dn = sb("w_dn", [128, HC, D])
        ffn_bias = sb("ffn_bias", [128, D])
        dn_bias = sb("dn_bias", [128, D])
        l1_wT = sb("l1_wT", [128, 4, D])
        bq = sb("bq", [128, 1])
        bk = sb("bk", [128, 1])
        bv = sb("bv", [1, D])
        bo = sb("bo", [128, D])
        k1T = sb("k1T", [128, NB, NK])
        v1 = sb("v1", [NK, NB, H, D1 + 1])
        wr = sb("wr", [128, NE])
        br = sb("br", [128, NE])

        NBF = NST * (HID // 2) * 4
        bf_w = sb("bf_w", [128, 2 * NBF])
        up_w, down_w = bf_w[:, 0:NBF], bf_w[:, NBF:2 * NBF]
        w1 = bf_w[:, 0:NE * HID].rearrange("p (e f) -> p e f", e=NE)
        w2 = bf_w[:, NBF:NBF + NE * HID].rearrange("p (e c d) -> p e c d", e=NE, c=HC)
        raw = sb("raw", [128, 4 * INNER])
        wq_in, wkv_in, wout_in = raw[:, 0:INNER], raw[:, INNER:3 * INNER], raw[:, 3 * INNER:4 * INNER]
        wT = sb("wT", [128, 3 * INNER])
        l1_in = sb("l1_in", [128, 4, D])
        wcon_in = sb("wcon_in", [128, HC, D])
        cT = wT[:, 0:NB * NK]
        xT_all = raw[:, 0:NB * S]
        up_t, dn_t, upb_t = (raw[0:n, 2 * HID * k:2 * HID * k + 2 * HID].rearrange("p (o f) -> p o f", o=2)
                             for k, n in enumerate((128, 128, 1)))

        ln_x = sb("ln_x", [128, NB, 2])
        ln_c = sb("ln_c", [NK, NB, 2])
        st6 = sb("st6", [128, NB, 6])
        st6c = sb("st6c", [NK, NB, 6])
        rs_x = sb("rs_x", [128, NB])
        rs_x2 = sb("rs_x2", [128, NB])
        rs_c = sb("rs_c", [NK, NB])
        p_lat = sb("p_lat", [128, D])
        p_ctx = sb("p_ctx", [NK, D])
        kv_lat = sb("kv_lat", [128, D])
        kv_ctx = sb("kv_ctx", [NK, D])
        kvT = sb("kvT", [128, KV])
        g_sb = sb("g_sb", [128, 2, 4, 128])
        negmax = sb("negmax", [128, H])
        rowsum = sb("rowsum", [128, H])
        inv = sb("inv", [128, H])
        prob = sb("prob", [128, 2, 4, KV])
        ptc = sb("ptc", [NK, 4, 128])
        ptl = sb("ptl", [128, 4, 128])
        z_sb = sb("z_sb", [128, 4, 128])
        f_st = sb("f_st", [128, 6])
        f_mv = sb("f_mv", [128, 2])
        f_rs = sb("f_rs", [128, 1])
        f_z = sb("f_z", [128, D])
        f_zT = sb("f_zT", [128, 128])
        f_h = sb("f_h", [128, HC, 128])
        b_st = sb("b_st", [128, 6])
        b_mv = sb("b_mv", [128, 2])
        b_rs = sb("b_rs", [128, 1])
        b_z = sb("b_z", [128, D])
        b_zT = sb("b_zT", [128, 128])
        b_q = sb("b_q", [128, 128])
        sw_at, p1_at = 2 * H * NK, 3 * H * NK
        sw = raw[:, 0:sw_at].rearrange("p (h w n) -> p h w n", h=H, w=2)
        p1 = raw[:, sw_at:p1_at].rearrange("p (h n) -> p h n", h=H)
        kbd = wT[:, NB * NK:NB * NK + H * NK].rearrange("p (h n) -> p h n", h=H)
        m8 = sb("m8", [128, H, ROUNDS, 8])
        p1T = sb("p1T", [NK, 4, 128])
        c_inv = sb("c_inv", [128, H])
        c_z = sb("c_z", [128, H, D1])
        c_zT = sb("c_zT", [128, 128])
        c_st = sb("c_st", [128, 6])
        c_mv = sb("c_mv", [128, 2])
        e_mv = sb("e_mv", [128, NB, 2])
        e_rs = sb("e_rs", [128, NB])
        route = sb("route", [128, NB, NE])
        r_max = sb("r_max", [128, NB])
        r_top = sb("r_top", [128, NB])
        r_eq = sb("r_eq", [128, NB, NE])
        r_pri = sb("r_pri", [128, NE])
        coef = sb("coef", [128, NB, NE])
        hT = bf_w[:, NE * HID:NE * HID + 2 * HC * 512].rearrange("p (u c q) -> p u c q", u=2, c=HC)
        e_at = NBF + NE * HID
        x_tile = bf_w[:, e_at:e_at + 512]
        acc = bf_w[:, e_at + 512:e_at + 1024].rearrange("p (n d) -> p n d", n=4)
        e_z = bf_w[:, e_at + 1024:e_at + 1536].rearrange("p (n d) -> p n d", n=4)

        bank = [ctx.enter_context(nc.psum_tensor(f"bank{n}", [128, 512], F32)) for n in range(8)]
        GZ, S0, S1, TC, TL, OA, X, M = bank
        s_bank = [S0, S1]
        CT0 = 256

        PER = dict(p_step=8, kvt_psum=1, kvt_ready=1, kv_copied=1, g_psum=4, g_ready=4, s_psum=8, max_ready=8,
                   exp_done=8, inv_ready=4, p_norm=4, pt_psum=4, pt_ready=4, z_psum=4, z_ready=4, o_psum=4,
                   x1_ready=1, f_stats=2, f_eps=1, frs_ready=1, fz_ready=1, fT_psum=1, fT_ready=1, h_psum=1,
                   h_ready=1, y_psum=1, xb_added=1, x2_ready=1, b_stats=2, b_eps=1, brs_ready=1, bz_ready=1,
                   bT_psum=1, bT_ready=1, q_psum=1, q_ready=1, kbd_ready=1, sc_psum=4, sc_ready=4,
                   topk_done=8, sub_done=4, e_done=4, p1_ready=4, p1T_psum=4, p1T_ready=4,
                   ctx_psum=4, cinv_ready=1, cz_ready=1, cT_psum=1, cT_ready=1, o1_psum=1, xo_added=1,
                   x3_ready=1, c_stats=2, e_stats=1)
        s = {n: sem(n) for n in PER}
        for n in """ld_x ld_c ld_mask ld_gain ld_gates ld_wq ld_wkv ld_wout ld_l1w ld_l1b ld_wcon ld_wexp
                ld_bfu ld_bfd ld_ffnb ld_router ld_w1 ld_w2 c_const c_ident c_hmask c_mask c_gate c_ffnb c_bo
                st_x st_c topk_step waits_apart rs_step rs_ready set_psum set_act set_dve up_mul up_done upb_mul upb_done dn_mul
                dn_done late_psum late_ready e_eps ers_ready ez_sub ez_ready xT_psum xT_ready lg_psum lg_ready
                r_exp r_step coef_ready eh_psum eh_ready ey_psum y_free tile_done store""".split():
            s[n] = sem(n)

        def reach(eng, name, b, n):
            if b is None:
                return
            value = b * PER[name] + n
            if not isinstance(b, int) or value > 0:
                eng.wait_ge(s[name], value)

        def apart(eng):
            eng.sem_inc(s["waits_apart"], 1)

        def run_steps(eng, step, after_step=lambda: None):
            def peeled(i):
                step(i, lambda n: i - n if 0 <= i - n < NB else None)
                after_step()
            for i in range(LAGS):
                peeled(i)
            with eng.Fori(LAGS, NB) as i:
                step(None, lambda n: i - n)
                after_step()
            for i in range(NB, NB + LAGS - 1):
                peeled(i)

        J_A = 6
        J_B = J_A + QUADS
        J_L1W = J_B + QUADS
        J_CT = J_L1W + 1
        J_WCON = J_CT + 3
        J_K1 = J_WCON + 1
        J_V1 = J_K1 + 3
        JOBS = J_V1 + NB // 4
        CT_PART = [(0, 6), (6, 6), (12, 4)]

        def job_heads(q):
            return [8 * (q // 2) + q % 2 + 2 * n for n in range(4)]

        def job_part(w, q):
            h0 = job_heads(q)[0]
            return w[:, h0:h0 + 7:2, :]

        def wait_job(eng, k):
            eng.wait_ge(s["set_act" if k % 2 == 0 else "set_dve"], k // 2 + 1)

        def move_jobs(eng, parity, copy, scaled, biased):
            done = s["set_dve" if parity else "set_act"]
            for k in range(parity, JOBS, 2):
                src = bank[k % 8]
                eng.wait_ge(s["set_psum"], k + 1)
                if k < J_A:
                    last = copy(wT[:, 512 * k:512 * k + 512], src[:, :])
                elif k < J_B:
                    q = k - J_A
                    last = scaled(job_part(a_w, q), src[:, :].rearrange("p (h d) -> p h d", h=4), DH ** -0.5)
                elif k < J_L1W:
                    q = k - J_B
                    last = copy(job_part(b_w, q), src[:, :].rearrange("p (h d) -> p h d", h=4))
                elif k == J_L1W:
                    last = copy(l1_wT[:, :, :], src[:, :].rearrange("p (w d) -> p w d", w=4))
                elif k < J_WCON:
                    b0, nb = CT_PART[k - J_CT]
                    last = copy(cT[:, b0 * NK:(b0 + nb) * NK], src[:, 0:nb * NK])
                elif k == J_WCON:
                    last = copy(w_dnT[:, :], src[:, :])
                elif k < J_V1:
                    b0, nb = CT_PART[k - J_K1]
                    eng.wait_ge(s["ld_l1b"], 64)
                    last = biased(k1T[:, b0:b0 + nb, :], src[:, 0:nb * NK].rearrange("p (b n) -> p b n", b=nb), bk[:, 0:1])
                else:
                    n = k - J_V1
                    for j in range(4):
                        last = copy(v1[:, 4 * n + j, :, 0:D1],
                                    src[0:NK, 128 * j:128 * j + 128].rearrange("p (h d) -> p h d", h=H))
                last.then_inc(done, 1)

        def pairs(v, nb):
            return v.rearrange("p (m o w) -> p m o w", m=nb, o=2)

        def bf_coef(w, st, nb, order):
            v = w[:, st * 2 * HID:(st + 1) * 2 * HID]
            if order == "o w i":
                return v.rearrange("p (m w o i) -> p m o w i", m=nb, o=2, i=2)
            return v.rearrange("p (m w o i) -> p m i w o", m=nb, o=2, i=2)

        block = ctx.enter_context(nc.Block())

        @block.sync
        def _(sp):
            def row(name, n=128):
                a = t[name]
                return a.rearrange("(a d) -> a d", a=1).to_broadcast([n, a.shape[0]])

            sp.dma_start(cx[:, :, :], t["ctx_1024"].rearrange("b n d -> n b d")).then_inc(s["ld_c"], 16)
            sp.dma_start(xs[:, :, :], t["x"].rearrange("b s d -> s b d")).then_inc(s["ld_x"], 16)
            sp.dma_start(wq_in, t["L0_xattn_Wq"]).then_inc(s["ld_wq"], 16)
            sp.dma_start(wkv_in, t["L0_xattn_Wkv"]).then_inc(s["ld_wkv"], 16)
            sp.dma_start(wout_in.rearrange("p (c e) -> p c e", c=NC),
                         t["L0_xattn_Wout"].rearrange("(c p) e -> p c e", p=128)).then_inc(s["ld_wout"], 16)
            for dst, name in ((g1, "L0_xattn_g1"), (b1, "L0_xattn_b1"), (g2, "L0_xattn_g2"), (b2, "L0_xattn_b2")):
                sp.dma_start(dst[:, :], row(name)).then_inc(s["ld_gain"], 16)
            sp.dma_start(mask_u8[:, :, :], t["mask_BxS2_bk0"].rearrange("(a b) n -> a b n", a=1)).then_inc(s["ld_mask"], 16)
            sp.dma_start(gates[:, 0:2], row("g_xattn")).then_inc(s["ld_gates"], 16)
            sp.dma_start(gates[:, 2:4], row("g_ffn")).then_inc(s["ld_gates"], 16)
            for n, name in enumerate(("Wq", "Wk", "Wv", "Wo")):
                sp.dma_start(l1_in[:, n, :], t[f"L1_xattn_{name}"]).then_inc(s["ld_l1w"], 16)
            sp.dma_start(wcon_in[:, :, :], t["L0_ffn_W_con"].rearrange("(c p) d -> p c d", p=128)).then_inc(s["ld_wcon"], 16)
            sp.dma_start(bq[:, :], t["L1_xattn_bq"].rearrange("(p a) -> p a", a=1)).then_inc(s["ld_l1b"], 16)
            sp.dma_start(bk[:, :], t["L1_xattn_bk"].rearrange("(p a) -> p a", a=1)).then_inc(s["ld_l1b"], 16)
            sp.dma_start(bv[:, :], row("L1_xattn_bv", 1)).then_inc(s["ld_l1b"], 16)
            sp.dma_start(bo[:, :], row("L1_xattn_bo")).then_inc(s["ld_l1b"], 16)
            sp.dma_start(w_up[:, :], t["L0_ffn_W_exp"]).then_inc(s["ld_wexp"], 16)
            sp.dma_start(bias_up[:, :], row("L0_ffn_b_exp", 1)).then_inc(s["ld_wexp"], 16)
            sp.dma_start(up_bias[:, :], row("L0_ffn_up_bias", 1)).then_inc(s["ld_wexp"], 16)
            for dst, name, done in ((up_w, "L0_ffn_up_weights", "ld_bfu"), (down_w, "L0_ffn_down_weights", "ld_bfd")):
                flat = t[name].rearrange("n k a b -> (n k a b)").rearrange("(a m) -> a m", a=1)
                sp.dma_start(dst, flat.to_broadcast([128, NBF])).then_inc(s[done], 16)
            sp.dma_start(ffn_bias[:, :], row("L0_ffn_b_con")).then_inc(s["ld_ffnb"], 16)
            sp.dma_start(dn_bias[:, :], row("L0_ffn_down_bias")).then_inc(s["ld_ffnb"], 16)
            sp.dma_start(wr[:, :], t["L1_ffn_Wr"]).then_inc(s["ld_router"], 16)
            sp.dma_start(br[:, :], row("L1_ffn_br")).then_inc(s["ld_router"], 16)
            sp.wait_ge(s["up_done"], NST)
            sp.wait_ge(s["upb_done"], NST)
            sp.dma_start(w1, t["L1_ffn_W1"].rearrange("e d f -> d e f")).then_inc(s["ld_w1"], 16)
            sp.wait_ge(s["dn_done"], NST)
            for e in range(NE):
                sp.dma_start(w2[:, e], t["L1_ffn_W2"][e].rearrange("(c p) d -> p c d", p=128)).then_inc(s["ld_w2"], 16)
            out_v = out.rearrange("b s d -> s b d")
            for n in range(TILES):
                sp.wait_ge(s["tile_done"], n + 1)
                sp.dma_start(out_v[:, 4 * n:4 * n + 4, :], xs[:, 4 * n:4 * n + 4, :]).then_inc(s["store"], 16)
            sp.wait_ge(s["store"], 16 * TILES)

        @block.gpsimd
        def _(pool):
            g = nc.gpsimd
            for v, c in ((ident, 0.0), (half, -0.5), (ones_row, 1.0), (one_f, 1.0), (head_mask, 1.0)):
                g.memset(v[:, :], c).then_inc(s["c_const"], 1)
            for e in range(NE):
                g.memset(r_pri[:, e:e + 1], float(NE - e)).then_inc(s["c_const"], 1)
            g.memset(v1[:, :, :, D1:D1 + 1], 1.0).then_inc(s["c_const"], 1)
            pool.wait_ge(s["c_const"], 6 + NE)
            g.affine_select(out=ident[:, :], in_=ident[:, :], compare_op=ALU.not_equal, fill=1.0, base=0,
                            pattern=[[-1, 128]], channel_multiplier=1).then_inc(s["c_ident"], 1)
            g.affine_select(out=head_mask[:, :], in_=head_mask[:, :], compare_op=ALU.is_ge, fill=0.0, base=0,
                            pattern=[[-D1, H]], channel_multiplier=1).then_inc(s["c_hmask"], 1)
            pool.wait_ge(s["c_hmask"], 1)
            g.affine_select(out=head_mask[:, :], in_=head_mask[:, :], compare_op=ALU.is_ge, fill=0.0, base=D1 - 1,
                            pattern=[[D1, H]], channel_multiplier=-1).then_inc(s["c_hmask"], 1)
            pool.wait_ge(s["c_hmask"], 2)

            count = [0]

            def then(ins):
                count[0] += 1
                ins.then_inc(s["rs_step"], 1)
                pool.wait_ge(s["rs_step"], count[0])

            pool.wait_ge(s["st_c"], 2 * NB)
            then(g.tensor_scalar(rs_c[:, :], ln_c[:, :, 1], EPS, 1.0, ALU.add, ALU.mult))
            then(g.tensor_tensor(rs_c[:, :], rs_c[:, :], half[0:NK, :], ALU.pow))
            pool.wait_ge(s["st_x"], 2 * NB)
            then(g.tensor_scalar(rs_x[:, :], ln_x[:, :, 1], EPS, 1.0, ALU.add, ALU.mult))
            then(g.tensor_tensor(rs_x[:, :], rs_x[:, :], half[:, :], ALU.pow))
            then(g.tensor_tensor(rs_x2[:, :], rs_x[:, :], rs_x[:, :], ALU.mult))
            then(g.tensor_tensor(rs_x2[:, :], rs_x2[:, :], ln_x[:, :, 1], ALU.mult))
            then(g.tensor_scalar(rs_x2[:, :], rs_x2[:, :], EPS, 1.0, ALU.add, ALU.mult))
            then(g.tensor_tensor(rs_x2[:, :], rs_x2[:, :], half[:, :], ALU.pow))
            g.tensor_tensor(rs_x[:, :], rs_x[:, :], rs_x2[:, :], ALU.mult).then_inc(s["rs_ready"], 1)
            pool.wait_ge(s["rs_ready"], 1)
            pool.wait_ge(s["ld_gain"], 64)

            def column(a, b, n, w):
                return a[:, bass.ds(b, 1)].to_broadcast([n, w])

            def batch(a, b):
                return a[:, bass.ds(b, 1), :].squeeze(1)

            def stage_inputs(b):
                reach(pool, "kvt_psum", b, 0)
                reach(pool, "kv_copied", b, 0)
                steps = ((p_ctx, batch(cx, b), column(ln_c[:, :, 0], b, NK, D), ALU.subtract),
                         (p_lat, batch(xs, b), column(ln_x[:, :, 0], b, 128, D), ALU.subtract),
                         (p_ctx, p_ctx[:, :], column(rs_c, b, NK, D), ALU.mult),
                         (p_lat, p_lat[:, :], column(rs_x, b, 128, D), ALU.mult),
                         (p_ctx, p_ctx[:, :], g1[0:NK, :], ALU.mult),
                         (p_lat, p_lat[:, :], g2[:, :], ALU.mult),
                         (p_ctx, p_ctx[:, :], b1[0:NK, :], ALU.add),
                         (p_lat, p_lat[:, :], b2[:, :], ALU.add))
                for n, (dst, a, c, op) in enumerate(steps):
                    if n >= 2:
                        reach(pool, "p_step", b, n - 1)
                    g.tensor_tensor(dst[:, :], a, c, op).then_inc(s["p_step"], 1)

            def copy_keys(b):
                reach(pool, "z_psum", b, 0)
                reach(pool, "p_step", b, 8)
                apart(pool)
                g.tensor_copy(kv_ctx[:, :], p_ctx[:, :])
                g.tensor_copy(kv_lat[:, :], p_lat[:, :]).then_inc(s["kv_copied"], 1)

            def normalise(b, q):
                reach(pool, "exp_done", b, 2 * q + 2)
                reach(pool, "inv_ready", b, q + 1)
                p = prob[:, q % 2, :, :]
                g.tensor_tensor(p, p, inv[:, 4 * q:4 * q + 4].unsqueeze(2).to_broadcast([128, 4, KV]),
                                ALU.mult).then_inc(s["p_norm"], 1)

            def rsqrt(b, mv, rs, stats, eps, ready):
                reach(pool, stats, b, 2)
                apart(pool)
                g.tensor_scalar(rs[:, :], mv[:, 1:2], EPS, 1.0, ALU.add, ALU.mult).then_inc(s[eps], 1)
                reach(pool, eps, b, 1)
                g.tensor_tensor(rs[:, :], rs[:, :], half[:, 0:1], ALU.pow).then_inc(s[ready], 1)

            def spread_keys(b):
                reach(pool, "sc_psum", b, 0)
                g.tensor_tensor(kbd[:, :, :], k1T[:, bass.ds(b, 1), :].to_broadcast([128, H, NK]),
                                head_mask[:, :].unsqueeze(2).to_broadcast([128, H, NK]),
                                ALU.mult).then_inc(s["kbd_ready"], 1)

            def below_max(b, q):
                reach(pool, "topk_done", b, 2 * q + 2)
                v = sw[:, 4 * q:4 * q + 4, :, :].rearrange("p h w n -> p h (w n)")
                g.tensor_tensor(v, v, m8[:, 4 * q:4 * q + 4, 0, 0:1].to_broadcast([128, 4, 2 * NK]),
                                ALU.subtract).then_inc(s["sub_done"], 1)

            def keep_top(b, q):
                reach(pool, "e_done", b, q + 1)
                reach(pool, "p1T_psum", b, q + 1 - QUADS)
                g.tensor_tensor(p1[:, 4 * q:4 * q + 4, :], sw[:, 4 * q:4 * q + 4, 0, :], sw[:, 4 * q:4 * q + 4, 1, :],
                                ALU.subtract).then_inc(s["p1_ready"], 1)

            def add_rows(b, rows, normed, done):
                reach(pool, normed, b, 1)
                v = batch(xs, b)
                g.tensor_tensor(v, v, rows[:, :], ALU.add).then_inc(s[done], 1)

            def down_stage(n):
                st = NST - 1 - n
                w = 2 ** st
                nb = HID // (2 * w)
                if n == 0:
                    wait_job(pool, J_WCON)
                    pool.wait_ge(s["ld_bfd"], 16)
                else:
                    pool.wait_ge(s["dn_done"], n)
                for o in range(2):
                    g.tensor_tensor(pairs(dn_t[:, o, :], nb), bf_coef(down_w, st, nb, "i w o")[:, :, :, :, o],
                                    pairs(w_dnT[:, :], nb)[:, :, o:o + 1, :].to_broadcast([128, nb, 2, w]),
                                    ALU.mult).then_inc(s["dn_mul"], 1)
                pool.wait_ge(s["dn_mul"], 2 * n + 2)
                g.tensor_tensor(w_dnT[:, :], dn_t[:, 0, :], dn_t[:, 1, :], ALU.add).then_inc(s["dn_done"], 1)

            def step(i, at):
                P, A, A2, B, C = (at(n) for n in range(5))
                for slot in range(SLOTS):
                    if slot == 0:
                        if B is not None:
                            rsqrt(B, b_mv, b_rs, "b_stats", "b_eps", "brs_ready")
                            spread_keys(B)
                        if C is not None:
                            keep_top(C, 0)
                    if slot == 1:
                        if B is not None:
                            if i == 3:
                                pool.wait_ge(s["c_bo"], 1)
                            add_rows(B, bo, "bz_ready", "xo_added")
                        if C is not None:
                            below_max(C, 1)
                        if A is not None:
                            normalise(A, 0)
                    if slot == 2:
                        if C is not None:
                            keep_top(C, 1)
                        if A is not None:
                            copy_keys(A)
                        if P is not None:
                            stage_inputs(P)
                    if slot == 3:
                        if A2 is not None:
                            rsqrt(A2, f_mv, f_rs, "f_stats", "f_eps", "frs_ready")
                        if C is not None:
                            below_max(C, 2)
                        if A is not None:
                            normalise(A, 1)
                    if slot == 4:
                        if A2 is not None:
                            if i == 2:
                                pool.wait_ge(s["c_ffnb"], 2)
                            add_rows(A2, ffn_bias, "fz_ready", "xb_added")
                        if C is not None:
                            keep_top(C, 2)
                    if slot == 5:
                        if C is not None:
                            below_max(C, 3)
                        if A is not None:
                            normalise(A, 2)
                    if slot == 6 and C is not None:
                        keep_top(C, 3)
                    if slot == 7:
                        if B is not None:
                            below_max(B, 0)
                        if A is not None:
                            normalise(A, 3)
                    if i in (1, 2) and 8 * (i - 1) + slot < NST:
                        down_stage(8 * (i - 1) + slot)

            run_steps(pool, step)

            reach(pool, "e_stats", NB - 1, 1)
            g.tensor_scalar(e_rs[:, :], e_mv[:, :, 1], EPS, 1.0, ALU.add, ALU.mult).then_inc(s["e_eps"], 1)
            pool.wait_ge(s["e_eps"], 1)
            g.tensor_tensor(e_rs[:, :], e_rs[:, :], half[:, :], ALU.pow).then_inc(s["ers_ready"], 1)

        @block.tensor
        def _(pe):
            mm = nc.tensor.matmul

            def turn(dst, src, rows=128):
                return nc.tensor.transpose(dst, src, ident[0:rows, 0:rows])

            def open_job(k):
                if k >= 8:
                    wait_job(pe, k - 8)
                return bank[k % 8]

            pe.wait_ge(s["c_ident"], 1)
            for k in range(6):
                pe.wait_ge(s["ld_wq" if k < 2 else "ld_wkv"], 16)
                src = wq_in[:, 512 * k:512 * k + 512] if k < 2 else wkv_in[:, 512 * (k - 2):512 * (k - 2) + 512]
                dst = open_job(k)
                for c in range(4):
                    last = turn(dst[:, 128 * c:128 * c + 128], src[:, 128 * c:128 * c + 128])
                last.then_inc(s["set_psum"], 1)

            def head_rows(w, h):
                r, c = DH * (h % 2), INNER * w + 128 * (h // 2)
                return wT[r:r + DH, c:c + 128]

            for k in range(4):
                wait_job(pe, k)
            for q in range(QUADS):
                dst = open_job(J_A + q)
                for n, h in enumerate(job_heads(q)):
                    last = mm(dst[:, 128 * n:128 * n + 128], head_rows(0, h), head_rows(1, h), start=True, stop=True)
                last.then_inc(s["set_psum"], 1)
            pe.wait_ge(s["ld_wout"], 16)
            wait_job(pe, 4)
            wait_job(pe, 5)
            for q in range(QUADS):
                dst = open_job(J_B + q)
                for n, h in enumerate(job_heads(q)):
                    r, c = DH * (h % 2), 128 * (h // 2)
                    last = mm(dst[:, 128 * n:128 * n + 128], head_rows(2, h), wout_in[r:r + DH, c:c + 128],
                              start=True, stop=True)
                last.then_inc(s["set_psum"], 1)
            pe.wait_ge(s["ld_l1w"], 64)
            dst = open_job(J_L1W)
            for n in range(4):
                last = turn(dst[:, 128 * n:128 * n + 128], l1_in[:, n, :])
            last.then_inc(s["set_psum"], 1)
            pe.wait_ge(s["ld_c"], 16)
            for k, (b0, nb) in enumerate(CT_PART):
                dst = open_job(J_CT + k)
                for n in range(nb):
                    last = turn(dst[:, n * NK:(n + 1) * NK], cx[:, b0 + n, :], NK)
                last.then_inc(s["set_psum"], 1)
            pe.wait_ge(s["ld_wcon"], 16)
            dst = open_job(J_WCON)
            for n in range(HC):
                last = turn(dst[:, 128 * n:128 * n + 128], wcon_in[:, n, :])
            last.then_inc(s["set_psum"], 1)
            wait_job(pe, J_L1W)
            for k, (b0, nb) in enumerate(CT_PART):
                wait_job(pe, J_CT + k)
                dst = open_job(J_K1 + k)
                mm(dst[:, 0:nb * NK], l1_wT[:, 1, :], cT[:, b0 * NK:(b0 + nb) * NK], start=True, stop=True)\
                    .then_inc(s["set_psum"], 1)
            pe.wait_ge(s["ld_l1b"], 64)
            for k in range(NB // 4):
                dst = open_job(J_V1 + k)
                for n in range(4):
                    b = 4 * k + n
                    v = dst[0:NK, 128 * n:128 * n + 128]
                    mm(v, one_f[:, 0:NK], bv[:, :], start=True, stop=False)
                    last = mm(v, cT[:, b * NK:(b + 1) * NK], l1_wT[:, 2, :], start=False, stop=True)
                last.then_inc(s["set_psum"], 1)
            for k in range(JOBS - 8, JOBS):
                wait_job(pe, k)
            pe.wait_ge(s["c_mask"], 1)

            reader, now = {}, dict(step=0, at=None)

            def free(name):
                if name in reader:
                    sem_name, lag, n, when = reader[name]
                    reach(pe, sem_name, now["at"](lag + now["step"] - when), n)

            def read_next(name, sem_name, lag, n):
                reader[name] = (sem_name, lag, n, now["step"])

            def keys_T(b):
                free("M")
                reach(pe, "p_step", b, 8)
                turn(M[:, 0:NK], p_ctx[:, :], NK)
                turn(M[:, NK:KV], p_lat[:, :]).then_inc(s["kvt_psum"], 1)
                read_next("M", "kvt_ready", 1, 1)

            def project(b, q):
                free("GZ")
                reach(pe, "kvt_ready", b, 1)
                for n in range(4):
                    last = mm(GZ[:, 128 * n:128 * n + 128], a_w[:, 4 * q + n, :], kvT[:, NK:KV], start=True, stop=True)
                last.then_inc(s["g_psum"], 1)
                read_next("GZ", "g_ready", 1, q + 1)

            def scores(b, p):
                dst = s_bank[p % 2][:, 0:2 * KV].rearrange("p (h n) -> p h n", h=2)
                reach(pe, "exp_done", b, p - 1)
                reach(pe, "g_ready", b, p // 2 + 1)
                apart(pe)
                mm(dst[:, :, 0:NK], ones_row[:, :], mask_row[:, bass.ds(b, 1), :].to_broadcast([1, 2, NK]),
                   start=True, stop=False, skip_group_check=True)
                for n in range(2):
                    last = mm(dst[:, n, :], g_sb[:, (p // 2) % 2, 2 * (p % 2) + n, :], kvT[:, :],
                              start=False, stop=(n == 1), skip_group_check=True)
                last.then_inc(s["s_psum"], 1)

            def probs_T(b, q):
                reach(pe, "p_norm", b, q + 1)
                reach(pe, "pt_ready", b, q)
                for n in range(4):
                    turn(TC[0:NK, 128 * n:128 * n + 128], prob[:, q % 2, n, 0:NK])
                    last = turn(TL[:, 128 * n:128 * n + 128], prob[:, q % 2, n, NK:KV])
                last.then_inc(s["pt_psum"], 1)

            def attend(b, q, lag):
                free("GZ")
                reach(pe, "pt_ready", b, q + 1)
                reach(pe, "kv_copied", b, 1)
                mm(GZ[:, :], kv_ctx[:, :], ptc[:, :, :].rearrange("p h q -> p (h q)"), start=True, stop=False)
                mm(GZ[:, :], kv_lat[:, :], ptl[:, :, :].rearrange("p h q -> p (h q)"), start=False, stop=True)\
                    .then_inc(s["z_psum"], 1)
                read_next("GZ", "z_ready", lag, q + 1)

            def project_out(b, q):
                reach(pe, "z_ready", b, q + 1)
                if q == 0:
                    reach(pe, "x1_ready", b, 0)
                for n in range(4):
                    last = mm(OA[:, 0:D], z_sb[:, n, :], b_w[:, 4 * q + n, :], start=(q == 0 and n == 0),
                              stop=(q == QUADS - 1 and n == 3))
                last.then_inc(s["o_psum"], 1)

            def ffn_T(b):
                free("M")
                reach(pe, "fz_ready", b, 1)
                turn(M[:, 0:128], f_z[:, :]).then_inc(s["fT_psum"], 1)
                read_next("M", "fT_ready", 2, 1)

            def hidden(b):
                free("X")
                reach(pe, "fT_ready", b, 1)
                for n in range(HC):
                    last = mm(X[:, 128 * n:128 * n + 128], w_up[:, 128 * n:128 * n + 128], f_zT[:, :], start=True, stop=True)
                last.then_inc(s["h_psum"], 1)
                read_next("X", "h_ready", 2, 1)

            def down(b):
                free("M")
                reach(pe, "h_ready", b, 1)
                for n in range(HC):
                    last = mm(M[:, 0:D], f_h[:, n, :], w_dn[:, n, :], start=(n == 0), stop=(n == HC - 1))
                last.then_inc(s["y_psum"], 1)
                read_next("M", "x2_ready", 3, 1)

            def second_T(b):
                free("M")
                reach(pe, "bz_ready", b, 1)
                turn(M[:, 0:128], b_z[:, :]).then_inc(s["bT_psum"], 1)
                read_next("M", "bT_ready", 3, 1)

            def queries(b):
                free("M")
                reach(pe, "bT_ready", b, 1)
                mm(M[:, 0:128], l1_wT[:, 0, :], b_zT[:, :], start=True, stop=True).then_inc(s["q_psum"], 1)
                read_next("M", "q_ready", 3, 1)

            def second_scores(b, q):
                free("X")
                reach(pe, "q_ready", b, 1)
                reach(pe, "kbd_ready", b, 1)
                mm(X[:, 0:4 * NK], b_q[:, :], kbd[:, 4 * q:4 * q + 4, :].rearrange("p h n -> p (h n)"),
                   start=True, stop=True).then_inc(s["sc_psum"], 1)
                read_next("X", "sc_ready", 3, q + 1)

            def second_probs_T(b, q):
                free("X")
                reach(pe, "p1_ready", b, q + 1)
                for n in range(4):
                    last = turn(X[0:NK, 128 * n:128 * n + 128], p1[:, 4 * q + n, :])
                last.then_inc(s["p1T_psum"], 1)
                read_next("X", "p1T_ready", 4, q + 1)

            def contexts(b, q):
                free("M")
                reach(pe, "p1T_ready", b, q + 1)
                for n in range(4):
                    c = CT0 + (4 * q + n) * (D1 + 1)
                    last = mm(M[:, c:c + D1 + 1], p1T[:, n, :], v1[:, bass.ds(b, 1), 4 * q + n, :].squeeze(1),
                              start=True, stop=True)
                last.then_inc(s["ctx_psum"], 1)
                if q == QUADS - 1:
                    read_next("M", "cz_ready", 5, 1)

            def context_T(b):
                free("M")
                reach(pe, "cz_ready", b, 1)
                turn(M[:, 0:128], c_z[:, :, :].rearrange("p h d -> p (h d)")).then_inc(s["cT_psum"], 1)
                read_next("M", "cT_ready", 5, 1)

            def second_out(b):
                free("M")
                reach(pe, "cT_ready", b, 1)
                mm(M[:, 0:D], c_zT[:, :], l1_wT[:, 3, :], start=True, stop=True).then_inc(s["o1_psum"], 1)
                read_next("M", "x3_ready", 5, 1)

            def bias_to_columns():
                pe.wait_ge(s["upb_done"], NST + 1)
                for n in range(HC):
                    last = mm(X[:, n:n + 1], bias_up[0:1, 128 * n:128 * n + 128], one_f[:, 0:1], start=True, stop=True)
                last.then_inc(s["late_psum"], 1)
                pe.wait_ge(s["up_done"], NST)
                pe.wait_ge(s["late_ready"], 1)

            def down_weight_back():
                free("X")
                pe.wait_ge(s["dn_done"], NST)
                for n in range(HC):
                    last = turn(X[:, 128 * n:128 * n + 128], w_dnT[:, 128 * n:128 * n + 128])
                last.then_inc(s["late_psum"], 1)
                pe.wait_ge(s["late_ready"], 2)

            def step(i, at):
                now["at"] = at
                P, A, A2, B, C, E = (at(n) for n in range(6))
                for slot in range(SLOTS):
                    if slot == 0:
                        if A is not None:
                            keys_T(A)
                        if A2 is not None:
                            attend(A2, 2, 2)
                        if A is not None:
                            project(A, 0)
                            scores(A, 0)
                        if B is not None:
                            down(B)
                    if slot == 1:
                        if A2 is not None:
                            project_out(A2, 2)
                            probs_T(A2, 3)
                        if A is not None:
                            project(A, 1)
                            scores(A, 1)
                        if E is not None:
                            contexts(E, 3)
                        if C is not None:
                            second_probs_T(C, 0)
                    if slot == 2:
                        if A2 is not None:
                            attend(A2, 3, 2)
                        if A is not None:
                            scores(A, 2)
                        if B is not None:
                            second_T(B)
                        if C is not None:
                            contexts(C, 0)
                        if E is not None:
                            context_T(E)
                    if slot == 3:
                        if A2 is not None:
                            project_out(A2, 3)
                        if A is not None:
                            project(A, 2)
                            probs_T(A, 0)
                            scores(A, 3)
                        if B is not None:
                            queries(B)
                        if C is not None:
                            second_probs_T(C, 1)
                        if E is not None:
                            second_out(E)
                    if slot == 4:
                        if A is not None:
                            attend(A, 0, 1)
                            scores(A, 4)
                        if C is not None:
                            contexts(C, 1)
                        if B is not None:
                            second_scores(B, 0)
                        if i == 2:
                            bias_to_columns()
                    if slot == 5:
                        if A is not None:
                            project_out(A, 0)
                            probs_T(A, 1)
                            project(A, 3)
                        if A2 is not None:
                            ffn_T(A2)
                        if C is not None:
                            second_probs_T(C, 2)
                        if A is not None:
                            scores(A, 5)
                        if B is not None:
                            second_scores(B, 1)
                    if slot == 6:
                        if A is not None:
                            attend(A, 1, 1)
                        if A2 is not None:
                            hidden(A2)
                        if A is not None:
                            scores(A, 6)
                        if C is not None:
                            contexts(C, 2)
                        if B is not None:
                            second_scores(B, 2)
                    if slot == 7:
                        if A is not None:
                            project_out(A, 1)
                            probs_T(A, 2)
                        if C is not None:
                            second_probs_T(C, 3)
                        if A is not None:
                            scores(A, 7)
                        if B is not None:
                            second_scores(B, 3)
                        if i == 2:
                            down_weight_back()
                now["step"] += 1

            run_steps(pe, step)

            pe.wait_ge(s["ld_router"], 32)
            reach(pe, "x3_ready", NB - 1, 1)
            with pe.Fori(1, TILES + 1) as n1:
                pe.wait_ge(s["ez_ready"], n1)
                for n in range(4):
                    last = turn(X[:, 128 * n:128 * n + 128], e_z[:, n, :])
                last.then_inc(s["xT_psum"], 1)
                pe.wait_ge(s["xT_ready"], n1)
                for n in range(4):
                    last = mm(M[:, NE * n:NE * n + NE], x_tile[:, 128 * n:128 * n + 128], wr[:, :], start=True, stop=True)
                last.then_inc(s["lg_psum"], 1)
                pe.wait_ge(s["lg_ready"], n1)

            pe.wait_ge(s["ld_w1"], 16)
            pe.wait_ge(s["ld_w2"], 16 * NE)

            def expert_up(n1, e, c):
                if e:
                    pe.wait_ge(s["eh_ready"], (n1 - 1) * NE * HC + HC * (e - 1) + c + 1)
                mm(bank[c][:, :], w1[:, e, 128 * c:128 * c + 128], xT_all[:, bass.ds((n1 - 1) * 512, 512)],
                   start=True, stop=True).then_inc(s["eh_psum"], 1)

            def expert_down(n1, e):
                y = bank[4 + e % 2]
                pe.wait_ge(s["eh_ready"], (n1 - 1) * NE * HC + HC * (e + 1))
                pe.wait_ge(s["y_free"], (n1 - 1) * NE + e + 1)
                for n in range(4):
                    for c in range(HC):
                        last = mm(y[:, 128 * n:128 * n + 128], hT[:, e % 2, c, 128 * n:128 * n + 128], w2[:, e, c, :],
                                  start=(c == 0), stop=(c == HC - 1))
                last.then_inc(s["ey_psum"], 1)

            with pe.Fori(1, TILES + 1) as n1:
                for e in range(NE):
                    for c in range(HC):
                        expert_up(n1, e, c)
                    if e:
                        expert_down(n1, e - 1)
                expert_down(n1, NE - 1)

        @block.scalar
        def _(act):
            def fn(dst, src, f, **kw):
                return nc.scalar.activation(dst, src, f, **kw)

            def copy(dst, src):
                return fn(dst, src, ACT.Copy)

            act.wait_ge(s["ld_gates"], 32)
            fn(tg[:, :], gates[:, :], ACT.Tanh).then_inc(s["c_gate"], 1)
            move_jobs(act, 0, copy, lambda d, v, c: fn(d, v, ACT.Copy, scale=c),
                      lambda d, v, b: fn(d, v, ACT.Identity, bias=b))

            def keys_out(b):
                reach(act, "kvt_psum", b, 1)
                copy(kvT[:, :], M[:, 0:KV]).then_inc(s["kvt_ready"], 1)

            def projected(b, q):
                reach(act, "g_psum", b, q + 1)
                copy(g_sb[:, q % 2, :, :].rearrange("p h q -> p (h q)"), GZ[:, :]).then_inc(s["g_ready"], 1)

            def exps(b, p):
                reach(act, "max_ready", b, p + 1)
                q = p // 2
                if p % 2 == 0:
                    reach(act, "pt_psum", b, q - 1)
                for n in range(2):
                    h = 2 * p + n
                    last = fn(prob[:, q % 2, 2 * (p % 2) + n, :], s_bank[p % 2][:, n * KV:(n + 1) * KV], ACT.Exp,
                              bias=negmax[:, h:h + 1], accum_out=rowsum[:, h:h + 1])
                last.then_inc(s["exp_done"], 1)

            def probs_out(b, q):
                reach(act, "pt_psum", b, q + 1)
                copy(ptc[:, :, :].rearrange("p h q -> p (h q)"), TC[0:NK, :])
                copy(ptl[:, :, :].rearrange("p h q -> p (h q)"), TL[:, :]).then_inc(s["pt_ready"], 1)

            def attended(b, q):
                reach(act, "z_psum", b, q + 1)
                copy(z_sb[:, :, :].rearrange("p h q -> p (h q)"), GZ[:, :]).then_inc(s["z_ready"], 1)

            def move(b, dst, psum, ready):
                reach(act, psum, b, 1)
                copy(dst[:, :], M[:, 0:128]).then_inc(s[ready], 1)

            def gelus(b):
                reach(act, "h_psum", b, 1)
                for n in range(HC):
                    last = fn(f_h[:, n, :], X[:, 128 * n:128 * n + 128], ACT.Gelu, bias=bias_cols[:, n:n + 1])
                last.then_inc(s["h_ready"], 1)

            def queries_out(b):
                reach(act, "q_psum", b, 1)
                fn(b_q[:, :], M[:, 0:128], ACT.Identity, bias=bq[:, 0:1]).then_inc(s["q_ready"], 1)

            def second_scores_out(b, q):
                reach(act, "sc_psum", b, q + 1)
                reach(act, "p1_ready", b, q + 1 - QUADS)
                copy(sw[:, 4 * q:4 * q + 4, 0, :], X[:, 0:4 * NK].rearrange("p (h n) -> p h n", h=4))\
                    .then_inc(s["sc_ready"], 1)

            def second_exps(b, q):
                reach(act, "sub_done", b, q + 1)
                v = sw[:, 4 * q:4 * q + 4, :, :].rearrange("p h w n -> p (h w n)")
                fn(v, v, ACT.Exp, scale=SC1).then_inc(s["e_done"], 1)

            def second_probs_out(b, q):
                reach(act, "p1T_psum", b, q + 1)
                copy(p1T[:, :, :].rearrange("p h q -> p (h q)"), X[0:NK, :]).then_inc(s["p1T_ready"], 1)

            def step(i, at):
                P, A, A2, B, C, E = (at(n) for n in range(6))
                for slot in range(SLOTS):
                    if slot == 0:
                        if A is not None:
                            keys_out(A)
                        if A2 is not None:
                            attended(A2, 2)
                        if A is not None:
                            projected(A, 0)
                            exps(A, 0)
                    if slot == 1:
                        if A2 is not None:
                            probs_out(A2, 3)
                        if A is not None:
                            projected(A, 1)
                            exps(A, 1)
                        if C is not None:
                            second_probs_out(C, 0)
                            second_exps(C, 1)
                    if slot == 2:
                        if A2 is not None:
                            attended(A2, 3)
                        if A is not None:
                            exps(A, 2)
                        if B is not None:
                            move(B, b_zT, "bT_psum", "bT_ready")
                        if E is not None:
                            move(E, c_zT, "cT_psum", "cT_ready")
                    if slot == 3:
                        if A is not None:
                            projected(A, 2)
                            probs_out(A, 0)
                            exps(A, 3)
                        if B is not None:
                            queries_out(B)
                        if C is not None:
                            second_probs_out(C, 1)
                            second_exps(C, 2)
                    if slot == 4:
                        if A is not None:
                            attended(A, 0)
                            exps(A, 4)
                        if B is not None:
                            second_scores_out(B, 0)
                        if i == 2:
                            act.wait_ge(s["late_psum"], 1)
                            copy(bias_cols[:, :], X[:, 0:HC]).then_inc(s["late_ready"], 1)
                    if slot == 5:
                        if A is not None:
                            probs_out(A, 1)
                            projected(A, 3)
                        if A2 is not None:
                            move(A2, f_zT, "fT_psum", "fT_ready")
                        if C is not None:
                            second_probs_out(C, 2)
                        if A is not None:
                            exps(A, 5)
                        if B is not None:
                            second_scores_out(B, 1)
                        if C is not None:
                            second_exps(C, 3)
                    if slot == 6:
                        if A is not None:
                            attended(A, 1)
                        if A2 is not None:
                            if i == 2:
                                act.wait_ge(s["late_ready"], 1)
                            gelus(A2)
                        if A is not None:
                            exps(A, 6)
                        if B is not None:
                            second_scores_out(B, 2)
                    if slot == 7:
                        if A is not None:
                            probs_out(A, 2)
                        if C is not None:
                            second_probs_out(C, 3)
                        if A is not None:
                            exps(A, 7)
                        if B is not None:
                            second_scores_out(B, 3)
                            second_exps(B, 0)
                        if i == 2:
                            act.wait_ge(s["late_psum"], 2)
                            copy(w_dn[:, :, :].rearrange("p c d -> p (c d)"), X[:, :]).then_inc(s["late_ready"], 1)

            run_steps(act, step)

            with act.Fori(1, TILES + 1) as n1:
                act.wait_ge(s["xT_psum"], n1)
                copy(xT_all[:, bass.ds((n1 - 1) * 512, 512)], X[:, :])
                copy(x_tile[:, :], X[:, :]).then_inc(s["xT_ready"], 1)
            act.wait_ge(s["lg_ready"], TILES)
            fn(route[:, :, :], route[:, :, :], ACT.Exp, scale=-1.0).then_inc(s["r_exp"], 1)
            with act.Fori(1, TILES + 1) as n1:
                for e in range(NE):
                    for c in range(HC):
                        act.wait_ge(s["eh_psum"], (n1 - 1) * NE * HC + HC * e + c + 1)
                        fn(hT[:, e % 2, c, :], bank[c][:, :], ACT.Gelu).then_inc(s["eh_ready"], 1)

        @block.vector
        def _(dve):
            v = nc.vector

            dve.wait_ge(s["ld_c"], 16)
            for b in range(NB):
                v.bn_stats(st6c[:, b, :], cx[:, b, :]).then_inc(s["st_c"], 1)
            dve.wait_ge(s["st_c"], NB)
            for b in range(NB):
                v.bn_aggr(ln_c[:, b, :], st6c[:, b, :]).then_inc(s["st_c"], 1)
            dve.wait_ge(s["ld_x"], 16)
            for b in range(NB):
                v.bn_stats(st6[:, b, :], xs[:, b, :]).then_inc(s["st_x"], 1)
            dve.wait_ge(s["st_x"], NB)
            for b in range(NB):
                v.bn_aggr(ln_x[:, b, :], st6[:, b, :]).then_inc(s["st_x"], 1)
            dve.wait_ge(s["ld_mask"], 16)
            v.tensor_scalar(mask_row[:, :, :], mask_u8[:, :, :], 1.0, -MASKED, ALU.subtract, ALU.mult)\
                .then_inc(s["c_mask"], 1)
            move_jobs(dve, 1, v.tensor_copy, lambda d, x, c: v.tensor_scalar(d, x, c, None, ALU.mult),
                      lambda d, x, b: v.tensor_scalar(d, x, b, None, ALU.add))
            dve.wait_ge(s["c_gate"], 1)
            dve.wait_ge(s["ld_ffnb"], 32)
            v.tensor_tensor(ffn_bias[:, :], ffn_bias[:, :], dn_bias[:, :], ALU.add).then_inc(s["c_ffnb"], 1)
            v.tensor_scalar(bo[:, :], bo[:, :], tg[:, 1:2], None, ALU.mult).then_inc(s["c_bo"], 1)
            dve.wait_ge(s["c_ffnb"], 1)
            v.tensor_scalar(ffn_bias[:, :], ffn_bias[:, :], tg[:, 2:3], None, ALU.mult).then_inc(s["c_ffnb"], 1)

            def up_stage(cur, part, n, mul, done, rows):
                w = 2 ** n
                nb = HID // (2 * w)
                if n == 0:
                    dve.wait_ge(s["ld_bfu"], 16)
                    dve.wait_ge(s["ld_wexp"], 48)
                else:
                    dve.wait_ge(s[done], n)
                for i in range(2):
                    v.tensor_tensor(pairs(part[:, i, :], nb), bf_coef(up_w, n, nb, "o w i")[0:rows, :, :, :, i],
                                    pairs(cur[:, :], nb)[:, :, i:i + 1, :].to_broadcast([rows, nb, 2, w]),
                                    ALU.mult).then_inc(s[mul], 1)
                dve.wait_ge(s[mul], 2 * n + 2)
                v.tensor_tensor(cur[:, :], part[:, 0, :], part[:, 1, :], ALU.add).then_inc(s[done], 1)

            def batch(a, b):
                return a[:, bass.ds(b, 1), :].squeeze(1)

            def maxima(b, p):
                reach(dve, "s_psum", b, p + 1)
                v.tensor_reduce(negmax[:, 2 * p:2 * p + 2], s_bank[p % 2][:, 0:2 * KV].rearrange("p (h n) -> p h n", h=2),
                                AX_X, ALU.max, negate=True).then_inc(s["max_ready"], 1)

            def inverses(b, q):
                reach(dve, "exp_done", b, 2 * q + 2)
                v.reciprocal(inv[:, 4 * q:4 * q + 4], rowsum[:, 4 * q:4 * q + 4]).then_inc(s["inv_ready"], 1)

            def residual(b, src, gate, ready):
                x = batch(xs, b)
                v.scalar_tensor_tensor(x, src, tg[:, gate:gate + 1], x, ALU.mult, ALU.add).then_inc(s[ready], 1)

            def statistics(b, st, mv, ready, done):
                reach(dve, ready, b, 1)
                apart(dve)
                v.bn_stats(st[:, :], batch(xs, b)).then_inc(s[done], 1)
                reach(dve, done, b, 1)
                apart(dve)
                v.bn_aggr(mv[:, :], st[:, :]).then_inc(s[done], 1)

            def normal(b, dst, mv, rs, rs_ready, done):
                reach(dve, rs_ready, b, 1)
                v.tensor_scalar(dst[:, :], batch(xs, b), mv[:, 0:1], rs[:, 0:1], ALU.subtract, ALU.mult).then_inc(s[done], 1)

            def top_32(b, k):
                if k % 2 == 0:
                    reach(dve, "sc_ready", b, k // 2 + 1)
                apart(dve)
                heads = (2 * k, 2 * k + 1)
                step = 0
                for r in range(ROUNDS):
                    src = 0 if r == 0 else 1
                    for h in heads:
                        if r:
                            dve.wait_ge(s["topk_step"], step - 1)
                        v.max(m8[:, h, r, :], sw[:, h, src, :]).then_inc(s["topk_step"], 1)
                        step += 1
                    for h in heads:
                        dve.wait_ge(s["topk_step"], step - 1)
                        v.match_replace(sw[:, h, 1, :], m8[:, h, r, :], sw[:, h, src, :], TAKEN)\
                            .then_inc(s["topk_step"], 1)
                        step += 1
                dve.wait_ge(s["topk_step"], step)
                dve.sem_clear(s["topk_step"]).then_inc(s["topk_done"], 1)

            def context_out(b):
                reach(dve, "ctx_psum", b, QUADS)
                c = M[:, CT0:CT0 + H * (D1 + 1)].rearrange("p (h d) -> p h d", h=H)
                v.reciprocal(c_inv[:, :], c[:, :, D1]).then_inc(s["cinv_ready"], 1)
                reach(dve, "cinv_ready", b, 1)
                v.tensor_tensor(c_z[:, :, :], c[:, :, 0:D1], c_inv[:, :].unsqueeze(2).to_broadcast([128, H, D1]),
                                ALU.mult).then_inc(s["cz_ready"], 1)

            def step(i, at):
                P, A, A2, B, C, E = (at(n) for n in range(6))
                for slot in range(SLOTS):
                    if A is not None:
                        if slot == 3 and A2 is not None:
                            pass
                        maxima(A, slot)
                    if slot == 0 and B is not None:
                        reach(dve, "y_psum", B, 1)
                        reach(dve, "xb_added", B, 1)
                        residual(B, M[:, 0:D], 2, "x2_ready")
                        statistics(B, b_st, b_mv, "x2_ready", "b_stats")
                    if slot == 1 and E is not None:
                        context_out(E)
                    if slot == 3:
                        if A2 is not None:
                            reach(dve, "o_psum", A2, QUADS)
                            residual(A2, OA[:, 0:D], 0, "x1_ready")
                            statistics(A2, f_st, f_mv, "x1_ready", "f_stats")
                        if E is not None:
                            reach(dve, "o1_psum", E, 1)
                            reach(dve, "xo_added", E, 1)
                            residual(E, M[:, 0:D], 1, "x3_ready")
                            statistics(E, c_st, c_mv, "x3_ready", "c_stats")
                            reach(dve, "c_stats", E, 2)
                            apart(dve)
                            v.tensor_copy(batch(e_mv, E), c_mv[:, :]).then_inc(s["e_stats"], 1)
                    if slot < 5 and C is not None:
                        top_32(C, slot + 3)
                    if slot >= 5 and B is not None:
                        top_32(B, slot - 5)
                    if slot % 2 == 1 and A is not None:
                        inverses(A, slot // 2)
                    if slot == 0 and B is not None:
                        normal(B, b_z, b_mv, b_rs, "brs_ready", "bz_ready")
                    if slot == 3 and A2 is not None:
                        normal(A2, f_z, f_mv, f_rs, "frs_ready", "fz_ready")
                    n = 8 * (i - 1) + slot if i in (1, 2) else NST
                    if n < NST:
                        up_stage(w_up, up_t, n, "up_mul", "up_done", 128)
                        up_stage(bias_up, upb_t, n, "upb_mul", "upb_done", 1)
                    if n == NST - 1:
                        dve.wait_ge(s["upb_done"], NST)
                        v.tensor_tensor(bias_up[:, :], bias_up[:, :], up_bias[:, :], ALU.add).then_inc(s["upb_done"], 1)

            run_steps(dve, step)

            dve.wait_ge(s["ers_ready"], 1)
            with dve.Fori(1, TILES + 1) as n1:
                b0 = (n1 - 1) * 4
                v.tensor_tensor(e_z[:, :, :], xs[:, bass.ds(b0, 4), :],
                                e_mv[:, bass.ds(b0, 4), 0:1].to_broadcast([128, 4, D]), ALU.subtract).then_inc(s["ez_sub"], 1)
                dve.wait_ge(s["ez_sub"], n1)
                v.tensor_tensor(e_z[:, :, :], e_z[:, :, :], e_rs[:, bass.ds(b0, 4)].unsqueeze(2).to_broadcast([128, 4, D]),
                                ALU.mult).then_inc(s["ez_ready"], 1)
                dve.wait_ge(s["lg_psum"], n1)
                v.tensor_tensor(route[:, bass.ds(b0, 4), :], M[:, 0:4 * NE].rearrange("p (n e) -> p n e", n=4),
                                br[:, :].unsqueeze(1).to_broadcast([128, 4, NE]), ALU.add).then_inc(s["lg_ready"], 1)

            count = [0]

            def then(ins):
                count[0] += 1
                ins.then_inc(s["r_step"], 1)
                dve.wait_ge(s["r_step"], count[0])

            wide = [128, NB, NE]
            dve.wait_ge(s["r_exp"], 1)
            then(v.tensor_scalar(route[:, :, :], route[:, :, :], 1.0, None, ALU.add))
            then(v.reciprocal(route[:, :, :], route[:, :, :]))
            then(v.reduce_max(r_max[:, :], route[:, :, :], AX_X))
            then(v.tensor_tensor(r_eq[:, :, :], route[:, :, :], r_max[:, :].unsqueeze(2).to_broadcast(wide), ALU.is_equal))
            then(v.tensor_tensor(r_eq[:, :, :], r_eq[:, :, :], r_pri[:, :].unsqueeze(1).to_broadcast(wide), ALU.mult))
            then(v.reduce_max(r_top[:, :], r_eq[:, :, :], AX_X))
            then(v.tensor_tensor(r_eq[:, :, :], r_eq[:, :, :], r_top[:, :].unsqueeze(2).to_broadcast(wide), ALU.is_equal))
            v.tensor_tensor(coef[:, :, :], r_eq[:, :, :], r_max[:, :].unsqueeze(2).to_broadcast(wide), ALU.mult)\
                .then_inc(s["coef_ready"], 1)
            dve.wait_ge(s["coef_ready"], 1)

            for n in range(2):
                v.memset(acc[:, n, 0:1], 0.0).then_inc(s["y_free"], 1)
            dve.wait_ge(s["y_free"], 2)
            with dve.Fori(1, TILES + 1) as n1:
                b0 = (n1 - 1) * 4
                for e in range(NE):
                    done = (n1 - 1) * NE + e
                    dve.wait_ge(s["ey_psum"], done + 1)
                    dve.wait_ge(s["y_free"], done + 2)
                    for n in range(4):
                        y = bank[4 + e % 2][:, 128 * n:128 * n + 128]
                        c = coef[:, bass.ds(b0 + n, 1), e]
                        if e == 0:
                            last = v.tensor_scalar(acc[:, n, :], y, c, None, ALU.mult)
                        else:
                            last = v.scalar_tensor_tensor(acc[:, n, :], y, c, acc[:, n, :], ALU.mult, ALU.add)
                    last.then_inc(s["y_free"], 1)
                dve.wait_ge(s["y_free"], n1 * NE + 2)
                x = xs[:, bass.ds(b0, 4), :]
                v.scalar_tensor_tensor(x, acc[:, :, :], tg[:, 3:4], x, ALU.mult, ALU.add).then_inc(s["tile_done"], 1)
                dve.wait_ge(s["tile_done"], n1)


INPUTS = ["x", "ctx_1024", "mask_BxS2_bk0", "g_xattn", "g_ffn", "L0_xattn_g1", "L0_xattn_b1", "L0_xattn_g2",
          "L0_xattn_b2", "L0_xattn_Wq", "L0_xattn_Wkv", "L0_xattn_Wout", "L0_ffn_W_exp", "L0_ffn_b_exp",
          "L0_ffn_up_weights", "L0_ffn_up_bias", "L0_ffn_down_weights", "L0_ffn_W_con", "L0_ffn_b_con",
          "L0_ffn_down_bias", "L1_xattn_Wq", "L1_xattn_bq", "L1_xattn_Wk", "L1_xattn_bk", "L1_xattn_Wv",
          "L1_xattn_bv", "L1_xattn_Wo", "L1_xattn_bo", "L1_ffn_Wr", "L1_ffn_br", "L1_ffn_W1", "L1_ffn_W2"]


def kernel(**inputs):
    import numpy as _np
    import concourse.bacc as _bacc
    from concourse.bass_utils import run_bass_kernel_spmd as _run

    nc = _bacc.Bacc("TRN2", target_bir_lowering=False, num_devices=1)
    arrays, t = {}, {}
    for name in INPUTS:
        a = _np.ascontiguousarray(inputs[name])
        arrays[f"in_{name}"] = a
        t[name] = nc.dram_tensor(f"in_{name}", a.shape, mybir.dt.from_np(a.dtype), kind="ExternalInput").ap()
    out = nc.dram_tensor("out_x", t["x"].shape, F32, kind="ExternalOutput").ap()
    flamingo_kernel(nc, t, out)
    r = _run(nc, [arrays], core_ids=[0])
    return r.results[0]["out_x"]
```

```python
from contextlib import ExitStack

import numpy as np

import concourse.bass as bass
from concourse import mybir

ALU = mybir.AluOpType
ACT = mybir.ActivationFunctionType
F32 = mybir.dt.float32
BF16 = mybir.dt.bfloat16
U8 = mybir.dt.uint8
I32 = mybir.dt.int32
U32 = mybir.dt.uint32
AX_X = mybir.AxisListType.X

EPS = 1e-5
MASKED = -3.0e38
TAKEN = -3.0e38
SLOTS = 8
LAGS = 6


def flamingo_kernel(nc, t, out):
    NB, S, D = t["x"].shape
    NK = t["ctx_1024"].shape[1]
    H = 16
    INNER = t["L0_xattn_Wq"].shape[1]
    DH = INNER // H
    NC = INNER // 128
    KV = NK + S
    QUADS = H // 4
    HID = t["L0_ffn_W_exp"].shape[1]
    HC = HID // 128
    NST = t["L0_ffn_up_weights"].shape[0]
    D1 = D // H
    SC1 = 1.0 / float(np.sqrt(D1))
    NE = t["L1_ffn_W1"].shape[0]
    ROUNDS = 4
    TILES = NB // 4
    GROUP = 4
    UNROLL = 2 * GROUP
    SORTED = -(-(NB + NE - 1) // UNROLL) * UNROLL
    assert S == 128 and D == 128 and DH == 64 and HID == 512 and NK * 4 <= 512

    with ExitStack() as ctx:
        def sb(name, shape, dt=F32):
            return ctx.enter_context(nc.sbuf_tensor(name, shape, dt))

        def sem(name):
            return ctx.enter_context(nc.semaphore(name))

        xs = sb("xs", [128, NB, D])
        cx = sb("cx", [NK, NB, D])
        ident = sb("ident", [128, 128])
        head_mask = sb("head_mask", [128, H])
        half = sb("half", [128, NB])
        ones_row = sb("ones_row", [1, 128], BF16)
        one_f = sb("one_f", [1, 128])
        mask_u8 = sb("mask_u8", [1, NB, NK], U8)
        mask_row = sb("mask_row", [1, NB, NK], BF16)
        g1 = sb("g1", [128, D])
        b1 = sb("b1", [128, D])
        g2 = sb("g2", [128, D])
        b2 = sb("b2", [128, D])
        gates = sb("gates", [128, 4])
        tg = sb("tg", [128, 4])
        a_w = sb("a_w", [128, H, D])
        b_w = sb("b_w", [128, H, D])
        w_up = sb("w_up", [128, HID])
        bias_up = sb("bias_up", [1, HID])
        up_bias = sb("up_bias", [1, HID])
        bias_cols = sb("bias_cols", [128, HC])
        w_dnT = sb("w_dnT", [128, HID])
        w_dn = sb("w_dn", [128, HC, D])
        ffn_bias = sb("ffn_bias", [128, D])
        dn_bias = sb("dn_bias", [128, D])
        l1_wT = sb("l1_wT", [128, 4, D])
        bq = sb("bq", [128, 1])
        bk = sb("bk", [128, 1])
        bv = sb("bv", [1, D])
        bo = sb("bo", [128, D])
        k1T = sb("k1T", [128, NB, NK])
        v1 = sb("v1", [NK, NB, H, D1 + 1])
        wr = sb("wr", [128, NE])
        br = sb("br", [128, NE])

        NBF = NST * (HID // 2) * 4
        bf_w = sb("bf_w", [128, 2 * NBF])
        up_w, down_w = bf_w[:, 0:NBF], bf_w[:, NBF:2 * NBF]
        w1 = bf_w[:, 0:NE * HID].rearrange("p (e f) -> p e f", e=NE)
        w2 = bf_w[:, NBF:NBF + NE * HID].rearrange("p (e c d) -> p e c d", e=NE, c=HC)
        raw = sb("raw", [128, 4 * INNER])
        wq_in, wkv_in, wout_in = raw[:, 0:INNER], raw[:, INNER:3 * INNER], raw[:, 3 * INNER:4 * INNER]
        wT = sb("wT", [128, 3 * INNER])
        l1_in = sb("l1_in", [128, 4, D])
        wcon_in = sb("wcon_in", [128, HC, D])
        cT = wT[:, 0:NB * NK]
        z_all = raw[:, 0:NB * D].rearrange("p (b d) -> p b d", b=NB)
        y_back = raw[:, NB * D:2 * NB * D].rearrange("p (b d) -> p b d", b=NB)
        up_t, dn_t, upb_t = (raw[0:n, 2 * HID * k:2 * HID * k + 2 * HID].rearrange("p (o f) -> p o f", o=2)
                             for k, n in enumerate((128, 128, 1)))

        ln_x = sb("ln_x", [128, NB, 2])
        ln_c = sb("ln_c", [NK, NB, 2])
        st6 = sb("st6", [128, NB, 6])
        st6c = sb("st6c", [NK, NB, 6])
        rs_x = sb("rs_x", [128, NB])
        rs_x2 = sb("rs_x2", [128, NB])
        rs_c = sb("rs_c", [NK, NB])
        p_lat = sb("p_lat", [128, D])
        p_ctx = sb("p_ctx", [NK, D])
        kv_lat = sb("kv_lat", [128, D])
        kv_ctx = sb("kv_ctx", [NK, D])
        kvT = sb("kvT", [128, KV])
        g_sb = sb("g_sb", [128, 2, 4, 128])
        negmax = sb("negmax", [128, H])
        rowsum = sb("rowsum", [128, H])
        inv = sb("inv", [128, H])
        prob = sb("prob", [128, 2, 4, KV])
        ptc = sb("ptc", [NK, 4, 128])
        ptl = sb("ptl", [128, 4, 128])
        z_sb = sb("z_sb", [128, 4, 128])
        f_st = sb("f_st", [128, 6])
        f_mv = sb("f_mv", [128, 2])
        f_rs = sb("f_rs", [128, 1])
        f_z = sb("f_z", [128, D])
        f_zT = sb("f_zT", [128, 128])
        f_h = sb("f_h", [128, HC, 128])
        b_st = sb("b_st", [128, 6])
        b_mv = sb("b_mv", [128, 2])
        b_rs = sb("b_rs", [128, 1])
        b_z = sb("b_z", [128, D])
        b_zT = sb("b_zT", [128, 128])
        b_q = sb("b_q", [128, 128])
        sw_at, p1_at = 2 * H * NK, 3 * H * NK
        sw = raw[:, 0:sw_at].rearrange("p (h w n) -> p h w n", h=H, w=2)
        p1 = raw[:, sw_at:p1_at].rearrange("p (h n) -> p h n", h=H)
        kbd = wT[:, NB * NK:NB * NK + H * NK].rearrange("p (h n) -> p h n", h=H)
        m8 = sb("m8", [128, H, ROUNDS, 8])
        p1T = sb("p1T", [NK, 4, 128])
        c_inv = sb("c_inv", [128, H])
        c_z = sb("c_z", [128, H, D1])
        c_zT = sb("c_zT", [128, 128])
        c_st = sb("c_st", [128, 6])
        c_mv = sb("c_mv", [128, 2])
        e_mv = sb("e_mv", [128, NB, 2])
        e_rs = sb("e_rs", [128, NB])
        route = sb("route", [128, NB, NE])
        r_max = sb("r_max", [128, NB])
        r_top = sb("r_top", [128, NB])
        r_eq = sb("r_eq", [128, NB, NE])
        r_pri = sb("r_pri", [128, NE])
        chosen = sb("chosen", [128, NB, NE], BF16)
        coef = sb("coef", [128, NB])
        spare = [NE * HID]

        def beside(n):
            at = spare[0]
            if at <= NBF < at + n:
                at = NBF + NE * HID
            spare[0] = at + n
            assert at + n <= 2 * NBF
            return bf_w[:, at:at + n]

        x_tile = beside(512)
        e_z = beside(4 * D).rearrange("p (n d) -> p n d", n=4)
        z_group = beside(2 * GROUP * D).rearrange("p (u n d) -> p u n d", u=2, n=GROUP)
        x_group = beside(2 * GROUP * S).rearrange("p (u n q) -> p u n q", u=2, n=GROUP)
        h_exp = beside(2 * HID).rearrange("p (u f) -> p u f", u=2)
        hT = beside(2 * HID).rearrange("p (u c q) -> p u c q", u=2, c=HC)
        y_all = beside(SORTED * D).rearrange("p (n d) -> p n d", n=SORTED)
        steps_128 = sb("steps_128", [128, NB])
        tile_no = sb("tile_no", [128, SORTED])
        before_e = sb("before_e", [128, NE, NE])
        before_p = sb("before_p", [128, 128], BF16)
        ones_bf = sb("ones_bf", [128, 128], BF16)
        zeros = sb("zeros", [128, D])
        n_full = beside(NE * NB).rearrange("p (e k) -> p e k", e=NE)
        n_tiles = sb("n_tiles", [128, NE])
        n_before = beside(NE * NE).rearrange("p (e k) -> p e k", e=NE)
        start = sb("start", [128, NE])
        end = sb("end", [128, NE])
        t_past = beside(SORTED * NE).rearrange("p (t e) -> p t e", t=SORTED)
        t_exp = sb("t_exp", [128, SORTED])
        tile_expert = sb("tile_expert", [128, SORTED], I32)
        place_e = beside(NB * NE).rearrange("p (b e) -> p b e", b=NB)
        place_f = sb("place_f", [128, NB])
        place = sb("place", [128, NB], U32)

        z_sorted = nc.dram_tensor("z_sorted", [SORTED * 128, D], F32, kind="Internal").ap()
        y_sorted = nc.dram_tensor("y_sorted", [SORTED * 128, D], F32, kind="Internal").ap()

        bank = [ctx.enter_context(nc.psum_tensor(f"bank{n}", [128, 512], F32)) for n in range(8)]
        GZ, S0, S1, TC, TL, OA, X, M = bank
        s_bank = [S0, S1]
        CT0 = 256

        PER = dict(p_step=8, kvt_psum=1, kvt_ready=1, kv_copied=1, g_psum=4, g_ready=4, s_psum=8, max_ready=8,
                   exp_done=8, inv_ready=4, p_norm=4, pt_psum=4, pt_ready=4, z_psum=4, z_ready=4, o_psum=4,
                   x1_ready=1, f_stats=2, f_eps=1, frs_ready=1, fz_ready=1, fT_psum=1, fT_ready=1, h_psum=1,
                   h_ready=1, y_psum=1, xb_added=1, x2_ready=1, b_stats=2, b_eps=1, brs_ready=1, bz_ready=1,
                   bT_psum=1, bT_ready=1, q_psum=1, q_ready=1, kbd_ready=1, sc_psum=4, sc_ready=4,
                   topk_done=8, sub_done=4, e_done=4, p1_ready=4, p1T_psum=4, p1T_ready=4,
                   ctx_psum=4, cinv_ready=1, cz_ready=1, cT_psum=1, cT_ready=1, o1_psum=1, xo_added=1,
                   x3_ready=1, c_stats=2, e_stats=1)
        s = {n: sem(n) for n in PER}
        for n in """ld_x ld_c ld_mask ld_gain ld_gates ld_wq ld_wkv ld_wout ld_l1w ld_l1b ld_wcon ld_wexp
                ld_bfu ld_bfd ld_ffnb ld_router ld_w1 ld_w2 c_const c_ident c_hmask c_mask c_gate c_ffnb c_bo
                st_x st_c topk_step waits_apart rs_step rs_ready set_psum set_act set_dve up_mul up_done upb_mul upb_done dn_mul
                dn_done late_psum late_ready e_eps ers_ready ez_kept ez_sub ez_ready xT_psum xT_ready lg_psum lg_ready
                r_exp r_step r_max_ready chosen_ready count_psum map_ready place_ready coef_ready c_sort c_zero c_past
                z_zeroed z_scattered z_loaded xg_psum xg_ready up_psum gelu_ready turned hT_ready
                ey_psum ey_ready y_stored y_part0 y_part1 y_part2 y_part3 y_times tile_done store""".split():
            s[n] = sem(n)

        def reach(eng, name, b, n):
            if b is None:
                return
            value = b * PER[name] + n
            if not isinstance(b, int) or value > 0:
                eng.wait_ge(s[name], value)

        def apart(eng):
            eng.sem_inc(s["waits_apart"], 1)

        def run_steps(eng, step, after_step=lambda: None):
            def peeled(i):
                step(i, lambda n: i - n if 0 <= i - n < NB else None)
                after_step()
            for i in range(LAGS):
                peeled(i)
            with eng.Fori(LAGS, NB) as i:
                step(None, lambda n: i - n)
                after_step()
            for i in range(NB, NB + LAGS - 1):
                peeled(i)

        J_A = 6
        J_B = J_A + QUADS
        J_L1W = J_B + QUADS
        J_CT = J_L1W + 1
        J_WCON = J_CT + 3
        J_K1 = J_WCON + 1
        J_V1 = J_K1 + 3
        JOBS = J_V1 + NB // 4
        CT_PART = [(0, 6), (6, 6), (12, 4)]

        def job_heads(q):
            return [8 * (q // 2) + q % 2 + 2 * n for n in range(4)]

        def job_part(w, q):
            h0 = job_heads(q)[0]
            return w[:, h0:h0 + 7:2, :]

        def wait_job(eng, k):
            eng.wait_ge(s["set_act" if k % 2 == 0 else "set_dve"], k // 2 + 1)

        def move_jobs(eng, parity, copy, scaled, biased):
            done = s["set_dve" if parity else "set_act"]
            for k in range(parity, JOBS, 2):
                src = bank[k % 8]
                eng.wait_ge(s["set_psum"], k + 1)
                if k < J_A:
                    last = copy(wT[:, 512 * k:512 * k + 512], src[:, :])
                elif k < J_B:
                    q = k - J_A
                    last = scaled(job_part(a_w, q), src[:, :].rearrange("p (h d) -> p h d", h=4), DH ** -0.5)
                elif k < J_L1W:
                    q = k - J_B
                    last = copy(job_part(b_w, q), src[:, :].rearrange("p (h d) -> p h d", h=4))
                elif k == J_L1W:
                    last = copy(l1_wT[:, :, :], src[:, :].rearrange("p (w d) -> p w d", w=4))
                elif k < J_WCON:
                    b0, nb = CT_PART[k - J_CT]
                    last = copy(cT[:, b0 * NK:(b0 + nb) * NK], src[:, 0:nb * NK])
                elif k == J_WCON:
                    last = copy(w_dnT[:, :], src[:, :])
                elif k < J_V1:
                    b0, nb = CT_PART[k - J_K1]
                    eng.wait_ge(s["ld_l1b"], 64)
                    last = biased(k1T[:, b0:b0 + nb, :], src[:, 0:nb * NK].rearrange("p (b n) -> p b n", b=nb), bk[:, 0:1])
                else:
                    n = k - J_V1
                    for j in range(4):
                        last = copy(v1[:, 4 * n + j, :, 0:D1],
                                    src[0:NK, 128 * j:128 * j + 128].rearrange("p (h d) -> p h d", h=H))
                last.then_inc(done, 1)

        def pairs(v, nb):
            return v.rearrange("p (m o w) -> p m o w", m=nb, o=2)

        def bf_coef(w, st, nb, order):
            v = w[:, st * 2 * HID:(st + 1) * 2 * HID]
            if order == "o w i":
                return v.rearrange("p (m w o i) -> p m o w i", m=nb, o=2, i=2)
            return v.rearrange("p (m w o i) -> p m i w o", m=nb, o=2, i=2)

        block = ctx.enter_context(nc.Block())

        @block.sync
        def _(sp):
            def row(name, n=128):
                a = t[name]
                return a.rearrange("(a d) -> a d", a=1).to_broadcast([n, a.shape[0]])

            sp.dma_start(cx[:, :, :], t["ctx_1024"].rearrange("b n d -> n b d")).then_inc(s["ld_c"], 16)
            sp.dma_start(xs[:, :, :], t["x"].rearrange("b s d -> s b d")).then_inc(s["ld_x"], 16)
            sp.dma_start(wq_in, t["L0_xattn_Wq"]).then_inc(s["ld_wq"], 16)
            sp.dma_start(wkv_in, t["L0_xattn_Wkv"]).then_inc(s["ld_wkv"], 16)
            sp.dma_start(wout_in.rearrange("p (c e) -> p c e", c=NC),
                         t["L0_xattn_Wout"].rearrange("(c p) e -> p c e", p=128)).then_inc(s["ld_wout"], 16)
            for dst, name in ((g1, "L0_xattn_g1"), (b1, "L0_xattn_b1"), (g2, "L0_xattn_g2"), (b2, "L0_xattn_b2")):
                sp.dma_start(dst[:, :], row(name)).then_inc(s["ld_gain"], 16)
            sp.dma_start(mask_u8[:, :, :], t["mask_BxS2_bk0"].rearrange("(a b) n -> a b n", a=1)).then_inc(s["ld_mask"], 16)
            sp.dma_start(gates[:, 0:2], row("g_xattn")).then_inc(s["ld_gates"], 16)
            sp.dma_start(gates[:, 2:4], row("g_ffn")).then_inc(s["ld_gates"], 16)
            for n, name in enumerate(("Wq", "Wk", "Wv", "Wo")):
                sp.dma_start(l1_in[:, n, :], t[f"L1_xattn_{name}"]).then_inc(s["ld_l1w"], 16)
            sp.dma_start(wcon_in[:, :, :], t["L0_ffn_W_con"].rearrange("(c p) d -> p c d", p=128)).then_inc(s["ld_wcon"], 16)
            sp.dma_start(bq[:, :], t["L1_xattn_bq"].rearrange("(p a) -> p a", a=1)).then_inc(s["ld_l1b"], 16)
            sp.dma_start(bk[:, :], t["L1_xattn_bk"].rearrange("(p a) -> p a", a=1)).then_inc(s["ld_l1b"], 16)
            sp.dma_start(bv[:, :], row("L1_xattn_bv", 1)).then_inc(s["ld_l1b"], 16)
            sp.dma_start(bo[:, :], row("L1_xattn_bo")).then_inc(s["ld_l1b"], 16)
            sp.dma_start(w_up[:, :], t["L0_ffn_W_exp"]).then_inc(s["ld_wexp"], 16)
            sp.dma_start(bias_up[:, :], row("L0_ffn_b_exp", 1)).then_inc(s["ld_wexp"], 16)
            sp.dma_start(up_bias[:, :], row("L0_ffn_up_bias", 1)).then_inc(s["ld_wexp"], 16)
            for dst, name, done in ((up_w, "L0_ffn_up_weights", "ld_bfu"), (down_w, "L0_ffn_down_weights", "ld_bfd")):
                flat = t[name].rearrange("n k a b -> (n k a b)").rearrange("(a m) -> a m", a=1)
                sp.dma_start(dst, flat.to_broadcast([128, NBF])).then_inc(s[done], 16)
            sp.dma_start(ffn_bias[:, :], row("L0_ffn_b_con")).then_inc(s["ld_ffnb"], 16)
            sp.dma_start(dn_bias[:, :], row("L0_ffn_down_bias")).then_inc(s["ld_ffnb"], 16)
            sp.dma_start(wr[:, :], t["L1_ffn_Wr"]).then_inc(s["ld_router"], 16)
            sp.dma_start(br[:, :], row("L1_ffn_br")).then_inc(s["ld_router"], 16)
            sp.wait_ge(s["up_done"], NST)
            sp.wait_ge(s["upb_done"], NST)
            sp.dma_start(w1, t["L1_ffn_W1"].rearrange("e d f -> d e f")).then_inc(s["ld_w1"], 16)
            sp.wait_ge(s["dn_done"], NST)
            for e in range(NE):
                sp.dma_start(w2[:, e], t["L1_ffn_W2"][e].rearrange("(c p) d -> p c d", p=128)).then_inc(s["ld_w2"], 16)
            sp.wait_ge(s["c_zero"], 1)
            sp.dma_start(z_sorted.rearrange("(n p) d -> p n d", p=128),
                         zeros[:, :].unsqueeze(1).to_broadcast([128, SORTED, D])).then_inc(s["z_zeroed"], 16)

            def load_group(g, u):
                v = z_sorted.rearrange("(g n p) d -> g p n d", n=GROUP, p=128)
                sp.dma_start(z_group[:, u], v[bass.ds(g, 1)].squeeze(0)).then_inc(s["z_loaded"], 16)

            sp.wait_ge(s["z_scattered"], 16 * NB)
            for u in range(2):
                load_group(u, u)
                sp.wait_ge(s["z_loaded"], 16 * (u + 1))
            with sp.Fori(1, SORTED // UNROLL) as n1:
                for u in range(2):
                    sp.wait_ge(s["xg_psum"], (n1 - 1) * 2 + u + 1)
                    apart(sp)
                    load_group(n1 * 2 + u, u)
                    sp.wait_ge(s["z_loaded"], (n1 * 2 + u + 1) * 16)
                    apart(sp)
            out_v = out.rearrange("b s d -> s b d")
            for n in range(TILES):
                sp.wait_ge(s["tile_done"], n + 1)
                sp.dma_start(out_v[:, 4 * n:4 * n + 4, :], xs[:, 4 * n:4 * n + 4, :]).then_inc(s["store"], 16)
            sp.wait_ge(s["store"], 16 * TILES)

        @block.gpsimd
        def _(pool):
            g = nc.gpsimd
            for v, c in ((ident, 0.0), (half, -0.5), (ones_row, 1.0), (one_f, 1.0), (head_mask, 1.0)):
                g.memset(v[:, :], c).then_inc(s["c_const"], 1)
            for e in range(NE):
                g.memset(r_pri[:, e:e + 1], float(NE - e)).then_inc(s["c_const"], 1)
            g.memset(zeros[:, :], 0.0).then_inc(s["c_zero"], 1)
            g.memset(v1[:, :, :, D1:D1 + 1], 1.0).then_inc(s["c_const"], 1)
            pool.wait_ge(s["c_const"], 6 + NE)
            g.affine_select(out=ident[:, :], in_=ident[:, :], compare_op=ALU.not_equal, fill=1.0, base=0,
                            pattern=[[-1, 128]], channel_multiplier=1).then_inc(s["c_ident"], 1)
            g.affine_select(out=head_mask[:, :], in_=head_mask[:, :], compare_op=ALU.is_ge, fill=0.0, base=0,
                            pattern=[[-D1, H]], channel_multiplier=1).then_inc(s["c_hmask"], 1)
            pool.wait_ge(s["c_hmask"], 1)
            g.affine_select(out=head_mask[:, :], in_=head_mask[:, :], compare_op=ALU.is_ge, fill=0.0, base=D1 - 1,
                            pattern=[[D1, H]], channel_multiplier=-1).then_inc(s["c_hmask"], 1)
            pool.wait_ge(s["c_hmask"], 2)

            count = [0]

            def then(ins):
                count[0] += 1
                ins.then_inc(s["rs_step"], 1)
                pool.wait_ge(s["rs_step"], count[0])

            pool.wait_ge(s["st_c"], 2 * NB)
            then(g.tensor_scalar(rs_c[:, :], ln_c[:, :, 1], EPS, 1.0, ALU.add, ALU.mult))
            then(g.tensor_tensor(rs_c[:, :], rs_c[:, :], half[0:NK, :], ALU.pow))
            pool.wait_ge(s["st_x"], 2 * NB)
            then(g.tensor_scalar(rs_x[:, :], ln_x[:, :, 1], EPS, 1.0, ALU.add, ALU.mult))
            then(g.tensor_tensor(rs_x[:, :], rs_x[:, :], half[:, :], ALU.pow))
            then(g.tensor_tensor(rs_x2[:, :], rs_x[:, :], rs_x[:, :], ALU.mult))
            then(g.tensor_tensor(rs_x2[:, :], rs_x2[:, :], ln_x[:, :, 1], ALU.mult))
            then(g.tensor_scalar(rs_x2[:, :], rs_x2[:, :], EPS, 1.0, ALU.add, ALU.mult))
            then(g.tensor_tensor(rs_x2[:, :], rs_x2[:, :], half[:, :], ALU.pow))
            g.tensor_tensor(rs_x[:, :], rs_x[:, :], rs_x2[:, :], ALU.mult).then_inc(s["rs_ready"], 1)
            pool.wait_ge(s["rs_ready"], 1)
            pool.wait_ge(s["ld_gain"], 64)

            def column(a, b, n, w):
                return a[:, bass.ds(b, 1)].to_broadcast([n, w])

            def batch(a, b):
                return a[:, bass.ds(b, 1), :].squeeze(1)

            def stage_inputs(b):
                reach(pool, "kvt_psum", b, 0)
                reach(pool, "kv_copied", b, 0)
                steps = ((p_ctx, batch(cx, b), column(ln_c[:, :, 0], b, NK, D), ALU.subtract),
                         (p_lat, batch(xs, b), column(ln_x[:, :, 0], b, 128, D), ALU.subtract),
                         (p_ctx, p_ctx[:, :], column(rs_c, b, NK, D), ALU.mult),
                         (p_lat, p_lat[:, :], column(rs_x, b, 128, D), ALU.mult),
                         (p_ctx, p_ctx[:, :], g1[0:NK, :], ALU.mult),
                         (p_lat, p_lat[:, :], g2[:, :], ALU.mult),
                         (p_ctx, p_ctx[:, :], b1[0:NK, :], ALU.add),
                         (p_lat, p_lat[:, :], b2[:, :], ALU.add))
                for n, (dst, a, c, op) in enumerate(steps):
                    if n >= 2:
                        reach(pool, "p_step", b, n - 1)
                    g.tensor_tensor(dst[:, :], a, c, op).then_inc(s["p_step"], 1)

            def copy_keys(b):
                reach(pool, "z_psum", b, 0)
                reach(pool, "p_step", b, 8)
                apart(pool)
                g.tensor_copy(kv_ctx[:, :], p_ctx[:, :])
                g.tensor_copy(kv_lat[:, :], p_lat[:, :]).then_inc(s["kv_copied"], 1)

            def normalise(b, q):
                reach(pool, "exp_done", b, 2 * q + 2)
                reach(pool, "inv_ready", b, q + 1)
                p = prob[:, q % 2, :, :]
                g.tensor_tensor(p, p, inv[:, 4 * q:4 * q + 4].unsqueeze(2).to_broadcast([128, 4, KV]),
                                ALU.mult).then_inc(s["p_norm"], 1)

            def rsqrt(b, mv, rs, stats, eps, ready):
                reach(pool, stats, b, 2)
                apart(pool)
                g.tensor_scalar(rs[:, :], mv[:, 1:2], EPS, 1.0, ALU.add, ALU.mult).then_inc(s[eps], 1)
                reach(pool, eps, b, 1)
                g.tensor_tensor(rs[:, :], rs[:, :], half[:, 0:1], ALU.pow).then_inc(s[ready], 1)

            def spread_keys(b):
                reach(pool, "sc_psum", b, 0)
                g.tensor_tensor(kbd[:, :, :], k1T[:, bass.ds(b, 1), :].to_broadcast([128, H, NK]),
                                head_mask[:, :].unsqueeze(2).to_broadcast([128, H, NK]),
                                ALU.mult).then_inc(s["kbd_ready"], 1)

            def below_max(b, q):
                reach(pool, "topk_done", b, 2 * q + 2)
                v = sw[:, 4 * q:4 * q + 4, :, :].rearrange("p h w n -> p h (w n)")
                g.tensor_tensor(v, v, m8[:, 4 * q:4 * q + 4, 0, 0:1].to_broadcast([128, 4, 2 * NK]),
                                ALU.subtract).then_inc(s["sub_done"], 1)

            def keep_top(b, q):
                reach(pool, "e_done", b, q + 1)
                reach(pool, "p1T_psum", b, q + 1 - QUADS)
                g.tensor_tensor(p1[:, 4 * q:4 * q + 4, :], sw[:, 4 * q:4 * q + 4, 0, :], sw[:, 4 * q:4 * q + 4, 1, :],
                                ALU.subtract).then_inc(s["p1_ready"], 1)

            def add_rows(b, rows, normed, done):
                reach(pool, normed, b, 1)
                v = batch(xs, b)
                g.tensor_tensor(v, v, rows[:, :], ALU.add).then_inc(s[done], 1)

            def down_stage(n):
                st = NST - 1 - n
                w = 2 ** st
                nb = HID // (2 * w)
                if n == 0:
                    wait_job(pool, J_WCON)
                    pool.wait_ge(s["ld_bfd"], 16)
                else:
                    pool.wait_ge(s["dn_done"], n)
                for o in range(2):
                    g.tensor_tensor(pairs(dn_t[:, o, :], nb), bf_coef(down_w, st, nb, "i w o")[:, :, :, :, o],
                                    pairs(w_dnT[:, :], nb)[:, :, o:o + 1, :].to_broadcast([128, nb, 2, w]),
                                    ALU.mult).then_inc(s["dn_mul"], 1)
                pool.wait_ge(s["dn_mul"], 2 * n + 2)
                g.tensor_tensor(w_dnT[:, :], dn_t[:, 0, :], dn_t[:, 1, :], ALU.add).then_inc(s["dn_done"], 1)

            def step(i, at):
                P, A, A2, B, C = (at(n) for n in range(5))
                for slot in range(SLOTS):
                    if slot == 0:
                        if B is not None:
                            rsqrt(B, b_mv, b_rs, "b_stats", "b_eps", "brs_ready")
                            spread_keys(B)
                        if C is not None:
                            keep_top(C, 0)
                    if slot == 1:
                        if B is not None:
                            if i == 3:
                                pool.wait_ge(s["c_bo"], 1)
                            add_rows(B, bo, "bz_ready", "xo_added")
                        if C is not None:
                            below_max(C, 1)
                        if A is not None:
                            normalise(A, 0)
                    if slot == 2:
                        if C is not None:
                            keep_top(C, 1)
                        if A is not None:
                            copy_keys(A)
                        if P is not None:
                            stage_inputs(P)
                    if slot == 3:
                        if A2 is not None:
                            rsqrt(A2, f_mv, f_rs, "f_stats", "f_eps", "frs_ready")
                        if C is not None:
                            below_max(C, 2)
                        if A is not None:
                            normalise(A, 1)
                    if slot == 4:
                        if A2 is not None:
                            if i == 2:
                                pool.wait_ge(s["c_ffnb"], 2)
                            add_rows(A2, ffn_bias, "fz_ready", "xb_added")
                        if C is not None:
                            keep_top(C, 2)
                    if slot == 5:
                        if C is not None:
                            below_max(C, 3)
                        if A is not None:
                            normalise(A, 2)
                    if slot == 6 and C is not None:
                        keep_top(C, 3)
                    if slot == 7:
                        if B is not None:
                            below_max(B, 0)
                        if A is not None:
                            normalise(A, 3)
                    if i in (1, 2) and 8 * (i - 1) + slot < NST:
                        down_stage(8 * (i - 1) + slot)

            run_steps(pool, step)

            reach(pool, "e_stats", NB - 1, 1)
            g.tensor_scalar(e_rs[:, :], e_mv[:, :, 1], EPS, 1.0, ALU.add, ALU.mult).then_inc(s["e_eps"], 1)
            pool.wait_ge(s["e_eps"], 1)
            g.tensor_tensor(e_rs[:, :], e_rs[:, :], half[:, :], ALU.pow).then_inc(s["ers_ready"], 1)

            for k in range(NB):
                g.memset(steps_128[:, k:k + 1], 128.0 * k).then_inc(s["c_sort"], 1)
            for k in range(SORTED):
                g.memset(tile_no[:, k:k + 1], float(k)).then_inc(s["c_sort"], 1)
            for w in (before_e, before_p, ones_bf):
                g.memset(w[tuple([slice(None)] * len(w.shape))], 1.0).then_inc(s["c_sort"], 1)
            pool.wait_ge(s["c_sort"], NB + SORTED + 3)
            g.affine_select(out=before_e[:, :, :], in_=before_e[:, :, :], compare_op=ALU.is_ge, fill=0.0, base=-1,
                            pattern=[[1, NE], [-1, NE]], channel_multiplier=0).then_inc(s["c_past"], 1)
            g.affine_select(out=before_p[:, :], in_=before_p[:, :], compare_op=ALU.is_ge, fill=0.0, base=-1,
                            pattern=[[1, 128]], channel_multiplier=-1).then_inc(s["c_past"], 1)

            pool.wait_ge(s["z_zeroed"], 16)
            pool.wait_ge(s["place_ready"], 1)
            for b in range(NB):
                g.indirect_dma_start(z_sorted, bass.IndirectOffsetOnAxis(ap=place[:, b:b + 1], axis=0),
                                     z_all[:, b, :], None).then_inc(s["z_scattered"], 16)
            y_groups = y_sorted.rearrange("(g n p) d -> g p n d", n=GROUP, p=128)
            with pool.Fori(1, SORTED // GROUP + 1) as n1:
                pool.wait_ge(s["ey_ready"], n1 * GROUP)
                apart(pool)
                g.dma_start(y_groups[bass.ds(n1 - 1, 1)].squeeze(0), y_all[:, bass.ds((n1 - 1) * GROUP, GROUP), :])\
                    .then_inc(s["y_stored"], 16)
            pool.wait_ge(s["y_stored"], 16 * (SORTED // GROUP))
            for b in range(NB):
                g.indirect_dma_start(y_back[:, b, :], None, y_sorted,
                                     bass.IndirectOffsetOnAxis(ap=place[:, b:b + 1], axis=0))\
                    .then_inc(s[f"y_part{b // 4}"], 16)

        @block.tensor
        def _(pe):
            mm = nc.tensor.matmul

            def turn(dst, src, rows=128):
                return nc.tensor.transpose(dst, src, ident[0:rows, 0:rows])

            def open_job(k):
                if k >= 8:
                    wait_job(pe, k - 8)
                return bank[k % 8]

            pe.wait_ge(s["c_ident"], 1)
            for k in range(6):
                pe.wait_ge(s["ld_wq" if k < 2 else "ld_wkv"], 16)
                src = wq_in[:, 512 * k:512 * k + 512] if k < 2 else wkv_in[:, 512 * (k - 2):512 * (k - 2) + 512]
                dst = open_job(k)
                for c in range(4):
                    last = turn(dst[:, 128 * c:128 * c + 128], src[:, 128 * c:128 * c + 128])
                last.then_inc(s["set_psum"], 1)

            def head_rows(w, h):
                r, c = DH * (h % 2), INNER * w + 128 * (h // 2)
                return wT[r:r + DH, c:c + 128]

            for k in range(4):
                wait_job(pe, k)
            for q in range(QUADS):
                dst = open_job(J_A + q)
                for n, h in enumerate(job_heads(q)):
                    last = mm(dst[:, 128 * n:128 * n + 128], head_rows(0, h), head_rows(1, h), start=True, stop=True)
                last.then_inc(s["set_psum"], 1)
            pe.wait_ge(s["ld_wout"], 16)
            wait_job(pe, 4)
            wait_job(pe, 5)
            for q in range(QUADS):
                dst = open_job(J_B + q)
                for n, h in enumerate(job_heads(q)):
                    r, c = DH * (h % 2), 128 * (h // 2)
                    last = mm(dst[:, 128 * n:128 * n + 128], head_rows(2, h), wout_in[r:r + DH, c:c + 128],
                              start=True, stop=True)
                last.then_inc(s["set_psum"], 1)
            pe.wait_ge(s["ld_l1w"], 64)
            dst = open_job(J_L1W)
            for n in range(4):
                last = turn(dst[:, 128 * n:128 * n + 128], l1_in[:, n, :])
            last.then_inc(s["set_psum"], 1)
            pe.wait_ge(s["ld_c"], 16)
            for k, (b0, nb) in enumerate(CT_PART):
                dst = open_job(J_CT + k)
                for n in range(nb):
                    last = turn(dst[:, n * NK:(n + 1) * NK], cx[:, b0 + n, :], NK)
                last.then_inc(s["set_psum"], 1)
            pe.wait_ge(s["ld_wcon"], 16)
            dst = open_job(J_WCON)
            for n in range(HC):
                last = turn(dst[:, 128 * n:128 * n + 128], wcon_in[:, n, :])
            last.then_inc(s["set_psum"], 1)
            wait_job(pe, J_L1W)
            for k, (b0, nb) in enumerate(CT_PART):
                wait_job(pe, J_CT + k)
                dst = open_job(J_K1 + k)
                mm(dst[:, 0:nb * NK], l1_wT[:, 1, :], cT[:, b0 * NK:(b0 + nb) * NK], start=True, stop=True)\
                    .then_inc(s["set_psum"], 1)
            pe.wait_ge(s["ld_l1b"], 64)
            for k in range(NB // 4):
                dst = open_job(J_V1 + k)
                for n in range(4):
                    b = 4 * k + n
                    v = dst[0:NK, 128 * n:128 * n + 128]
                    mm(v, one_f[:, 0:NK], bv[:, :], start=True, stop=False)
                    last = mm(v, cT[:, b * NK:(b + 1) * NK], l1_wT[:, 2, :], start=False, stop=True)
                last.then_inc(s["set_psum"], 1)
            for k in range(JOBS - 8, JOBS):
                wait_job(pe, k)
            pe.wait_ge(s["c_mask"], 1)

            reader, now = {}, dict(step=0, at=None)

            def free(name):
                if name in reader:
                    sem_name, lag, n, when = reader[name]
                    reach(pe, sem_name, now["at"](lag + now["step"] - when), n)

            def read_next(name, sem_name, lag, n):
                reader[name] = (sem_name, lag, n, now["step"])

            def keys_T(b):
                free("M")
                reach(pe, "p_step", b, 8)
                turn(M[:, 0:NK], p_ctx[:, :], NK)
                turn(M[:, NK:KV], p_lat[:, :]).then_inc(s["kvt_psum"], 1)
                read_next("M", "kvt_ready", 1, 1)

            def project(b, q):
                free("GZ")
                reach(pe, "kvt_ready", b, 1)
                for n in range(4):
                    last = mm(GZ[:, 128 * n:128 * n + 128], a_w[:, 4 * q + n, :], kvT[:, NK:KV], start=True, stop=True)
                last.then_inc(s["g_psum"], 1)
                read_next("GZ", "g_ready", 1, q + 1)

            def scores(b, p):
                dst = s_bank[p % 2][:, 0:2 * KV].rearrange("p (h n) -> p h n", h=2)
                reach(pe, "exp_done", b, p - 1)
                reach(pe, "g_ready", b, p // 2 + 1)
                apart(pe)
                mm(dst[:, :, 0:NK], ones_row[:, :], mask_row[:, bass.ds(b, 1), :].to_broadcast([1, 2, NK]),
                   start=True, stop=False, skip_group_check=True)
                for n in range(2):
                    last = mm(dst[:, n, :], g_sb[:, (p // 2) % 2, 2 * (p % 2) + n, :], kvT[:, :],
                              start=False, stop=(n == 1), skip_group_check=True)
                last.then_inc(s["s_psum"], 1)

            def probs_T(b, q):
                reach(pe, "p_norm", b, q + 1)
                reach(pe, "pt_ready", b, q)
                for n in range(4):
                    turn(TC[0:NK, 128 * n:128 * n + 128], prob[:, q % 2, n, 0:NK])
                    last = turn(TL[:, 128 * n:128 * n + 128], prob[:, q % 2, n, NK:KV])
                last.then_inc(s["pt_psum"], 1)

            def attend(b, q, lag):
                free("GZ")
                reach(pe, "pt_ready", b, q + 1)
                reach(pe, "kv_copied", b, 1)
                mm(GZ[:, :], kv_ctx[:, :], ptc[:, :, :].rearrange("p h q -> p (h q)"), start=True, stop=False)
                mm(GZ[:, :], kv_lat[:, :], ptl[:, :, :].rearrange("p h q -> p (h q)"), start=False, stop=True)\
                    .then_inc(s["z_psum"], 1)
                read_next("GZ", "z_ready", lag, q + 1)

            def project_out(b, q):
                reach(pe, "z_ready", b, q + 1)
                if q == 0:
                    reach(pe, "x1_ready", b, 0)
                for n in range(4):
                    last = mm(OA[:, 0:D], z_sb[:, n, :], b_w[:, 4 * q + n, :], start=(q == 0 and n == 0),
                              stop=(q == QUADS - 1 and n == 3))
                last.then_inc(s["o_psum"], 1)

            def ffn_T(b):
                free("M")
                reach(pe, "fz_ready", b, 1)
                turn(M[:, 0:128], f_z[:, :]).then_inc(s["fT_psum"], 1)
                read_next("M", "fT_ready", 2, 1)

            def hidden(b):
                free("X")
                reach(pe, "fT_ready", b, 1)
                for n in range(HC):
                    last = mm(X[:, 128 * n:128 * n + 128], w_up[:, 128 * n:128 * n + 128], f_zT[:, :], start=True, stop=True)
                last.then_inc(s["h_psum"], 1)
                read_next("X", "h_ready", 2, 1)

            def down(b):
                free("M")
                reach(pe, "h_ready", b, 1)
                for n in range(HC):
                    last = mm(M[:, 0:D], f_h[:, n, :], w_dn[:, n, :], start=(n == 0), stop=(n == HC - 1))
                last.then_inc(s["y_psum"], 1)
                read_next("M", "x2_ready", 3, 1)

            def second_T(b):
                free("M")
                reach(pe, "bz_ready", b, 1)
                turn(M[:, 0:128], b_z[:, :]).then_inc(s["bT_psum"], 1)
                read_next("M", "bT_ready", 3, 1)

            def queries(b):
                free("M")
                reach(pe, "bT_ready", b, 1)
                mm(M[:, 0:128], l1_wT[:, 0, :], b_zT[:, :], start=True, stop=True).then_inc(s["q_psum"], 1)
                read_next("M", "q_ready", 3, 1)

            def second_scores(b, q):
                free("X")
                reach(pe, "q_ready", b, 1)
                reach(pe, "kbd_ready", b, 1)
                mm(X[:, 0:4 * NK], b_q[:, :], kbd[:, 4 * q:4 * q + 4, :].rearrange("p h n -> p (h n)"),
                   start=True, stop=True).then_inc(s["sc_psum"], 1)
                read_next("X", "sc_ready", 3, q + 1)

            def second_probs_T(b, q):
                free("X")
                reach(pe, "p1_ready", b, q + 1)
                for n in range(4):
                    last = turn(X[0:NK, 128 * n:128 * n + 128], p1[:, 4 * q + n, :])
                last.then_inc(s["p1T_psum"], 1)
                read_next("X", "p1T_ready", 4, q + 1)

            def contexts(b, q):
                free("M")
                reach(pe, "p1T_ready", b, q + 1)
                for n in range(4):
                    c = CT0 + (4 * q + n) * (D1 + 1)
                    last = mm(M[:, c:c + D1 + 1], p1T[:, n, :], v1[:, bass.ds(b, 1), 4 * q + n, :].squeeze(1),
                              start=True, stop=True)
                last.then_inc(s["ctx_psum"], 1)
                if q == QUADS - 1:
                    read_next("M", "cz_ready", 5, 1)

            def context_T(b):
                free("M")
                reach(pe, "cz_ready", b, 1)
                turn(M[:, 0:128], c_z[:, :, :].rearrange("p h d -> p (h d)")).then_inc(s["cT_psum"], 1)
                read_next("M", "cT_ready", 5, 1)

            def second_out(b):
                free("M")
                reach(pe, "cT_ready", b, 1)
                mm(M[:, 0:D], c_zT[:, :], l1_wT[:, 3, :], start=True, stop=True).then_inc(s["o1_psum"], 1)
                read_next("M", "x3_ready", 5, 1)

            def bias_to_columns():
                pe.wait_ge(s["upb_done"], NST + 1)
                for n in range(HC):
                    last = mm(X[:, n:n + 1], bias_up[0:1, 128 * n:128 * n + 128], one_f[:, 0:1], start=True, stop=True)
                last.then_inc(s["late_psum"], 1)
                pe.wait_ge(s["up_done"], NST)
                pe.wait_ge(s["late_ready"], 1)

            def down_weight_back():
                free("X")
                pe.wait_ge(s["dn_done"], NST)
                for n in range(HC):
                    last = turn(X[:, 128 * n:128 * n + 128], w_dnT[:, 128 * n:128 * n + 128])
                last.then_inc(s["late_psum"], 1)
                pe.wait_ge(s["late_ready"], 2)

            def step(i, at):
                now["at"] = at
                P, A, A2, B, C, E = (at(n) for n in range(6))
                for slot in range(SLOTS):
                    if slot == 0:
                        if A is not None:
                            keys_T(A)
                        if A2 is not None:
                            attend(A2, 2, 2)
                        if A is not None:
                            project(A, 0)
                            scores(A, 0)
                        if B is not None:
                            down(B)
                    if slot == 1:
                        if A2 is not None:
                            project_out(A2, 2)
                            probs_T(A2, 3)
                        if A is not None:
                            project(A, 1)
                            scores(A, 1)
                        if E is not None:
                            contexts(E, 3)
                        if C is not None:
                            second_probs_T(C, 0)
                    if slot == 2:
                        if A2 is not None:
                            attend(A2, 3, 2)
                        if A is not None:
                            scores(A, 2)
                        if B is not None:
                            second_T(B)
                        if C is not None:
                            contexts(C, 0)
                        if E is not None:
                            context_T(E)
                    if slot == 3:
                        if A2 is not None:
                            project_out(A2, 3)
                        if A is not None:
                            project(A, 2)
                            probs_T(A, 0)
                            scores(A, 3)
                        if B is not None:
                            queries(B)
                        if C is not None:
                            second_probs_T(C, 1)
                        if E is not None:
                            second_out(E)
                    if slot == 4:
                        if A is not None:
                            attend(A, 0, 1)
                            scores(A, 4)
                        if C is not None:
                            contexts(C, 1)
                        if B is not None:
                            second_scores(B, 0)
                        if i == 2:
                            bias_to_columns()
                    if slot == 5:
                        if A is not None:
                            project_out(A, 0)
                            probs_T(A, 1)
                            project(A, 3)
                        if A2 is not None:
                            ffn_T(A2)
                        if C is not None:
                            second_probs_T(C, 2)
                        if A is not None:
                            scores(A, 5)
                        if B is not None:
                            second_scores(B, 1)
                    if slot == 6:
                        if A is not None:
                            attend(A, 1, 1)
                        if A2 is not None:
                            hidden(A2)
                        if A is not None:
                            scores(A, 6)
                        if C is not None:
                            contexts(C, 2)
                        if B is not None:
                            second_scores(B, 2)
                    if slot == 7:
                        if A is not None:
                            project_out(A, 1)
                            probs_T(A, 2)
                        if C is not None:
                            second_probs_T(C, 3)
                        if A is not None:
                            scores(A, 7)
                        if B is not None:
                            second_scores(B, 3)
                        if i == 2:
                            down_weight_back()
                now["step"] += 1

            run_steps(pe, step)

            pe.wait_ge(s["ld_router"], 32)
            reach(pe, "x3_ready", NB - 1, 1)
            with pe.Fori(1, TILES + 1) as n1:
                pe.wait_ge(s["ez_ready"], n1)
                for n in range(4):
                    last = turn(X[:, 128 * n:128 * n + 128], e_z[:, n, :])
                last.then_inc(s["xT_psum"], 1)
                pe.wait_ge(s["xT_ready"], n1)
                for n in range(4):
                    last = mm(M[:, NE * n:NE * n + NE], x_tile[:, 128 * n:128 * n + 128], wr[:, :], start=True, stop=True)
                last.then_inc(s["lg_psum"], 1)
                pe.wait_ge(s["lg_ready"], n1)

            pe.wait_ge(s["c_past"], 2)
            pe.wait_ge(s["chosen_ready"], 1)
            places, totals = S0[:, 0:NB * NE], S1[:, 0:NE]
            rows = chosen[:, :, :].rearrange("p b e -> p (b e)")
            mm(places, before_p[:, :], rows, start=True, stop=False, skip_group_check=True)
            for k in range(1, NB):
                mm(S0[:, k * NE:NB * NE], ones_bf[:, :], rows[:, 0:(NB - k) * NE], start=False, stop=(k == NB - 1),
                   skip_group_check=True)
            for b in range(NB):
                last = mm(totals, ones_bf[:, :], chosen[:, b, :], start=(b == 0), stop=(b == NB - 1))
            last.then_inc(s["count_psum"], 1)

            pe.wait_ge(s["ld_w1"], 16)
            pe.wait_ge(s["ld_w2"], 16 * NE)
            pe.wait_ge(s["map_ready"], 1)
            pe.wait_ge(s["place_ready"], 1)

            def turn_group(n0, u):
                pe.wait_ge(s["z_loaded"], (n0 * 2 + u + 1) * 16)
                apart(pe)
                for n in range(GROUP):
                    last = turn(X[:, 128 * n:128 * n + 128], z_group[:, u, n, :])
                last.then_inc(s["xg_psum"], 1)

            def tile_up(n0, k, e):
                if k % GROUP == 0:
                    pe.wait_ge(s["xg_ready"], n0 * 2 + k // GROUP + 1)
                if k >= 2:
                    pe.wait_ge(s["gelu_ready"], n0 * UNROLL + k - 1)
                apart(pe)
                mm(bank[k % 2][:, :], x_group[:, k // GROUP, k % GROUP, :], w1[:, bass.ds(e, 1), :].squeeze(1),
                   start=True, stop=True).then_inc(s["up_psum"], 1)

            def tile_turn(n0, k):
                pe.wait_ge(s["gelu_ready"], n0 * UNROLL + k + 1)
                dst = bank[2 + k % 2]
                apart(pe)
                for c in range(HC):
                    last = turn(dst[:, 128 * c:128 * c + 128], h_exp[:, k % 2, 128 * c:128 * c + 128])
                last.then_inc(s["turned"], 1)

            def tile_down(n0, k, e):
                pe.wait_ge(s["hT_ready"], n0 * UNROLL + k + 1)
                if k >= 2:
                    pe.wait_ge(s["ey_ready"], n0 * UNROLL + k - 1)
                apart(pe)
                for c in range(HC):
                    last = mm(bank[4 + k % 2][:, 0:D], hT[:, k % 2, c, :], w2[:, bass.ds(e, 1), c, :].squeeze(1),
                              start=(c == 0), stop=(c == HC - 1))
                last.then_inc(s["ey_psum"], 1)

            with pe.Fori(0, SORTED // UNROLL) as n0:
                experts = [pe.value_load(tile_expert[0:1, bass.ds(n0 * UNROLL + k, 1)], min_val=0, max_val=NE - 1)
                           for k in range(UNROLL)]
                turn_group(n0, 0)
                for k in range(UNROLL):
                    tile_up(n0, k, experts[k])
                    if k == GROUP - 1:
                        turn_group(n0, 1)
                    if k:
                        tile_down(n0, k - 1, experts[k - 1])
                    tile_turn(n0, k)
                tile_down(n0, UNROLL - 1, experts[UNROLL - 1])
                pe.wait_ge(s["ey_ready"], n0 * UNROLL + UNROLL)

        @block.scalar
        def _(act):
            def fn(dst, src, f, **kw):
                return nc.scalar.activation(dst, src, f, **kw)

            def copy(dst, src):
                return fn(dst, src, ACT.Copy)

            act.wait_ge(s["ld_gates"], 32)
            fn(tg[:, :], gates[:, :], ACT.Tanh).then_inc(s["c_gate"], 1)
            move_jobs(act, 0, copy, lambda d, v, c: fn(d, v, ACT.Copy, scale=c),
                      lambda d, v, b: fn(d, v, ACT.Identity, bias=b))

            def keys_out(b):
                reach(act, "kvt_psum", b, 1)
                copy(kvT[:, :], M[:, 0:KV]).then_inc(s["kvt_ready"], 1)

            def projected(b, q):
                reach(act, "g_psum", b, q + 1)
                copy(g_sb[:, q % 2, :, :].rearrange("p h q -> p (h q)"), GZ[:, :]).then_inc(s["g_ready"], 1)

            def exps(b, p):
                reach(act, "max_ready", b, p + 1)
                q = p // 2
                if p % 2 == 0:
                    reach(act, "pt_psum", b, q - 1)
                for n in range(2):
                    h = 2 * p + n
                    last = fn(prob[:, q % 2, 2 * (p % 2) + n, :], s_bank[p % 2][:, n * KV:(n + 1) * KV], ACT.Exp,
                              bias=negmax[:, h:h + 1], accum_out=rowsum[:, h:h + 1])
                last.then_inc(s["exp_done"], 1)

            def probs_out(b, q):
                reach(act, "pt_psum", b, q + 1)
                copy(ptc[:, :, :].rearrange("p h q -> p (h q)"), TC[0:NK, :])
                copy(ptl[:, :, :].rearrange("p h q -> p (h q)"), TL[:, :]).then_inc(s["pt_ready"], 1)

            def attended(b, q):
                reach(act, "z_psum", b, q + 1)
                copy(z_sb[:, :, :].rearrange("p h q -> p (h q)"), GZ[:, :]).then_inc(s["z_ready"], 1)

            def move(b, dst, psum, ready):
                reach(act, psum, b, 1)
                copy(dst[:, :], M[:, 0:128]).then_inc(s[ready], 1)

            def gelus(b):
                reach(act, "h_psum", b, 1)
                for n in range(HC):
                    last = fn(f_h[:, n, :], X[:, 128 * n:128 * n + 128], ACT.Gelu, bias=bias_cols[:, n:n + 1])
                last.then_inc(s["h_ready"], 1)

            def queries_out(b):
                reach(act, "q_psum", b, 1)
                fn(b_q[:, :], M[:, 0:128], ACT.Identity, bias=bq[:, 0:1]).then_inc(s["q_ready"], 1)

            def second_scores_out(b, q):
                reach(act, "sc_psum", b, q + 1)
                reach(act, "p1_ready", b, q + 1 - QUADS)
                copy(sw[:, 4 * q:4 * q + 4, 0, :], X[:, 0:4 * NK].rearrange("p (h n) -> p h n", h=4))\
                    .then_inc(s["sc_ready"], 1)

            def second_exps(b, q):
                reach(act, "sub_done", b, q + 1)
                v = sw[:, 4 * q:4 * q + 4, :, :].rearrange("p h w n -> p (h w n)")
                fn(v, v, ACT.Exp, scale=SC1).then_inc(s["e_done"], 1)

            def second_probs_out(b, q):
                reach(act, "p1T_psum", b, q + 1)
                copy(p1T[:, :, :].rearrange("p h q -> p (h q)"), X[0:NK, :]).then_inc(s["p1T_ready"], 1)

            def step(i, at):
                P, A, A2, B, C, E = (at(n) for n in range(6))
                for slot in range(SLOTS):
                    if slot == 0:
                        if A is not None:
                            keys_out(A)
                        if A2 is not None:
                            attended(A2, 2)
                        if A is not None:
                            projected(A, 0)
                            exps(A, 0)
                    if slot == 1:
                        if A2 is not None:
                            probs_out(A2, 3)
                        if A is not None:
                            projected(A, 1)
                            exps(A, 1)
                        if C is not None:
                            second_probs_out(C, 0)
                            second_exps(C, 1)
                    if slot == 2:
                        if A2 is not None:
                            attended(A2, 3)
                        if A is not None:
                            exps(A, 2)
                        if B is not None:
                            move(B, b_zT, "bT_psum", "bT_ready")
                        if E is not None:
                            move(E, c_zT, "cT_psum", "cT_ready")
                    if slot == 3:
                        if A is not None:
                            projected(A, 2)
                            probs_out(A, 0)
                            exps(A, 3)
                        if B is not None:
                            queries_out(B)
                        if C is not None:
                            second_probs_out(C, 1)
                            second_exps(C, 2)
                    if slot == 4:
                        if A is not None:
                            attended(A, 0)
                            exps(A, 4)
                        if B is not None:
                            second_scores_out(B, 0)
                        if i == 2:
                            act.wait_ge(s["late_psum"], 1)
                            copy(bias_cols[:, :], X[:, 0:HC]).then_inc(s["late_ready"], 1)
                    if slot == 5:
                        if A is not None:
                            probs_out(A, 1)
                            projected(A, 3)
                        if A2 is not None:
                            move(A2, f_zT, "fT_psum", "fT_ready")
                        if C is not None:
                            second_probs_out(C, 2)
                        if A is not None:
                            exps(A, 5)
                        if B is not None:
                            second_scores_out(B, 1)
                        if C is not None:
                            second_exps(C, 3)
                    if slot == 6:
                        if A is not None:
                            attended(A, 1)
                        if A2 is not None:
                            if i == 2:
                                act.wait_ge(s["late_ready"], 1)
                            gelus(A2)
                        if A is not None:
                            exps(A, 6)
                        if B is not None:
                            second_scores_out(B, 2)
                    if slot == 7:
                        if A is not None:
                            probs_out(A, 2)
                        if C is not None:
                            second_probs_out(C, 3)
                        if A is not None:
                            exps(A, 7)
                        if B is not None:
                            second_scores_out(B, 3)
                            second_exps(B, 0)
                        if i == 2:
                            act.wait_ge(s["late_psum"], 2)
                            copy(w_dn[:, :, :].rearrange("p c d -> p (c d)"), X[:, :]).then_inc(s["late_ready"], 1)

            run_steps(act, step)

            with act.Fori(1, TILES + 1) as n1:
                act.wait_ge(s["xT_psum"], n1)
                copy(x_tile[:, :], X[:, :]).then_inc(s["xT_ready"], 1)
            act.wait_ge(s["lg_ready"], TILES)
            fn(route[:, :, :], route[:, :, :], ACT.Exp, scale=-1.0).then_inc(s["r_exp"], 1)

            def group_out(n0, u):
                act.wait_ge(s["xg_psum"], n0 * 2 + u + 1)
                copy(x_group[:, u, :, :].rearrange("p n q -> p (n q)"), X[:, :]).then_inc(s["xg_ready"], 1)

            with act.Fori(0, SORTED // UNROLL) as n0:
                group_out(n0, 0)
                for k in range(UNROLL):
                    act.wait_ge(s["up_psum"], n0 * UNROLL + k + 1)
                    if k >= 2:
                        act.wait_ge(s["turned"], n0 * UNROLL + k - 1)
                    fn(h_exp[:, k % 2, :], bank[k % 2][:, :], ACT.Gelu).then_inc(s["gelu_ready"], 1)
                    if k == GROUP - 1:
                        group_out(n0, 1)
                act.wait_ge(s["turned"], n0 * UNROLL + UNROLL)

        @block.vector
        def _(dve):
            v = nc.vector

            dve.wait_ge(s["ld_c"], 16)
            for b in range(NB):
                v.bn_stats(st6c[:, b, :], cx[:, b, :]).then_inc(s["st_c"], 1)
            dve.wait_ge(s["st_c"], NB)
            for b in range(NB):
                v.bn_aggr(ln_c[:, b, :], st6c[:, b, :]).then_inc(s["st_c"], 1)
            dve.wait_ge(s["ld_x"], 16)
            for b in range(NB):
                v.bn_stats(st6[:, b, :], xs[:, b, :]).then_inc(s["st_x"], 1)
            dve.wait_ge(s["st_x"], NB)
            for b in range(NB):
                v.bn_aggr(ln_x[:, b, :], st6[:, b, :]).then_inc(s["st_x"], 1)
            dve.wait_ge(s["ld_mask"], 16)
            v.tensor_scalar(mask_row[:, :, :], mask_u8[:, :, :], 1.0, -MASKED, ALU.subtract, ALU.mult)\
                .then_inc(s["c_mask"], 1)
            move_jobs(dve, 1, v.tensor_copy, lambda d, x, c: v.tensor_scalar(d, x, c, None, ALU.mult),
                      lambda d, x, b: v.tensor_scalar(d, x, b, None, ALU.add))
            dve.wait_ge(s["c_gate"], 1)
            dve.wait_ge(s["ld_ffnb"], 32)
            v.tensor_tensor(ffn_bias[:, :], ffn_bias[:, :], dn_bias[:, :], ALU.add).then_inc(s["c_ffnb"], 1)
            v.tensor_scalar(bo[:, :], bo[:, :], tg[:, 1:2], None, ALU.mult).then_inc(s["c_bo"], 1)
            dve.wait_ge(s["c_ffnb"], 1)
            v.tensor_scalar(ffn_bias[:, :], ffn_bias[:, :], tg[:, 2:3], None, ALU.mult).then_inc(s["c_ffnb"], 1)

            def up_stage(cur, part, n, mul, done, rows):
                w = 2 ** n
                nb = HID // (2 * w)
                if n == 0:
                    dve.wait_ge(s["ld_bfu"], 16)
                    dve.wait_ge(s["ld_wexp"], 48)
                else:
                    dve.wait_ge(s[done], n)
                for i in range(2):
                    v.tensor_tensor(pairs(part[:, i, :], nb), bf_coef(up_w, n, nb, "o w i")[0:rows, :, :, :, i],
                                    pairs(cur[:, :], nb)[:, :, i:i + 1, :].to_broadcast([rows, nb, 2, w]),
                                    ALU.mult).then_inc(s[mul], 1)
                dve.wait_ge(s[mul], 2 * n + 2)
                v.tensor_tensor(cur[:, :], part[:, 0, :], part[:, 1, :], ALU.add).then_inc(s[done], 1)

            def batch(a, b):
                return a[:, bass.ds(b, 1), :].squeeze(1)

            def maxima(b, p):
                reach(dve, "s_psum", b, p + 1)
                v.tensor_reduce(negmax[:, 2 * p:2 * p + 2], s_bank[p % 2][:, 0:2 * KV].rearrange("p (h n) -> p h n", h=2),
                                AX_X, ALU.max, negate=True).then_inc(s["max_ready"], 1)

            def inverses(b, q):
                reach(dve, "exp_done", b, 2 * q + 2)
                v.reciprocal(inv[:, 4 * q:4 * q + 4], rowsum[:, 4 * q:4 * q + 4]).then_inc(s["inv_ready"], 1)

            def residual(b, src, gate, ready):
                x = batch(xs, b)
                v.scalar_tensor_tensor(x, src, tg[:, gate:gate + 1], x, ALU.mult, ALU.add).then_inc(s[ready], 1)

            def statistics(b, st, mv, ready, done):
                reach(dve, ready, b, 1)
                apart(dve)
                v.bn_stats(st[:, :], batch(xs, b)).then_inc(s[done], 1)
                reach(dve, done, b, 1)
                apart(dve)
                v.bn_aggr(mv[:, :], st[:, :]).then_inc(s[done], 1)

            def normal(b, dst, mv, rs, rs_ready, done):
                reach(dve, rs_ready, b, 1)
                v.tensor_scalar(dst[:, :], batch(xs, b), mv[:, 0:1], rs[:, 0:1], ALU.subtract, ALU.mult).then_inc(s[done], 1)

            def top_32(b, k):
                if k % 2 == 0:
                    reach(dve, "sc_ready", b, k // 2 + 1)
                apart(dve)
                heads = (2 * k, 2 * k + 1)
                step = 0
                for r in range(ROUNDS):
                    src = 0 if r == 0 else 1
                    for h in heads:
                        if r:
                            dve.wait_ge(s["topk_step"], step - 1)
                        v.max(m8[:, h, r, :], sw[:, h, src, :]).then_inc(s["topk_step"], 1)
                        step += 1
                    for h in heads:
                        dve.wait_ge(s["topk_step"], step - 1)
                        v.match_replace(sw[:, h, 1, :], m8[:, h, r, :], sw[:, h, src, :], TAKEN)\
                            .then_inc(s["topk_step"], 1)
                        step += 1
                dve.wait_ge(s["topk_step"], step)
                dve.sem_clear(s["topk_step"]).then_inc(s["topk_done"], 1)

            def context_out(b):
                reach(dve, "ctx_psum", b, QUADS)
                c = M[:, CT0:CT0 + H * (D1 + 1)].rearrange("p (h d) -> p h d", h=H)
                v.reciprocal(c_inv[:, :], c[:, :, D1]).then_inc(s["cinv_ready"], 1)
                reach(dve, "cinv_ready", b, 1)
                v.tensor_tensor(c_z[:, :, :], c[:, :, 0:D1], c_inv[:, :].unsqueeze(2).to_broadcast([128, H, D1]),
                                ALU.mult).then_inc(s["cz_ready"], 1)

            def step(i, at):
                P, A, A2, B, C, E = (at(n) for n in range(6))
                for slot in range(SLOTS):
                    if A is not None:
                        if slot == 3 and A2 is not None:
                            pass
                        maxima(A, slot)
                    if slot == 0 and B is not None:
                        reach(dve, "y_psum", B, 1)
                        reach(dve, "xb_added", B, 1)
                        residual(B, M[:, 0:D], 2, "x2_ready")
                        statistics(B, b_st, b_mv, "x2_ready", "b_stats")
                    if slot == 1 and E is not None:
                        context_out(E)
                    if slot == 3:
                        if A2 is not None:
                            reach(dve, "o_psum", A2, QUADS)
                            residual(A2, OA[:, 0:D], 0, "x1_ready")
                            statistics(A2, f_st, f_mv, "x1_ready", "f_stats")
                        if E is not None:
                            reach(dve, "o1_psum", E, 1)
                            reach(dve, "xo_added", E, 1)
                            residual(E, M[:, 0:D], 1, "x3_ready")
                            statistics(E, c_st, c_mv, "x3_ready", "c_stats")
                            reach(dve, "c_stats", E, 2)
                            apart(dve)
                            v.tensor_copy(batch(e_mv, E), c_mv[:, :]).then_inc(s["e_stats"], 1)
                    if slot < 5 and C is not None:
                        top_32(C, slot + 3)
                    if slot >= 5 and B is not None:
                        top_32(B, slot - 5)
                    if slot % 2 == 1 and A is not None:
                        inverses(A, slot // 2)
                    if slot == 0 and B is not None:
                        normal(B, b_z, b_mv, b_rs, "brs_ready", "bz_ready")
                    if slot == 3 and A2 is not None:
                        normal(A2, f_z, f_mv, f_rs, "frs_ready", "fz_ready")
                    n = 8 * (i - 1) + slot if i in (1, 2) else NST
                    if n < NST:
                        up_stage(w_up, up_t, n, "up_mul", "up_done", 128)
                        up_stage(bias_up, upb_t, n, "upb_mul", "upb_done", 1)
                    if n == NST - 1:
                        dve.wait_ge(s["upb_done"], NST)
                        v.tensor_tensor(bias_up[:, :], bias_up[:, :], up_bias[:, :], ALU.add).then_inc(s["upb_done"], 1)

            run_steps(dve, step)

            dve.wait_ge(s["ers_ready"], 1)
            with dve.Fori(1, TILES + 1) as n1:
                b0 = (n1 - 1) * 4
                v.tensor_tensor(e_z[:, :, :], xs[:, bass.ds(b0, 4), :],
                                e_mv[:, bass.ds(b0, 4), 0:1].to_broadcast([128, 4, D]), ALU.subtract).then_inc(s["ez_sub"], 1)
                dve.wait_ge(s["ez_sub"], n1)
                v.tensor_tensor(e_z[:, :, :], e_z[:, :, :], e_rs[:, bass.ds(b0, 4)].unsqueeze(2).to_broadcast([128, 4, D]),
                                ALU.mult).then_inc(s["ez_ready"], 1)
                dve.wait_ge(s["ez_ready"], n1)
                v.tensor_copy(z_all[:, bass.ds(b0, 4), :], e_z[:, :, :]).then_inc(s["ez_kept"], 1)
                dve.wait_ge(s["lg_psum"], n1)
                v.tensor_tensor(route[:, bass.ds(b0, 4), :], M[:, 0:4 * NE].rearrange("p (n e) -> p n e", n=4),
                                br[:, :].unsqueeze(1).to_broadcast([128, 4, NE]), ALU.add).then_inc(s["lg_ready"], 1)
                dve.wait_ge(s["ez_kept"], n1)

            count = [0]

            def then(ins):
                count[0] += 1
                ins.then_inc(s["r_step"], 1)
                dve.wait_ge(s["r_step"], count[0])

            wide = [128, NB, NE]
            dve.wait_ge(s["r_exp"], 1)
            then(v.tensor_scalar(route[:, :, :], route[:, :, :], 1.0, None, ALU.add))
            then(v.reciprocal(route[:, :, :], route[:, :, :]))
            then(v.reduce_max(r_max[:, :], route[:, :, :], AX_X))
            then(v.tensor_tensor(r_eq[:, :, :], route[:, :, :], r_max[:, :].unsqueeze(2).to_broadcast(wide), ALU.is_equal))
            then(v.tensor_tensor(r_eq[:, :, :], r_eq[:, :, :], r_pri[:, :].unsqueeze(1).to_broadcast(wide), ALU.mult))
            then(v.reduce_max(r_top[:, :], r_eq[:, :, :], AX_X))
            v.tensor_tensor(chosen[:, :, :], r_eq[:, :, :], r_top[:, :].unsqueeze(2).to_broadcast(wide), ALU.is_equal)\
                .then_inc(s["chosen_ready"], 1)
            v.tensor_scalar(coef[:, :], r_max[:, :], tg[:, 3:4], None, ALU.mult).then_inc(s["coef_ready"], 1)

            dve.wait_ge(s["c_past"], 2)
            dve.wait_ge(s["count_psum"], 1)
            places, totals = S0[:, 0:NB * NE].rearrange("p (b e) -> p b e", b=NB), S1[:, 0:NE]
            then(v.tensor_tensor(n_full[:, :, :], totals.unsqueeze(2).to_broadcast([128, NE, NB]),
                                 steps_128[:, :].unsqueeze(1).to_broadcast([128, NE, NB]), ALU.is_gt))
            then(v.tensor_reduce(n_tiles[:, :], n_full[:, :, :], AX_X, ALU.add))
            then(v.tensor_tensor(n_before[:, :, :], before_e[:, :, :], n_tiles[:, :].unsqueeze(1).to_broadcast([128, NE, NE]),
                                 ALU.mult))
            then(v.tensor_reduce(start[:, :], n_before[:, :, :], AX_X, ALU.add))
            v.tensor_tensor(end[:, :], start[:, :], n_tiles[:, :], ALU.add)
            then(v.tensor_scalar(start[:, :], start[:, :], 128.0, None, ALU.mult))
            then(v.tensor_tensor(place_e[:, :, :], places, start[:, :].unsqueeze(1).to_broadcast(wide), ALU.add))
            then(v.tensor_tensor(place_e[:, :, :], place_e[:, :, :], chosen[:, :, :], ALU.mult))
            then(v.tensor_reduce(place_f[:, :], place_e[:, :, :], AX_X, ALU.add))
            v.tensor_copy(place[:, :], place_f[:, :]).then_inc(s["place_ready"], 1)
            then(v.tensor_tensor(t_past[:, :, :], tile_no[:, :].unsqueeze(2).to_broadcast([128, SORTED, NE]),
                                 end[:, :].unsqueeze(1).to_broadcast([128, SORTED, NE]), ALU.is_ge))
            then(v.tensor_reduce(t_exp[:, :], t_past[:, :, :], AX_X, ALU.add))
            v.tensor_scalar(tile_expert[:, :], t_exp[:, :], NE - 1.0, None, ALU.min).then_inc(s["map_ready"], 1)

            def output_out(n0, k):
                dve.wait_ge(s["ey_psum"], n0 * UNROLL + k + 1)
                apart(dve)
                v.tensor_copy(y_all[:, bass.ds(n0 * UNROLL + k, 1), :].squeeze(1), bank[4 + k % 2][:, 0:D])\
                    .then_inc(s["ey_ready"], 1)

            with dve.Fori(0, SORTED // UNROLL) as n0:
                for k in range(UNROLL):
                    dve.wait_ge(s["turned"], n0 * UNROLL + k + 1)
                    v.tensor_copy(hT[:, k % 2, :, :].rearrange("p c q -> p (c q)"), bank[2 + k % 2][:, :])\
                        .then_inc(s["hT_ready"], 1)
                    if k:
                        output_out(n0, k - 1)
                output_out(n0, UNROLL - 1)

            dve.wait_ge(s["coef_ready"], 1)
            for n in range(TILES):
                y, x = y_back[:, 4 * n:4 * n + 4, :], xs[:, 4 * n:4 * n + 4, :]
                dve.wait_ge(s[f"y_part{n}"], 64)
                v.tensor_tensor(y, y, coef[:, 4 * n:4 * n + 4].unsqueeze(2).to_broadcast([128, 4, D]), ALU.mult)\
                    .then_inc(s["y_times"], 1)
                dve.wait_ge(s["y_times"], n + 1)
                v.tensor_tensor(x, x, y, ALU.add).then_inc(s["tile_done"], 1)


INPUTS = ["x", "ctx_1024", "mask_BxS2_bk0", "g_xattn", "g_ffn", "L0_xattn_g1", "L0_xattn_b1", "L0_xattn_g2",
          "L0_xattn_b2", "L0_xattn_Wq", "L0_xattn_Wkv", "L0_xattn_Wout", "L0_ffn_W_exp", "L0_ffn_b_exp",
          "L0_ffn_up_weights", "L0_ffn_up_bias", "L0_ffn_down_weights", "L0_ffn_W_con", "L0_ffn_b_con",
          "L0_ffn_down_bias", "L1_xattn_Wq", "L1_xattn_bq", "L1_xattn_Wk", "L1_xattn_bk", "L1_xattn_Wv",
          "L1_xattn_bv", "L1_xattn_Wo", "L1_xattn_bo", "L1_ffn_Wr", "L1_ffn_br", "L1_ffn_W1", "L1_ffn_W2"]


def kernel(**inputs):
    import numpy as _np
    import concourse.bacc as _bacc
    from concourse.bass_utils import run_bass_kernel_spmd as _run

    nc = _bacc.Bacc("TRN2", target_bir_lowering=False, num_devices=1)
    arrays, t = {}, {}
    for name in INPUTS:
        a = _np.ascontiguousarray(inputs[name])
        arrays[f"in_{name}"] = a
        t[name] = nc.dram_tensor(f"in_{name}", a.shape, mybir.dt.from_np(a.dtype), kind="ExternalInput").ap()
    out = nc.dram_tensor("out_x", t["x"].shape, F32, kind="ExternalOutput").ap()
    flamingo_kernel(nc, t, out)
    r = _run(nc, [arrays], core_ids=[0])
    return r.results[0]["out_x"]
```

```python
from contextlib import ExitStack

import numpy as np

import concourse.bass as bass
from concourse import mybir

ALU = mybir.AluOpType
ACT = mybir.ActivationFunctionType
F32 = mybir.dt.float32
BF16 = mybir.dt.bfloat16
U8 = mybir.dt.uint8
I32 = mybir.dt.int32
U32 = mybir.dt.uint32
AX_X = mybir.AxisListType.X

EPS = 1e-5
MASKED = -3.0e38
TAKEN = -3.0e38
SLOTS = 8
LAGS = 6


def flamingo_kernel(nc, t, out):
    NB, S, D = t["x"].shape
    NK = t["ctx_1024"].shape[1]
    H = 16
    INNER = t["L0_xattn_Wq"].shape[1]
    DH = INNER // H
    NC = INNER // 128
    KV = NK + S
    QUADS = H // 4
    HID = t["L0_ffn_W_exp"].shape[1]
    HC = HID // 128
    NST = t["L0_ffn_up_weights"].shape[0]
    D1 = D // H
    SC1 = 1.0 / float(np.sqrt(D1))
    NE = t["L1_ffn_W1"].shape[0]
    ROUNDS = 4
    TILES = NB // 4
    GROUP = 4
    UNROLL = 2 * GROUP
    SORTED = -(-(NB + NE - 1) // UNROLL) * UNROLL
    assert S == 128 and D == 128 and DH == 64 and HID == 512 and NK * 4 <= 512

    with ExitStack() as ctx:
        def sb(name, shape, dt=F32):
            return ctx.enter_context(nc.sbuf_tensor(name, shape, dt))

        def sem(name):
            return ctx.enter_context(nc.semaphore(name))

        xs = sb("xs", [128, NB, D])
        cx = sb("cx", [NK, NB, D])
        ident = sb("ident", [128, 128])
        head_mask = sb("head_mask", [128, H])
        half = sb("half", [128, NB])
        ones_row = sb("ones_row", [1, 128], BF16)
        one_f = sb("one_f", [1, 128])
        mask_u8 = sb("mask_u8", [1, NB, NK], U8)
        mask_row = sb("mask_row", [1, NB, NK], BF16)
        g1 = sb("g1", [128, D])
        b1 = sb("b1", [128, D])
        g2 = sb("g2", [128, D])
        b2 = sb("b2", [128, D])
        gates = sb("gates", [128, 4])
        tg = sb("tg", [128, 4])
        a_w = sb("a_w", [128, H, D])
        b_w = sb("b_w", [128, H, D])
        w_up = sb("w_up", [128, HID])
        bias_up = sb("bias_up", [1, HID])
        up_bias = sb("up_bias", [1, HID])
        bias_cols = sb("bias_cols", [128, HC])
        w_dnT = sb("w_dnT", [128, HID])
        w_dn = sb("w_dn", [128, HC, D])
        ffn_bias = sb("ffn_bias", [128, D])
        dn_bias = sb("dn_bias", [128, D])
        l1_wT = sb("l1_wT", [128, 4, D])
        bq = sb("bq", [128, 1])
        bk = sb("bk", [128, 1])
        bv = sb("bv", [128, 1])
        bo = sb("bo", [128, D])
        k1T = sb("k1T", [128, NB, NK])
        v1 = sb("v1", [NK, NB, H, D1 + 1])
        wr = sb("wr", [128, NE])
        br = sb("br", [128, NE])

        NBF = NST * (HID // 2) * 4
        bf_w = sb("bf_w", [128, 2 * NBF])
        up_w, down_w = bf_w[:, 0:NBF], bf_w[:, NBF:2 * NBF]
        w1 = bf_w[:, 0:NE * HID].rearrange("p (e f) -> p e f", e=NE)
        w2 = bf_w[:, NBF:NBF + NE * HID].rearrange("p (e c d) -> p e c d", e=NE, c=HC)
        raw = sb("raw", [128, 4 * INNER])
        wq_in, wkv_in, wout_in = raw[:, 0:INNER], raw[:, INNER:3 * INNER], raw[:, 3 * INNER:4 * INNER]
        wT = sb("wT", [128, 3 * INNER])
        l1_in = sb("l1_in", [128, 4, D])
        wcon_in = sb("wcon_in", [128, HC, D])
        cT = wT[:, 0:NB * NK]
        y_all = raw[:, 0:SORTED * D].rearrange("p (n d) -> p n d", n=SORTED)
        up_t, dn_t, upb_t = (raw[0:n, 2 * HID * k:2 * HID * k + 2 * HID].rearrange("p (o f) -> p o f", o=2)
                             for k, n in enumerate((128, 128, 1)))

        ln_x = sb("ln_x", [128, NB, 2])
        ln_c = sb("ln_c", [NK, NB, 2])
        st6 = sb("st6", [128, NB, 6])
        st6c = sb("st6c", [NK, NB, 6])
        rs_x = sb("rs_x", [128, NB])
        rs_x2 = sb("rs_x2", [128, NB])
        rs_c = sb("rs_c", [NK, NB])
        p_lat = sb("p_lat", [128, D])
        p_ctx = sb("p_ctx", [NK, D])
        kv_lat = sb("kv_lat", [128, D])
        kv_ctx = sb("kv_ctx", [NK, D])
        kvT = sb("kvT", [128, KV])
        g_sb = sb("g_sb", [128, 2, 4, 128])
        negmax = sb("negmax", [128, H])
        rowsum = sb("rowsum", [128, H])
        inv = sb("inv", [128, H])
        prob = sb("prob", [128, 2, 4, KV])
        ptc = sb("ptc", [NK, 4, 128])
        ptl = sb("ptl", [128, 4, 128])
        z_sb = sb("z_sb", [128, 4, 128])
        f_st = sb("f_st", [128, 6])
        f_mv = sb("f_mv", [128, 2])
        f_rs = sb("f_rs", [128, 1])
        f_z = sb("f_z", [128, D])
        f_zT = sb("f_zT", [128, 128])
        f_h = sb("f_h", [128, HC, 128])
        b_st = sb("b_st", [128, 6])
        b_mv = sb("b_mv", [128, 2])
        b_rs = sb("b_rs", [128, 1])
        b_z = sb("b_z", [128, D])
        b_zT = sb("b_zT", [128, 128])
        b_q = sb("b_q", [128, 128])
        sw_at, p1_at = 2 * H * NK, 3 * H * NK
        sw = raw[:, 0:sw_at].rearrange("p (h w n) -> p h w n", h=H, w=2)
        p1 = raw[:, sw_at:p1_at].rearrange("p (h n) -> p h n", h=H)
        kbd = wT[:, NB * NK:NB * NK + H * NK].rearrange("p (h n) -> p h n", h=H)
        m8 = sb("m8", [128, H, ROUNDS, 8])
        p1T = sb("p1T", [NK, 4, 128])
        c_inv = sb("c_inv", [128, H])
        c_z = sb("c_z", [128, H, D1])
        c_zT = sb("c_zT", [128, 128])
        c_st = sb("c_st", [128, 6])
        c_mv = sb("c_mv", [128, 2])
        c_rs = sb("c_rs", [128, 1])
        r_z = sb("r_z", [128, D])
        r_zT = sb("r_zT", [128, 128])
        route = sb("route", [128, NB, NE])
        r_max = sb("r_max", [128, NB])
        r_top = sb("r_top", [128, NB])
        r_eq = sb("r_eq", [128, NB, NE])
        r_pri = sb("r_pri", [128, NE])
        chosen = sb("chosen", [128, NB, NE], BF16)
        coef = sb("coef", [128, NB])
        spare = [NE * HID]

        def beside(n):
            at = spare[0]
            if at <= NBF < at + n:
                at = NBF + NE * HID
            spare[0] = at + n
            assert at + n <= 2 * NBF
            return bf_w[:, at:at + n]

        z_group = beside(2 * GROUP * D).rearrange("p (u n d) -> p u n d", u=2, n=GROUP)
        x_group = beside(2 * GROUP * S).rearrange("p (u n q) -> p u n q", u=2, n=GROUP)
        h_exp = beside(2 * HID).rearrange("p (u f) -> p u f", u=2)
        hT = beside(2 * HID).rearrange("p (u c q) -> p u c q", u=2, c=HC)
        z_all = beside(NB * D).rearrange("p (b d) -> p b d", b=NB)
        y_back = z_all
        steps_128 = sb("steps_128", [128, NB])
        tile_no = sb("tile_no", [128, SORTED])
        before_e = sb("before_e", [128, NE, NE])
        before_p = sb("before_p", [128, 128], BF16)
        ones_bf = sb("ones_bf", [128, 128], BF16)
        zeros = sb("zeros", [128, D])
        n_full = beside(NE * NB).rearrange("p (e k) -> p e k", e=NE)
        n_tiles = sb("n_tiles", [128, NE])
        n_before = beside(NE * NE).rearrange("p (e k) -> p e k", e=NE)
        start = sb("start", [128, NE])
        end = sb("end", [128, NE])
        t_past = beside(SORTED * NE).rearrange("p (t e) -> p t e", t=SORTED)
        t_exp = sb("t_exp", [128, SORTED])
        tile_expert = sb("tile_expert", [128, SORTED], I32)
        place_e = beside(NB * NE).rearrange("p (b e) -> p b e", b=NB)
        place_f = sb("place_f", [128, NB])
        place = sb("place", [128, NB], U32)

        z_sorted = nc.dram_tensor("z_sorted", [SORTED * 128, D], F32, kind="Internal").ap()
        y_sorted = nc.dram_tensor("y_sorted", [SORTED * 128, D], F32, kind="Internal").ap()

        bank = [ctx.enter_context(nc.psum_tensor(f"bank{n}", [128, 512], F32)) for n in range(8)]
        GZ, S0, S1, TC, TL, OA, X, M = bank
        s_bank = [S0, S1]
        CT0 = 256

        PER = dict(p_step=8, kvt_psum=1, kvt_ready=1, kv_copied=1, g_psum=4, g_ready=4, s_psum=8, max_ready=8,
                   exp_done=8, inv_ready=4, p_norm=4, pt_psum=4, pt_ready=4, z_psum=4, z_ready=4, o_psum=4,
                   x1_ready=1, f_stats=2, f_eps=1, frs_ready=1, fz_ready=1, fT_psum=1, fT_ready=1, h_psum=1,
                   h_ready=1, y_psum=1, xb_added=1, x2_ready=1, b_stats=2, b_eps=1, brs_ready=1, bz_ready=1,
                   bT_psum=1, bT_ready=1, q_psum=1, q_ready=1, kbd_ready=1, sc_psum=4, sc_ready=4,
                   topk_done=8, sub_done=4, e_done=4, p1_ready=4, p1T_psum=4, p1T_ready=4,
                   ctx_psum=4, cinv_ready=1, cz_ready=1, cT_psum=1, cT_ready=1, o1_psum=1, xo_added=1,
                   x3_ready=1, c_stats=2, c_eps=1, crs_ready=1, rz_ready=1, rz_kept=1, rT_psum=1, rT_ready=1,
                   lg_psum=1, lg_ready=1)
        s = {n: sem(n) for n in PER}
        for n in """ld_x ld_c ld_mask ld_gain ld_gates ld_wq ld_wkv ld_wout ld_l1w ld_l1b ld_wcon ld_wexp
                ld_bfu ld_bfd ld_ffnb ld_router ld_w1 ld_w2 c_const c_ident c_hmask c_mask c_gate c_ffnb c_bo
                st_x st_c topk_step waits_apart rs_step rs_ready set_psum set_act set_dve up_mul up_done upb_mul upb_done dn_mul
                dn_done late_psum late_ready r_exp r_step chosen_ready count_psum map_ready place_ready coef_ready c_sort c_zero c_past
                z_zeroed z_scattered z_loaded xg_psum xg_ready up_psum gelu_ready turned hT_ready
                ey_psum ey_ready y_stored y_part0 y_part1 y_part2 y_part3 y_times tile_done store""".split():
            s[n] = sem(n)

        def reach(eng, name, b, n):
            if b is None:
                return
            value = b * PER[name] + n
            if not isinstance(b, int) or value > 0:
                eng.wait_ge(s[name], value)

        def apart(eng):
            eng.sem_inc(s["waits_apart"], 1)

        def run_steps(eng, step):
            def peeled(i):
                step(i, lambda n: i - n if 0 <= i - n < NB else None)

            for i in range(LAGS):
                peeled(i)
            with eng.Fori(LAGS, NB) as i:
                step(None, lambda n: i - n)
            for i in range(NB, NB + LAGS - 1):
                peeled(i)

        J_A = 6
        J_B = J_A + QUADS
        J_L1W = J_B + QUADS
        J_CT = J_L1W + 1
        J_WCON = J_CT + 3
        J_BO = J_WCON + 1
        J_K1 = J_BO + 1
        J_V1 = J_K1 + 3
        JOBS = J_V1 + NB // 4
        assert J_BO % 2
        CT_PART = [(0, 6), (6, 6), (12, 4)]

        DOWN_AT = {(0, 7): (0, 1, 2), (1, 2): (3,), (1, 3): (4,), (1, 4): (5,), (1, 5): (6,), (1, 6): (7,), (1, 7): (8,)}
        UP_AT = {at: n for n, at in enumerate([(1, n) for n in range(SLOTS)] + [(2, 0)])}
        assert NST == len(UP_AT)

        def job_heads(q):
            return [8 * (q // 2) + q % 2 + 2 * n for n in range(4)]

        def job_part(w, q):
            h0 = job_heads(q)[0]
            return w[:, h0:h0 + 7:2, :]

        def wait_job(eng, k):
            eng.wait_ge(s["set_act" if k % 2 == 0 else "set_dve"], k // 2 + 1)

        def move_jobs(eng, jobs, copy, scaled, biased, added=None):
            done = s["set_dve" if jobs[0] % 2 else "set_act"]
            for k in jobs:
                src = bank[k % 8]
                eng.wait_ge(s["set_psum"], k + 1)
                if k < J_A:
                    last = copy(wT[:, 512 * k:512 * k + 512], src[:, :])
                elif k < J_B:
                    q = k - J_A
                    last = scaled(job_part(a_w, q), src[:, :].rearrange("p (h d) -> p h d", h=4), DH ** -0.5)
                elif k < J_L1W:
                    q = k - J_B
                    last = copy(job_part(b_w, q), src[:, :].rearrange("p (h d) -> p h d", h=4))
                elif k == J_L1W:
                    last = copy(l1_wT[:, :, :], src[:, :].rearrange("p (w d) -> p w d", w=4))
                elif k < J_WCON:
                    b0, nb = CT_PART[k - J_CT]
                    last = copy(cT[:, b0 * NK:(b0 + nb) * NK], src[:, 0:nb * NK])
                elif k == J_WCON:
                    last = copy(w_dnT[:, :], src[:, :])
                elif k == J_BO:
                    eng.wait_ge(s["ld_l1b"], 64)
                    last = added(bo[:, :], src[:, 0:D])
                elif k < J_V1:
                    b0, nb = CT_PART[k - J_K1]
                    eng.wait_ge(s["ld_l1b"], 64)
                    last = biased(k1T[:, b0:b0 + nb, :], src[:, 0:nb * NK].rearrange("p (b n) -> p b n", b=nb), bk[:, 0:1])
                else:
                    n = k - J_V1
                    for j in range(4):
                        last = copy(v1[:, 4 * n + j, :, 0:D1],
                                    src[0:NK, 128 * j:128 * j + 128].rearrange("p (h d) -> p h d", h=H))
                last.then_inc(done, 1)

        def pairs(v, nb):
            return v.rearrange("p (m o w) -> p m o w", m=nb, o=2)

        def bf_coef(w, st, nb, order):
            v = w[:, st * 2 * HID:(st + 1) * 2 * HID]
            if order == "o w i":
                return v.rearrange("p (m w o i) -> p m o w i", m=nb, o=2, i=2)
            return v.rearrange("p (m w o i) -> p m i w o", m=nb, o=2, i=2)

        block = ctx.enter_context(nc.Block())

        @block.sync
        def _(sp):
            def row(name, n=128):
                a = t[name]
                return a.rearrange("(a d) -> a d", a=1).to_broadcast([n, a.shape[0]])

            sp.dma_start(wq_in, t["L0_xattn_Wq"]).then_inc(s["ld_wq"], 16)
            sp.dma_start(wkv_in, t["L0_xattn_Wkv"]).then_inc(s["ld_wkv"], 16)
            sp.dma_start(cx[:, :, :], t["ctx_1024"].rearrange("b n d -> n b d")).then_inc(s["ld_c"], 16)
            sp.dma_start(xs[:, :, :], t["x"].rearrange("b s d -> s b d")).then_inc(s["ld_x"], 16)
            sp.dma_start(wout_in.rearrange("p (c e) -> p c e", c=NC),
                         t["L0_xattn_Wout"].rearrange("(c p) e -> p c e", p=128)).then_inc(s["ld_wout"], 16)
            for dst, name in ((g1, "L0_xattn_g1"), (b1, "L0_xattn_b1"), (g2, "L0_xattn_g2"), (b2, "L0_xattn_b2")):
                sp.dma_start(dst[:, :], row(name)).then_inc(s["ld_gain"], 16)
            sp.dma_start(mask_u8[:, :, :], t["mask_BxS2_bk0"].rearrange("(a b) n -> a b n", a=1)).then_inc(s["ld_mask"], 16)
            sp.dma_start(gates[:, 0:2], row("g_xattn")).then_inc(s["ld_gates"], 16)
            sp.dma_start(gates[:, 2:4], row("g_ffn")).then_inc(s["ld_gates"], 16)
            for n, name in enumerate(("Wq", "Wk", "Wv", "Wo")):
                sp.dma_start(l1_in[:, n, :], t[f"L1_xattn_{name}"]).then_inc(s["ld_l1w"], 16)
            sp.dma_start(wcon_in[:, :, :], t["L0_ffn_W_con"].rearrange("(c p) d -> p c d", p=128)).then_inc(s["ld_wcon"], 16)
            sp.dma_start(bq[:, :], t["L1_xattn_bq"].rearrange("(p a) -> p a", a=1)).then_inc(s["ld_l1b"], 16)
            sp.dma_start(bk[:, :], t["L1_xattn_bk"].rearrange("(p a) -> p a", a=1)).then_inc(s["ld_l1b"], 16)
            sp.dma_start(bv[:, :], t["L1_xattn_bv"].rearrange("(p a) -> p a", a=1)).then_inc(s["ld_l1b"], 16)
            sp.dma_start(bo[:, :], row("L1_xattn_bo")).then_inc(s["ld_l1b"], 16)
            sp.dma_start(w_up[:, :], t["L0_ffn_W_exp"]).then_inc(s["ld_wexp"], 16)
            sp.dma_start(bias_up[:, :], row("L0_ffn_b_exp", 1)).then_inc(s["ld_wexp"], 16)
            sp.dma_start(up_bias[:, :], row("L0_ffn_up_bias", 1)).then_inc(s["ld_wexp"], 16)
            for dst, name, done in ((down_w, "L0_ffn_down_weights", "ld_bfd"), (up_w, "L0_ffn_up_weights", "ld_bfu")):
                flat = t[name].rearrange("n k a b -> (n k a b)").rearrange("(a m) -> a m", a=1)
                sp.dma_start(dst, flat.to_broadcast([128, NBF])).then_inc(s[done], 16)
            sp.dma_start(ffn_bias[:, :], row("L0_ffn_b_con")).then_inc(s["ld_ffnb"], 16)
            sp.dma_start(dn_bias[:, :], row("L0_ffn_down_bias")).then_inc(s["ld_ffnb"], 16)
            sp.dma_start(wr[:, :], t["L1_ffn_Wr"]).then_inc(s["ld_router"], 16)
            sp.dma_start(br[:, :], row("L1_ffn_br")).then_inc(s["ld_router"], 16)
            sp.wait_ge(s["up_done"], NST)
            sp.wait_ge(s["upb_done"], NST)
            sp.dma_start(w1, t["L1_ffn_W1"].rearrange("e d f -> d e f")).then_inc(s["ld_w1"], 16)
            sp.wait_ge(s["dn_done"], NST)
            for e in range(NE):
                sp.dma_start(w2[:, e], t["L1_ffn_W2"][e].rearrange("(c p) d -> p c d", p=128)).then_inc(s["ld_w2"], 16)
            sp.wait_ge(s["c_zero"], 1)
            sp.dma_start(z_sorted.rearrange("(n p) d -> p n d", p=128),
                         zeros[:, :].unsqueeze(1).to_broadcast([128, SORTED, D])).then_inc(s["z_zeroed"], 16)

            def load_group(g, u):
                v = z_sorted.rearrange("(g n p) d -> g p n d", n=GROUP, p=128)
                sp.dma_start(z_group[:, u], v[bass.ds(g, 1)].squeeze(0)).then_inc(s["z_loaded"], 16)

            sp.wait_ge(s["z_scattered"], 16 * NB)
            for u in range(2):
                load_group(u, u)
                sp.wait_ge(s["z_loaded"], 16 * (u + 1))
            with sp.Fori(1, SORTED // UNROLL) as n1:
                for u in range(2):
                    sp.wait_ge(s["xg_psum"], (n1 - 1) * 2 + u + 1)
                    apart(sp)
                    load_group(n1 * 2 + u, u)
                    sp.wait_ge(s["z_loaded"], (n1 * 2 + u + 1) * 16)
                    apart(sp)
            out_v = out.rearrange("b s d -> s b d")
            for n in range(TILES):
                sp.wait_ge(s["tile_done"], n + 1)
                sp.dma_start(out_v[:, 4 * n:4 * n + 4, :], xs[:, 4 * n:4 * n + 4, :]).then_inc(s["store"], 16)
            sp.wait_ge(s["store"], 16 * TILES)

        @block.gpsimd
        def _(pool):
            g = nc.gpsimd
            for v, c in ((ident, 0.0), (half, -0.5), (ones_row, 1.0), (one_f, 1.0), (head_mask, 1.0)):
                g.memset(v[:, :], c).then_inc(s["c_const"], 1)
            for e in range(NE):
                g.memset(r_pri[:, e:e + 1], float(NE - e)).then_inc(s["c_const"], 1)
            g.memset(zeros[:, :], 0.0).then_inc(s["c_zero"], 1)
            g.memset(v1[:, :, :, D1:D1 + 1], 1.0).then_inc(s["c_const"], 1)
            pool.wait_ge(s["c_const"], 6 + NE)
            g.affine_select(out=ident[:, :], in_=ident[:, :], compare_op=ALU.not_equal, fill=1.0, base=0,
                            pattern=[[-1, 128]], channel_multiplier=1).then_inc(s["c_ident"], 1)
            g.affine_select(out=head_mask[:, :], in_=head_mask[:, :], compare_op=ALU.is_ge, fill=0.0, base=0,
                            pattern=[[-D1, H]], channel_multiplier=1).then_inc(s["c_hmask"], 1)
            pool.wait_ge(s["c_hmask"], 1)
            g.affine_select(out=head_mask[:, :], in_=head_mask[:, :], compare_op=ALU.is_ge, fill=0.0, base=D1 - 1,
                            pattern=[[D1, H]], channel_multiplier=-1).then_inc(s["c_hmask"], 1)
            pool.wait_ge(s["c_hmask"], 2)

            count = [0]

            def then(ins):
                count[0] += 1
                ins.then_inc(s["rs_step"], 1)
                pool.wait_ge(s["rs_step"], count[0])

            pool.wait_ge(s["st_c"], 2 * NB)
            then(g.tensor_scalar(rs_c[:, :], ln_c[:, :, 1], EPS, 1.0, ALU.add, ALU.mult))
            then(g.tensor_tensor(rs_c[:, :], rs_c[:, :], half[0:NK, :], ALU.pow))
            pool.wait_ge(s["st_x"], 2 * NB)
            then(g.tensor_scalar(rs_x[:, :], ln_x[:, :, 1], EPS, 1.0, ALU.add, ALU.mult))
            then(g.tensor_tensor(rs_x[:, :], rs_x[:, :], half[:, :], ALU.pow))
            then(g.tensor_tensor(rs_x2[:, :], rs_x[:, :], rs_x[:, :], ALU.mult))
            then(g.tensor_tensor(rs_x2[:, :], rs_x2[:, :], ln_x[:, :, 1], ALU.mult))
            then(g.tensor_scalar(rs_x2[:, :], rs_x2[:, :], EPS, 1.0, ALU.add, ALU.mult))
            then(g.tensor_tensor(rs_x2[:, :], rs_x2[:, :], half[:, :], ALU.pow))
            g.tensor_tensor(rs_x[:, :], rs_x[:, :], rs_x2[:, :], ALU.mult).then_inc(s["rs_ready"], 1)
            pool.wait_ge(s["rs_ready"], 1)
            pool.wait_ge(s["ld_gain"], 64)

            def column(a, b, n, w):
                return a[:, bass.ds(b, 1)].to_broadcast([n, w])

            def batch(a, b):
                return a[:, bass.ds(b, 1), :].squeeze(1)

            def stage_inputs(b):
                reach(pool, "kvt_psum", b, 0)
                reach(pool, "kv_copied", b, 0)
                steps = ((p_ctx, batch(cx, b), column(ln_c[:, :, 0], b, NK, D), ALU.subtract),
                         (p_lat, batch(xs, b), column(ln_x[:, :, 0], b, 128, D), ALU.subtract),
                         (p_ctx, p_ctx[:, :], column(rs_c, b, NK, D), ALU.mult),
                         (p_lat, p_lat[:, :], column(rs_x, b, 128, D), ALU.mult),
                         (p_ctx, p_ctx[:, :], g1[0:NK, :], ALU.mult),
                         (p_lat, p_lat[:, :], g2[:, :], ALU.mult),
                         (p_ctx, p_ctx[:, :], b1[0:NK, :], ALU.add),
                         (p_lat, p_lat[:, :], b2[:, :], ALU.add))
                for n, (dst, a, c, op) in enumerate(steps):
                    if n >= 2:
                        reach(pool, "p_step", b, n - 1)
                    g.tensor_tensor(dst[:, :], a, c, op).then_inc(s["p_step"], 1)

            def copy_keys(b):
                reach(pool, "z_psum", b, 0)
                reach(pool, "p_step", b, 8)
                apart(pool)
                g.tensor_copy(kv_ctx[:, :], p_ctx[:, :])
                g.tensor_copy(kv_lat[:, :], p_lat[:, :]).then_inc(s["kv_copied"], 1)

            def normalise(b, q):
                reach(pool, "exp_done", b, 2 * q + 2)
                reach(pool, "inv_ready", b, q + 1)
                p = prob[:, q % 2, :, :]
                g.tensor_tensor(p, p, inv[:, 4 * q:4 * q + 4].unsqueeze(2).to_broadcast([128, 4, KV]),
                                ALU.mult).then_inc(s["p_norm"], 1)

            def rsqrt(b, mv, rs, stats, eps, ready):
                reach(pool, stats, b, 2)
                apart(pool)
                g.tensor_scalar(rs[:, :], mv[:, 1:2], EPS, 1.0, ALU.add, ALU.mult).then_inc(s[eps], 1)
                reach(pool, eps, b, 1)
                g.tensor_tensor(rs[:, :], rs[:, :], half[:, 0:1], ALU.pow).then_inc(s[ready], 1)

            def spread_keys(b):
                reach(pool, "sc_psum", b, 0)
                g.tensor_tensor(kbd[:, :, :], k1T[:, bass.ds(b, 1), :].to_broadcast([128, H, NK]),
                                head_mask[:, :].unsqueeze(2).to_broadcast([128, H, NK]),
                                ALU.mult).then_inc(s["kbd_ready"], 1)

            def below_max(b, q):
                reach(pool, "topk_done", b, 2 * q + 2)
                v = sw[:, 4 * q:4 * q + 4, :, :].rearrange("p h w n -> p h (w n)")
                g.tensor_tensor(v, v, m8[:, 4 * q:4 * q + 4, 0, 0:1].to_broadcast([128, 4, 2 * NK]),
                                ALU.subtract).then_inc(s["sub_done"], 1)

            def keep_top(b, q):
                reach(pool, "e_done", b, q + 1)
                reach(pool, "p1T_psum", b, q + 1 - QUADS)
                g.tensor_tensor(p1[:, 4 * q:4 * q + 4, :], sw[:, 4 * q:4 * q + 4, 0, :], sw[:, 4 * q:4 * q + 4, 1, :],
                                ALU.subtract).then_inc(s["p1_ready"], 1)

            def keep_input(b):
                reach(pool, "rz_ready", b, 1)
                apart(pool)
                g.tensor_copy(batch(z_all, b), r_z[:, :]).then_inc(s["rz_kept"], 1)

            def add_rows(b, rows, normed, done):
                reach(pool, normed, b, 1)
                v = batch(xs, b)
                g.tensor_tensor(v, v, rows[:, :], ALU.add).then_inc(s[done], 1)

            def down_stage(n):
                st = NST - 1 - n
                w = 2 ** st
                nb = HID // (2 * w)
                if n == 0:
                    wait_job(pool, J_WCON)
                    pool.wait_ge(s["ld_bfd"], 16)
                else:
                    pool.wait_ge(s["dn_done"], n)
                for o in range(2):
                    g.tensor_tensor(pairs(dn_t[:, o, :], nb), bf_coef(down_w, st, nb, "i w o")[:, :, :, :, o],
                                    pairs(w_dnT[:, :], nb)[:, :, o:o + 1, :].to_broadcast([128, nb, 2, w]),
                                    ALU.mult).then_inc(s["dn_mul"], 1)
                pool.wait_ge(s["dn_mul"], 2 * n + 2)
                g.tensor_tensor(w_dnT[:, :], dn_t[:, 0, :], dn_t[:, 1, :], ALU.add).then_inc(s["dn_done"], 1)

            def step(i, at):
                P, A, A2, B, C, E = (at(n) for n in range(6))
                for slot in range(SLOTS):
                    if slot == 0:
                        if C is not None:
                            keep_top(C, 0)
                        if B is not None:
                            rsqrt(B, b_mv, b_rs, "b_stats", "b_eps", "brs_ready")
                            spread_keys(B)
                    if slot == 1:
                        if B is not None:
                            if i == 3:
                                pool.wait_ge(s["c_bo"], 1)
                            add_rows(B, bo, "bz_ready", "xo_added")
                        if C is not None:
                            below_max(C, 1)
                        if A is not None:
                            normalise(A, 0)
                    if slot == 2:
                        if C is not None:
                            keep_top(C, 1)
                        if A is not None:
                            copy_keys(A)
                    if slot == 3:
                        if C is not None:
                            below_max(C, 2)
                        if A2 is not None:
                            rsqrt(A2, f_mv, f_rs, "f_stats", "f_eps", "frs_ready")
                        if E is not None:
                            rsqrt(E, c_mv, c_rs, "c_stats", "c_eps", "crs_ready")
                        if A is not None:
                            normalise(A, 1)
                    if slot == 4:
                        if A2 is not None:
                            if i == 2:
                                pool.wait_ge(s["c_ffnb"], 2)
                            add_rows(A2, ffn_bias, "fz_ready", "xb_added")
                        if C is not None:
                            keep_top(C, 2)
                        if P is not None:
                            stage_inputs(P)
                    if slot == 5:
                        if C is not None:
                            below_max(C, 3)
                        if A is not None:
                            normalise(A, 2)
                        if E is not None:
                            keep_input(E)
                    if slot == 6 and C is not None:
                        keep_top(C, 3)
                    if slot == 7:
                        if B is not None:
                            below_max(B, 0)
                        if A is not None:
                            normalise(A, 3)
                    for n in DOWN_AT.get((i, slot), ()):
                        down_stage(n)

            run_steps(pool, step)

            for k in range(NB):
                g.memset(steps_128[:, k:k + 1], 128.0 * k).then_inc(s["c_sort"], 1)
            for k in range(SORTED):
                g.memset(tile_no[:, k:k + 1], float(k)).then_inc(s["c_sort"], 1)
            for w in (before_e, before_p, ones_bf):
                g.memset(w[tuple([slice(None)] * len(w.shape))], 1.0).then_inc(s["c_sort"], 1)
            pool.wait_ge(s["c_sort"], NB + SORTED + 3)
            g.affine_select(out=before_e[:, :, :], in_=before_e[:, :, :], compare_op=ALU.is_ge, fill=0.0, base=-1,
                            pattern=[[1, NE], [-1, NE]], channel_multiplier=0).then_inc(s["c_past"], 1)
            g.affine_select(out=before_p[:, :], in_=before_p[:, :], compare_op=ALU.is_ge, fill=0.0, base=-1,
                            pattern=[[1, 128]], channel_multiplier=-1).then_inc(s["c_past"], 1)

            pool.wait_ge(s["z_zeroed"], 16)
            reach(pool, "rz_kept", NB - 1, 1)
            pool.wait_ge(s["place_ready"], 1)
            for b in range(NB):
                g.indirect_dma_start(z_sorted, bass.IndirectOffsetOnAxis(ap=place[:, b:b + 1], axis=0),
                                     z_all[:, b, :], None).then_inc(s["z_scattered"], 16)
            y_groups = y_sorted.rearrange("(g n p) d -> g p n d", n=GROUP, p=128)
            with pool.Fori(1, SORTED // GROUP + 1) as n1:
                pool.wait_ge(s["ey_ready"], n1 * GROUP)
                apart(pool)
                g.dma_start(y_groups[bass.ds(n1 - 1, 1)].squeeze(0), y_all[:, bass.ds((n1 - 1) * GROUP, GROUP), :])\
                    .then_inc(s["y_stored"], 16)
            pool.wait_ge(s["y_stored"], 16 * (SORTED // GROUP))
            for b in range(NB):
                g.indirect_dma_start(y_back[:, b, :], None, y_sorted,
                                     bass.IndirectOffsetOnAxis(ap=place[:, b:b + 1], axis=0))\
                    .then_inc(s[f"y_part{b // 4}"], 16)

        @block.tensor
        def _(pe):
            mm = nc.tensor.matmul

            def turn(dst, src, rows=128):
                return nc.tensor.transpose(dst, src, ident[0:rows, 0:rows])

            def open_job(k):
                if k >= 8:
                    wait_job(pe, k - 8)
                return bank[k % 8]

            pe.wait_ge(s["c_ident"], 1)
            for k in range(6):
                pe.wait_ge(s["ld_wq" if k < 2 else "ld_wkv"], 16)
                src = wq_in[:, 512 * k:512 * k + 512] if k < 2 else wkv_in[:, 512 * (k - 2):512 * (k - 2) + 512]
                dst = open_job(k)
                for c in range(4):
                    last = turn(dst[:, 128 * c:128 * c + 128], src[:, 128 * c:128 * c + 128])
                last.then_inc(s["set_psum"], 1)

            def head_rows(w, h):
                r, c = DH * (h % 2), INNER * w + 128 * (h // 2)
                return wT[r:r + DH, c:c + 128]

            for k in range(4):
                wait_job(pe, k)
            for q in range(QUADS):
                dst = open_job(J_A + q)
                for n, h in enumerate(job_heads(q)):
                    last = mm(dst[:, 128 * n:128 * n + 128], head_rows(0, h), head_rows(1, h), start=True, stop=True)
                last.then_inc(s["set_psum"], 1)
            pe.wait_ge(s["ld_wout"], 16)
            wait_job(pe, 4)
            wait_job(pe, 5)
            for q in range(QUADS):
                dst = open_job(J_B + q)
                for n, h in enumerate(job_heads(q)):
                    r, c = DH * (h % 2), 128 * (h // 2)
                    last = mm(dst[:, 128 * n:128 * n + 128], head_rows(2, h), wout_in[r:r + DH, c:c + 128],
                              start=True, stop=True)
                last.then_inc(s["set_psum"], 1)
            pe.wait_ge(s["ld_l1w"], 64)
            dst = open_job(J_L1W)
            for n in range(4):
                last = turn(dst[:, 128 * n:128 * n + 128], l1_in[:, n, :])
            last.then_inc(s["set_psum"], 1)
            pe.wait_ge(s["ld_c"], 16)
            for k, (b0, nb) in enumerate(CT_PART):
                dst = open_job(J_CT + k)
                for n in range(nb):
                    last = turn(dst[:, n * NK:(n + 1) * NK], cx[:, b0 + n, :], NK)
                last.then_inc(s["set_psum"], 1)
            pe.wait_ge(s["ld_wcon"], 16)
            dst = open_job(J_WCON)
            for n in range(HC):
                last = turn(dst[:, 128 * n:128 * n + 128], wcon_in[:, n, :])
            last.then_inc(s["set_psum"], 1)
            wait_job(pe, J_L1W)
            pe.wait_ge(s["ld_l1b"], 64)
            dst = open_job(J_BO)
            mm(dst[:, 0:D], bv[:, 0:1].to_broadcast([128, 128]), l1_wT[:, 3, :], start=True, stop=True)\
                .then_inc(s["set_psum"], 1)
            for k, (b0, nb) in enumerate(CT_PART):
                wait_job(pe, J_CT + k)
                dst = open_job(J_K1 + k)
                mm(dst[:, 0:nb * NK], l1_wT[:, 1, :], cT[:, b0 * NK:(b0 + nb) * NK], start=True, stop=True)\
                    .then_inc(s["set_psum"], 1)
            for k in range(NB // 4):
                dst = open_job(J_V1 + k)
                for n in range(4):
                    b = 4 * k + n
                    v = dst[0:NK, 128 * n:128 * n + 128]
                    last = mm(v, cT[:, b * NK:(b + 1) * NK], l1_wT[:, 2, :], start=True, stop=True)
                last.then_inc(s["set_psum"], 1)
            for k in range(JOBS - 8, JOBS):
                wait_job(pe, k)
            pe.wait_ge(s["c_mask"], 1)

            reader, now = {}, dict(step=0, at=None)

            def free(name):
                if name in reader:
                    sem_name, lag, n, when = reader[name]
                    reach(pe, sem_name, now["at"](lag + now["step"] - when), n)

            def read_next(name, sem_name, lag, n):
                reader[name] = (sem_name, lag, n, now["step"])

            def keys_T(b):
                free("M")
                reach(pe, "p_step", b, 8)
                turn(M[:, 0:NK], p_ctx[:, :], NK)
                turn(M[:, NK:KV], p_lat[:, :]).then_inc(s["kvt_psum"], 1)
                read_next("M", "kvt_ready", 1, 1)

            def project(b, q):
                free("GZ")
                reach(pe, "kvt_ready", b, 1)
                for n in range(4):
                    last = mm(GZ[:, 128 * n:128 * n + 128], a_w[:, 4 * q + n, :], kvT[:, NK:KV], start=True, stop=True)
                last.then_inc(s["g_psum"], 1)
                read_next("GZ", "g_ready", 1, q + 1)

            def scores(b, p):
                dst = s_bank[p % 2][:, 0:2 * KV].rearrange("p (h n) -> p h n", h=2)
                reach(pe, "exp_done", b, p - 1)
                reach(pe, "g_ready", b, p // 2 + 1)
                apart(pe)
                mm(dst[:, :, 0:NK], ones_row[:, :], mask_row[:, bass.ds(b, 1), :].to_broadcast([1, 2, NK]),
                   start=True, stop=False, skip_group_check=True)
                for n in range(2):
                    last = mm(dst[:, n, :], g_sb[:, (p // 2) % 2, 2 * (p % 2) + n, :], kvT[:, :],
                              start=False, stop=(n == 1), skip_group_check=True)
                last.then_inc(s["s_psum"], 1)

            def probs_T(b, q):
                reach(pe, "p_norm", b, q + 1)
                reach(pe, "pt_ready", b, q)
                for n in range(4):
                    turn(TC[0:NK, 128 * n:128 * n + 128], prob[:, q % 2, n, 0:NK])
                    last = turn(TL[:, 128 * n:128 * n + 128], prob[:, q % 2, n, NK:KV])
                last.then_inc(s["pt_psum"], 1)

            def attend(b, q, lag):
                free("GZ")
                reach(pe, "pt_ready", b, q + 1)
                reach(pe, "kv_copied", b, 1)
                mm(GZ[:, :], kv_ctx[:, :], ptc[:, :, :].rearrange("p h q -> p (h q)"), start=True, stop=False)
                mm(GZ[:, :], kv_lat[:, :], ptl[:, :, :].rearrange("p h q -> p (h q)"), start=False, stop=True)\
                    .then_inc(s["z_psum"], 1)
                read_next("GZ", "z_ready", lag, q + 1)

            def project_out(b, q):
                reach(pe, "z_ready", b, q + 1)
                if q == 0:
                    reach(pe, "x1_ready", b, 0)
                for n in range(4):
                    last = mm(OA[:, 0:D], z_sb[:, n, :], b_w[:, 4 * q + n, :], start=(q == 0 and n == 0),
                              stop=(q == QUADS - 1 and n == 3))
                last.then_inc(s["o_psum"], 1)

            def ffn_T(b):
                free("M")
                reach(pe, "fz_ready", b, 1)
                turn(M[:, 0:128], f_z[:, :]).then_inc(s["fT_psum"], 1)
                read_next("M", "fT_ready", 2, 1)

            def hidden(b):
                free("X")
                reach(pe, "fT_ready", b, 1)
                for n in range(HC):
                    last = mm(X[:, 128 * n:128 * n + 128], w_up[:, 128 * n:128 * n + 128], f_zT[:, :], start=True, stop=True)
                last.then_inc(s["h_psum"], 1)
                read_next("X", "h_ready", 2, 1)

            def down(b):
                free("M")
                reach(pe, "h_ready", b, 1)
                for n in range(HC):
                    last = mm(M[:, 0:D], f_h[:, n, :], w_dn[:, n, :], start=(n == 0), stop=(n == HC - 1))
                last.then_inc(s["y_psum"], 1)
                read_next("M", "x2_ready", 3, 1)

            def second_T(b):
                free("M")
                reach(pe, "bz_ready", b, 1)
                turn(M[:, 0:128], b_z[:, :]).then_inc(s["bT_psum"], 1)
                read_next("M", "bT_ready", 3, 1)

            def queries(b):
                free("M")
                reach(pe, "bT_ready", b, 1)
                mm(M[:, 0:128], l1_wT[:, 0, :], b_zT[:, :], start=True, stop=True).then_inc(s["q_psum"], 1)
                read_next("M", "q_ready", 3, 1)

            def second_scores(b, q):
                free("X")
                reach(pe, "q_ready", b, 1)
                reach(pe, "kbd_ready", b, 1)
                mm(X[:, 0:4 * NK], b_q[:, :], kbd[:, 4 * q:4 * q + 4, :].rearrange("p h n -> p (h n)"),
                   start=True, stop=True).then_inc(s["sc_psum"], 1)
                read_next("X", "sc_ready", 3, q + 1)

            def second_probs_T(b, q, lag):
                free("X")
                reach(pe, "p1_ready", b, q + 1)
                for n in range(4):
                    last = turn(X[0:NK, 128 * n:128 * n + 128], p1[:, 4 * q + n, :])
                last.then_inc(s["p1T_psum"], 1)
                read_next("X", "p1T_ready", lag, q + 1)

            def contexts(b, q):
                free("M")
                reach(pe, "p1T_ready", b, q + 1)
                for n in range(4):
                    c = CT0 + (4 * q + n) * (D1 + 1)
                    last = mm(M[:, c:c + D1 + 1], p1T[:, n, :], v1[:, bass.ds(b, 1), 4 * q + n, :].squeeze(1),
                              start=True, stop=True)
                last.then_inc(s["ctx_psum"], 1)
                if q == QUADS - 1:
                    read_next("M", "cz_ready", 5, 1)

            def context_T(b):
                free("M")
                reach(pe, "cz_ready", b, 1)
                turn(M[:, 0:128], c_z[:, :, :].rearrange("p h d -> p (h d)")).then_inc(s["cT_psum"], 1)
                read_next("M", "cT_ready", 5, 1)

            def second_out(b):
                free("M")
                reach(pe, "cT_ready", b, 1)
                mm(M[:, 0:D], c_zT[:, :], l1_wT[:, 3, :], start=True, stop=True).then_inc(s["o1_psum"], 1)
                read_next("M", "x3_ready", 5, 1)

            def router_T(b):
                free("M")
                reach(pe, "rz_ready", b, 1)
                turn(M[:, 0:128], r_z[:, :]).then_inc(s["rT_psum"], 1)
                read_next("M", "rT_ready", 5, 1)

            def logits(b):
                free("M")
                reach(pe, "rT_ready", b, 1)
                mm(M[:, 0:NE], r_zT[:, :], wr[:, :], start=True, stop=True).then_inc(s["lg_psum"], 1)
                read_next("M", "lg_ready", 5, 1)

            def bias_to_columns():
                pe.wait_ge(s["upb_done"], NST + 1)
                for n in range(HC):
                    last = mm(X[:, n:n + 1], bias_up[0:1, 128 * n:128 * n + 128], one_f[:, 0:1], start=True, stop=True)
                last.then_inc(s["late_psum"], 1)
                pe.wait_ge(s["up_done"], NST)
                pe.wait_ge(s["late_ready"], 1)

            def down_weight_back():
                free("X")
                pe.wait_ge(s["dn_done"], NST)
                for n in range(HC):
                    last = turn(X[:, 128 * n:128 * n + 128], w_dnT[:, 128 * n:128 * n + 128])
                last.then_inc(s["late_psum"], 1)
                pe.wait_ge(s["late_ready"], 2)

            def step(i, at):
                now["at"] = at
                P, A, A2, B, C, E = (at(n) for n in range(6))
                for slot in range(SLOTS):
                    if slot == 0:
                        if A is not None:
                            keys_T(A)
                        if A2 is not None:
                            attend(A2, 2, 2)
                        if B is not None:
                            down(B)
                        if A is not None:
                            project(A, 0)
                        if A2 is not None:
                            project_out(A2, 2)
                        if E is not None:
                            second_probs_T(E, 3, 5)
                        if A is not None:
                            scores(A, 0)
                    if slot == 1:
                        if A2 is not None:
                            probs_T(A2, 3)
                        if A is not None:
                            project(A, 1)
                            scores(A, 1)
                        if E is not None:
                            contexts(E, 3)
                        if C is not None:
                            second_probs_T(C, 0, 4)
                    if slot == 2:
                        if A2 is not None:
                            attend(A2, 3, 2)
                        if B is not None:
                            second_T(B)
                        if A is not None:
                            scores(A, 2)
                        if C is not None:
                            contexts(C, 0)
                        if B is not None:
                            queries(B)
                    if slot == 3:
                        if A2 is not None:
                            project_out(A2, 3)
                        if E is not None:
                            context_T(E)
                        if A is not None:
                            project(A, 2)
                            probs_T(A, 0)
                        if E is not None:
                            second_out(E)
                        if A is not None:
                            scores(A, 3)
                        if C is not None:
                            second_probs_T(C, 1, 4)
                    if slot == 4:
                        if A is not None:
                            attend(A, 0, 1)
                        if A is not None:
                            scores(A, 4)
                        if B is not None:
                            second_scores(B, 0)
                        if C is not None:
                            contexts(C, 1)
                        if B is not None:
                            second_scores(B, 1)
                        if i == 2:
                            bias_to_columns()
                    if slot == 5:
                        if A is not None:
                            project_out(A, 0)
                            probs_T(A, 1)
                            project(A, 3)
                        if A2 is not None:
                            ffn_T(A2)
                        if C is not None:
                            second_probs_T(C, 2, 4)
                        if A is not None:
                            scores(A, 5)
                        if E is not None:
                            router_T(E)
                        if B is not None:
                            second_scores(B, 2)
                    if slot == 6:
                        if A is not None:
                            attend(A, 1, 1)
                        if A2 is not None:
                            hidden(A2)
                        if A is not None:
                            scores(A, 6)
                        if C is not None:
                            contexts(C, 2)
                        if A is not None:
                            project_out(A, 1)
                        if E is not None:
                            if i == 5:
                                pe.wait_ge(s["ld_router"], 32)
                            logits(E)
                    if slot == 7:
                        if A is not None:
                            probs_T(A, 2)
                        if A is not None:
                            scores(A, 7)
                        if B is not None:
                            second_scores(B, 3)
                        if i == 2:
                            down_weight_back()
                now["step"] += 1

            run_steps(pe, step)

            pe.wait_ge(s["c_past"], 2)
            pe.wait_ge(s["chosen_ready"], 1)
            places, totals = S0[:, 0:NB * NE], S1[:, 0:NE]
            rows = chosen[:, :, :].rearrange("p b e -> p (b e)")
            mm(places, before_p[:, :], rows, start=True, stop=False, skip_group_check=True)
            for k in range(1, NB):
                mm(S0[:, k * NE:NB * NE], ones_bf[:, :], rows[:, 0:(NB - k) * NE], start=False, stop=(k == NB - 1),
                   skip_group_check=True)
            for b in range(NB):
                last = mm(totals, ones_bf[:, :], chosen[:, b, :], start=(b == 0), stop=(b == NB - 1))
            last.then_inc(s["count_psum"], 1)

            pe.wait_ge(s["ld_w1"], 16)
            pe.wait_ge(s["ld_w2"], 16 * NE)
            pe.wait_ge(s["map_ready"], 1)
            pe.wait_ge(s["place_ready"], 1)

            def turn_group(n0, u):
                pe.wait_ge(s["z_loaded"], (n0 * 2 + u + 1) * 16)
                apart(pe)
                for n in range(GROUP):
                    last = turn(X[:, 128 * n:128 * n + 128], z_group[:, u, n, :])
                last.then_inc(s["xg_psum"], 1)

            def expert_of(n0, k):
                n = n0 * UNROLL + k
                return pe.value_load(tile_expert[0:1, bass.ds(n, 1)], min_val=0, max_val=NE - 1)

            def tile_up(n0, k, e):
                if k % GROUP == 0:
                    pe.wait_ge(s["xg_ready"], n0 * 2 + k // GROUP + 1)
                    apart(pe)
                mm(bank[k % 2][:, :], x_group[:, (k // GROUP) % 2, k % GROUP, :], w1[:, bass.ds(e, 1), :].squeeze(1),
                   start=True, stop=True).then_inc(s["up_psum"], 1)

            def tile_turn(n0, k):
                pe.wait_ge(s["gelu_ready"], n0 * UNROLL + k + 1)
                dst = bank[2 + k % 2]
                apart(pe)
                for c in range(HC):
                    last = turn(dst[:, 128 * c:128 * c + 128], h_exp[:, k % 2, 128 * c:128 * c + 128])
                last.then_inc(s["turned"], 1)

            def tile_down(n0, k, e):
                for c in range(HC):
                    if c % 2 == 0:
                        pe.wait_ge(s["hT_ready"], (n0 * UNROLL + k) * 2 + c // 2 + 1)
                        apart(pe)
                    last = mm(bank[4 + k % 2][:, 0:D], hT[:, k % 2, c, :], w2[:, bass.ds(e, 1), c, :].squeeze(1),
                              start=(c == 0), stop=(c == HC - 1))
                last.then_inc(s["ey_psum"], 1)

            def tiles(n0, last_k):
                e = expert_of(n0, 1)
                for k in range(1, last_k + 1):
                    tile_up(n0, k, e)
                    if k == 1:
                        before = expert_of(n0, 0)
                    if k % GROUP == 2 and (k < GROUP or last_k == UNROLL):
                        turn_group(n0 + (k > GROUP), (k < GROUP) * 1)
                    tile_down(n0, k - 1, before)
                    before = e
                    if k < last_k:
                        e = expert_of(n0, k + 1)
                    tile_turn(n0, k)
                return before

            TURNS = SORTED // UNROLL
            turn_group(0, 0)
            tile_up(0, 0, expert_of(0, 0))
            tile_turn(0, 0)
            with pe.Fori(0, TURNS - 1) as n0:
                tiles(n0, UNROLL)
            e = tiles(TURNS - 1, UNROLL - 1)
            tile_down(TURNS - 1, UNROLL - 1, e)

        @block.scalar
        def _(act):
            def fn(dst, src, f, **kw):
                return nc.scalar.activation(dst, src, f, **kw)

            def copy(dst, src):
                return fn(dst, src, ACT.Copy)

            move_jobs(act, range(0, JOBS, 2), copy, lambda d, v, c: fn(d, v, ACT.Copy, scale=c),
                      lambda d, v, b: fn(d, v, ACT.Identity, bias=b))
            act.wait_ge(s["ld_gates"], 32)
            fn(tg[:, :], gates[:, :], ACT.Tanh).then_inc(s["c_gate"], 1)

            def keys_out(b):
                reach(act, "kvt_psum", b, 1)
                copy(kvT[:, :], M[:, 0:KV]).then_inc(s["kvt_ready"], 1)

            def projected(b, q):
                reach(act, "g_psum", b, q + 1)
                copy(g_sb[:, q % 2, :, :].rearrange("p h q -> p (h q)"), GZ[:, :]).then_inc(s["g_ready"], 1)

            def exps(b, p):
                reach(act, "max_ready", b, p + 1)
                q = p // 2
                if p % 2 == 0:
                    reach(act, "pt_psum", b, q - 1)
                for n in range(2):
                    h = 2 * p + n
                    last = fn(prob[:, q % 2, 2 * (p % 2) + n, :], s_bank[p % 2][:, n * KV:(n + 1) * KV], ACT.Exp,
                              bias=negmax[:, h:h + 1], accum_out=rowsum[:, h:h + 1])
                last.then_inc(s["exp_done"], 1)

            def probs_out(b, q):
                reach(act, "pt_psum", b, q + 1)
                copy(ptc[:, :, :].rearrange("p h q -> p (h q)"), TC[0:NK, :])
                copy(ptl[:, :, :].rearrange("p h q -> p (h q)"), TL[:, :]).then_inc(s["pt_ready"], 1)

            def attended(b, q):
                reach(act, "z_psum", b, q + 1)
                copy(z_sb[:, :, :].rearrange("p h q -> p (h q)"), GZ[:, :]).then_inc(s["z_ready"], 1)

            def move(b, dst, psum, ready):
                reach(act, psum, b, 1)
                copy(dst[:, :], M[:, 0:128]).then_inc(s[ready], 1)

            def gelus(b):
                reach(act, "h_psum", b, 1)
                for n in range(HC):
                    last = fn(f_h[:, n, :], X[:, 128 * n:128 * n + 128], ACT.Gelu, bias=bias_cols[:, n:n + 1])
                last.then_inc(s["h_ready"], 1)

            def queries_out(b):
                reach(act, "q_psum", b, 1)
                fn(b_q[:, :], M[:, 0:128], ACT.Identity, bias=bq[:, 0:1]).then_inc(s["q_ready"], 1)

            def second_scores_out(b, q):
                reach(act, "sc_psum", b, q + 1)
                reach(act, "p1_ready", b, q + 1 - QUADS)
                copy(sw[:, 4 * q:4 * q + 4, 0, :], X[:, 0:4 * NK].rearrange("p (h n) -> p h n", h=4))\
                    .then_inc(s["sc_ready"], 1)

            def second_exps(b, q):
                reach(act, "sub_done", b, q + 1)
                v = sw[:, 4 * q:4 * q + 4, :, :].rearrange("p h w n -> p (h w n)")
                fn(v, v, ACT.Exp, scale=SC1).then_inc(s["e_done"], 1)

            def second_probs_out(b, q):
                reach(act, "p1T_psum", b, q + 1)
                copy(p1T[:, :, :].rearrange("p h q -> p (h q)"), X[0:NK, :]).then_inc(s["p1T_ready"], 1)

            def step(i, at):
                P, A, A2, B, C, E = (at(n) for n in range(6))
                for slot in range(SLOTS):
                    if slot == 0:
                        if A is not None:
                            keys_out(A)
                        if A2 is not None:
                            attended(A2, 2)
                        if A is not None:
                            projected(A, 0)
                        if E is not None:
                            second_probs_out(E, 3)
                        if A is not None:
                            exps(A, 0)
                    if slot == 1:
                        if A2 is not None:
                            probs_out(A2, 3)
                        if A is not None:
                            projected(A, 1)
                            exps(A, 1)
                        if C is not None:
                            second_probs_out(C, 0)
                    if slot == 2:
                        if A2 is not None:
                            attended(A2, 3)
                        if B is not None:
                            move(B, b_zT, "bT_psum", "bT_ready")
                        if C is not None:
                            second_exps(C, 1)
                        if A is not None:
                            exps(A, 2)
                        if B is not None:
                            queries_out(B)
                    if slot == 3:
                        if E is not None:
                            move(E, c_zT, "cT_psum", "cT_ready")
                        if A is not None:
                            projected(A, 2)
                            probs_out(A, 0)
                            exps(A, 3)
                        if C is not None:
                            second_probs_out(C, 1)
                    if slot == 4:
                        if A is not None:
                            attended(A, 0)
                        if B is not None:
                            second_scores_out(B, 0)
                        if C is not None:
                            second_exps(C, 2)
                        if A is not None:
                            exps(A, 4)
                        if B is not None:
                            second_scores_out(B, 1)
                        if i == 2:
                            act.wait_ge(s["late_psum"], 1)
                            copy(bias_cols[:, :], X[:, 0:HC]).then_inc(s["late_ready"], 1)
                    if slot == 5:
                        if A is not None:
                            probs_out(A, 1)
                            projected(A, 3)
                        if A2 is not None:
                            move(A2, f_zT, "fT_psum", "fT_ready")
                        if C is not None:
                            second_probs_out(C, 2)
                        if A is not None:
                            exps(A, 5)
                        if E is not None:
                            move(E, r_zT, "rT_psum", "rT_ready")
                        if B is not None:
                            second_scores_out(B, 2)
                        if C is not None:
                            second_exps(C, 3)
                    if slot == 6:
                        if A is not None:
                            attended(A, 1)
                        if A2 is not None:
                            if i == 2:
                                act.wait_ge(s["late_ready"], 1)
                            gelus(A2)
                        if A is not None:
                            exps(A, 6)
                    if slot == 7:
                        if A is not None:
                            probs_out(A, 2)
                        if A is not None:
                            exps(A, 7)
                        if B is not None:
                            second_scores_out(B, 3)
                            second_exps(B, 0)
                        if i == 2:
                            act.wait_ge(s["late_psum"], 2)
                            copy(w_dn[:, :, :].rearrange("p c d -> p (c d)"), X[:, :]).then_inc(s["late_ready"], 1)

            run_steps(act, step)

            act.wait_ge(s["lg_ready"], NB)
            fn(route[:, :, :], route[:, :, :], ACT.Exp, scale=-1.0).then_inc(s["r_exp"], 1)

            with act.Fori(0, SORTED // 2) as n0:
                for k in range(2):
                    act.wait_ge(s["up_psum"], n0 * 2 + k + 1)
                    fn(h_exp[:, k, :], bank[k][:, :], ACT.Gelu).then_inc(s["gelu_ready"], 1)

        @block.vector
        def _(dve):
            v = nc.vector

            def my_jobs(jobs):
                move_jobs(dve, jobs, v.tensor_copy, lambda d, x, c: v.tensor_scalar(d, x, c, None, ALU.mult),
                          lambda d, x, b: v.tensor_scalar(d, x, b, None, ALU.add),
                          lambda d, x: v.tensor_tensor(d, d, x, ALU.add))

            FIRST = 9
            my_jobs(range(1, FIRST, 2))
            dve.wait_ge(s["ld_c"], 16)
            for b in range(NB):
                v.bn_stats(st6c[:, b, :], cx[:, b, :]).then_inc(s["st_c"], 1)
            dve.wait_ge(s["st_c"], NB)
            for b in range(NB):
                v.bn_aggr(ln_c[:, b, :], st6c[:, b, :]).then_inc(s["st_c"], 1)
            dve.wait_ge(s["ld_x"], 16)
            for b in range(NB):
                v.bn_stats(st6[:, b, :], xs[:, b, :]).then_inc(s["st_x"], 1)
            dve.wait_ge(s["st_x"], NB)
            for b in range(NB):
                v.bn_aggr(ln_x[:, b, :], st6[:, b, :]).then_inc(s["st_x"], 1)
            dve.wait_ge(s["ld_mask"], 16)
            v.tensor_scalar(mask_row[:, :, :], mask_u8[:, :, :], 1.0, -MASKED, ALU.subtract, ALU.mult)\
                .then_inc(s["c_mask"], 1)
            my_jobs(range(FIRST, JOBS, 2))
            dve.wait_ge(s["c_gate"], 1)
            dve.wait_ge(s["ld_ffnb"], 32)
            v.tensor_tensor(ffn_bias[:, :], ffn_bias[:, :], dn_bias[:, :], ALU.add).then_inc(s["c_ffnb"], 1)
            wait_job(dve, J_BO)
            v.tensor_scalar(bo[:, :], bo[:, :], tg[:, 1:2], None, ALU.mult).then_inc(s["c_bo"], 1)
            dve.wait_ge(s["c_ffnb"], 1)
            v.tensor_scalar(ffn_bias[:, :], ffn_bias[:, :], tg[:, 2:3], None, ALU.mult).then_inc(s["c_ffnb"], 1)

            def up_stage(cur, part, n, mul, done, rows):
                w = 2 ** n
                nb = HID // (2 * w)
                if n == 0:
                    dve.wait_ge(s["ld_bfu"], 16)
                    dve.wait_ge(s["ld_wexp"], 48)
                else:
                    dve.wait_ge(s[done], n)
                for i in range(2):
                    v.tensor_tensor(pairs(part[:, i, :], nb), bf_coef(up_w, n, nb, "o w i")[0:rows, :, :, :, i],
                                    pairs(cur[:, :], nb)[:, :, i:i + 1, :].to_broadcast([rows, nb, 2, w]),
                                    ALU.mult).then_inc(s[mul], 1)
                dve.wait_ge(s[mul], 2 * n + 2)
                v.tensor_tensor(cur[:, :], part[:, 0, :], part[:, 1, :], ALU.add).then_inc(s[done], 1)

            def batch(a, b):
                return a[:, bass.ds(b, 1), :].squeeze(1)

            def maxima(b, p):
                reach(dve, "s_psum", b, p + 1)
                v.tensor_reduce(negmax[:, 2 * p:2 * p + 2], s_bank[p % 2][:, 0:2 * KV].rearrange("p (h n) -> p h n", h=2),
                                AX_X, ALU.max, negate=True).then_inc(s["max_ready"], 1)

            def inverses(b, q):
                reach(dve, "exp_done", b, 2 * q + 2)
                v.reciprocal(inv[:, 4 * q:4 * q + 4], rowsum[:, 4 * q:4 * q + 4]).then_inc(s["inv_ready"], 1)

            def residual(b, src, gate, ready):
                x = batch(xs, b)
                v.scalar_tensor_tensor(x, src, tg[:, gate:gate + 1], x, ALU.mult, ALU.add).then_inc(s[ready], 1)

            def statistics(b, st, mv, ready, done):
                reach(dve, ready, b, 1)
                apart(dve)
                v.bn_stats(st[:, :], batch(xs, b)).then_inc(s[done], 1)
                reach(dve, done, b, 1)
                apart(dve)
                v.bn_aggr(mv[:, :], st[:, :]).then_inc(s[done], 1)

            def normal(b, dst, mv, rs, rs_ready, done):
                reach(dve, rs_ready, b, 1)
                v.tensor_scalar(dst[:, :], batch(xs, b), mv[:, 0:1], rs[:, 0:1], ALU.subtract, ALU.mult).then_inc(s[done], 1)

            def top_32(b, k, between):
                if k % 2 == 0:
                    reach(dve, "sc_ready", b, k // 2 + 1)
                apart(dve)
                heads = (2 * k, 2 * k + 1)
                step = 0
                for r in range(ROUNDS):
                    if r == ROUNDS // 2:
                        between()
                    src = 0 if r == 0 else 1
                    for h in heads:
                        if r:
                            dve.wait_ge(s["topk_step"], step - 1)
                        v.max(m8[:, h, r, :], sw[:, h, src, :]).then_inc(s["topk_step"], 1)
                        step += 1
                    for h in heads:
                        dve.wait_ge(s["topk_step"], step - 1)
                        v.match_replace(sw[:, h, 1, :], m8[:, h, r, :], sw[:, h, src, :], TAKEN)\
                            .then_inc(s["topk_step"], 1)
                        step += 1
                dve.wait_ge(s["topk_step"], step)
                dve.sem_clear(s["topk_step"]).then_inc(s["topk_done"], 1)

            def context_out(b):
                reach(dve, "ctx_psum", b, QUADS)
                c = M[:, CT0:CT0 + H * (D1 + 1)].rearrange("p (h d) -> p h d", h=H)
                v.reciprocal(c_inv[:, :], c[:, :, D1]).then_inc(s["cinv_ready"], 1)
                reach(dve, "cinv_ready", b, 1)
                v.tensor_tensor(c_z[:, :, :], c[:, :, 0:D1], c_inv[:, :].unsqueeze(2).to_broadcast([128, H, D1]),
                                ALU.mult).then_inc(s["cz_ready"], 1)

            def step(i, at):
                P, A, A2, B, C, E = (at(n) for n in range(6))
                for slot in range(SLOTS):
                    if slot == 0 and B is not None:
                        reach(dve, "y_psum", B, 1)
                        reach(dve, "xb_added", B, 1)
                        residual(B, M[:, 0:D], 2, "x2_ready")
                        statistics(B, b_st, b_mv, "x2_ready", "b_stats")
                        normal(B, b_z, b_mv, b_rs, "brs_ready", "bz_ready")
                    if slot == 3 and A2 is not None:
                        reach(dve, "o_psum", A2, QUADS)
                        residual(A2, OA[:, 0:D], 0, "x1_ready")
                        statistics(A2, f_st, f_mv, "x1_ready", "f_stats")
                        normal(A2, f_z, f_mv, f_rs, "frs_ready", "fz_ready")
                    if slot == 7 and E is not None:
                        if i == 5:
                            dve.wait_ge(s["ld_router"], 32)
                        reach(dve, "lg_psum", E, 1)
                        v.tensor_tensor(batch(route, E), M[:, 0:NE], br[:, :], ALU.add).then_inc(s["lg_ready"], 1)
                    if A is not None:
                        maxima(A, slot)
                    if slot == 1 and E is not None:
                        context_out(E)
                    if slot == 3 and E is not None:
                        reach(dve, "o1_psum", E, 1)
                        reach(dve, "xo_added", E, 1)
                        residual(E, M[:, 0:D], 1, "x3_ready")
                        statistics(E, c_st, c_mv, "x3_ready", "c_stats")
                    if slot == 4 and E is not None:
                        reach(dve, "rz_kept", E, 0)
                        normal(E, r_z, c_mv, c_rs, "crs_ready", "rz_ready")
                    if slot == 3 and A is not None:
                        inverses(A, 1)

                    def between():
                        if slot in (1, 5, 7) and A is not None:
                            inverses(A, slot // 2)

                    if slot < 5 and C is not None:
                        top_32(C, slot + 3, between)
                    elif slot >= 5 and B is not None:
                        top_32(B, slot - 5, between)
                    else:
                        between()
                    n = UP_AT.get((i, slot))
                    if n is not None:
                        up_stage(w_up, up_t, n, "up_mul", "up_done", 128)
                        up_stage(bias_up, upb_t, n, "upb_mul", "upb_done", 1)
                    if n == NST - 1:
                        dve.wait_ge(s["upb_done"], NST)
                        v.tensor_tensor(bias_up[:, :], bias_up[:, :], up_bias[:, :], ALU.add).then_inc(s["upb_done"], 1)

            run_steps(dve, step)

            count = [0]

            def then(ins):
                count[0] += 1
                ins.then_inc(s["r_step"], 1)
                dve.wait_ge(s["r_step"], count[0])

            wide = [128, NB, NE]
            dve.wait_ge(s["r_exp"], 1)
            then(v.tensor_scalar(route[:, :, :], route[:, :, :], 1.0, None, ALU.add))
            then(v.reciprocal(route[:, :, :], route[:, :, :]))
            then(v.reduce_max(r_max[:, :], route[:, :, :], AX_X))
            then(v.tensor_tensor(r_eq[:, :, :], route[:, :, :], r_max[:, :].unsqueeze(2).to_broadcast(wide), ALU.is_equal))
            then(v.tensor_tensor(r_eq[:, :, :], r_eq[:, :, :], r_pri[:, :].unsqueeze(1).to_broadcast(wide), ALU.mult))
            then(v.reduce_max(r_top[:, :], r_eq[:, :, :], AX_X))
            v.tensor_tensor(chosen[:, :, :], r_eq[:, :, :], r_top[:, :].unsqueeze(2).to_broadcast(wide), ALU.is_equal)\
                .then_inc(s["chosen_ready"], 1)
            v.tensor_scalar(coef[:, :], r_max[:, :], tg[:, 3:4], None, ALU.mult).then_inc(s["coef_ready"], 1)

            dve.wait_ge(s["c_past"], 2)
            dve.wait_ge(s["count_psum"], 1)
            places, totals = S0[:, 0:NB * NE].rearrange("p (b e) -> p b e", b=NB), S1[:, 0:NE]
            then(v.tensor_tensor(n_full[:, :, :], totals.unsqueeze(2).to_broadcast([128, NE, NB]),
                                 steps_128[:, :].unsqueeze(1).to_broadcast([128, NE, NB]), ALU.is_gt))
            then(v.tensor_reduce(n_tiles[:, :], n_full[:, :, :], AX_X, ALU.add))
            then(v.tensor_tensor(n_before[:, :, :], before_e[:, :, :], n_tiles[:, :].unsqueeze(1).to_broadcast([128, NE, NE]),
                                 ALU.mult))
            then(v.tensor_reduce(start[:, :], n_before[:, :, :], AX_X, ALU.add))
            v.tensor_tensor(end[:, :], start[:, :], n_tiles[:, :], ALU.add)
            then(v.tensor_scalar(start[:, :], start[:, :], 128.0, None, ALU.mult))
            then(v.tensor_tensor(place_e[:, :, :], places, start[:, :].unsqueeze(1).to_broadcast(wide), ALU.add))
            then(v.tensor_tensor(place_e[:, :, :], place_e[:, :, :], chosen[:, :, :], ALU.mult))
            then(v.tensor_reduce(place_f[:, :], place_e[:, :, :], AX_X, ALU.add))
            v.tensor_copy(place[:, :], place_f[:, :]).then_inc(s["place_ready"], 1)
            then(v.tensor_tensor(t_past[:, :, :], tile_no[:, :].unsqueeze(2).to_broadcast([128, SORTED, NE]),
                                 end[:, :].unsqueeze(1).to_broadcast([128, SORTED, NE]), ALU.is_ge))
            then(v.tensor_reduce(t_exp[:, :], t_past[:, :, :], AX_X, ALU.add))
            v.tensor_scalar(tile_expert[:, :], t_exp[:, :], NE - 1.0, None, ALU.min).then_inc(s["map_ready"], 1)

            def output_out(n0, k):
                dve.wait_ge(s["ey_psum"], n0 * UNROLL + k + 1)
                apart(dve)
                v.tensor_copy(y_all[:, bass.ds(n0 * UNROLL + k, 1), :].squeeze(1), bank[4 + k % 2][:, 0:D])\
                    .then_inc(s["ey_ready"], 1)

            def group_out(n0, u):
                dve.wait_ge(s["xg_psum"], n0 * 2 + u + 1)
                v.tensor_copy(x_group[:, u, :, :].rearrange("p n q -> p (n q)"), X[:, :]).then_inc(s["xg_ready"], 1)

            def hidden_out(n0, k):
                dve.wait_ge(s["turned"], n0 * UNROLL + k + 1)
                for half_no in range(2):
                    c0 = half_no * HC // 2
                    v.tensor_copy(hT[:, k % 2, c0:c0 + HC // 2, :].rearrange("p c q -> p (c q)"),
                                  bank[2 + k % 2][:, 128 * c0:128 * c0 + HID // 2]).then_inc(s["hT_ready"], 1)

            def tiles(n0, last_k):
                for k in range(1, last_k + 1):
                    if k % GROUP == 2 and (k < GROUP or last_k == UNROLL):
                        group_out(n0 + (k > GROUP), (k < GROUP) * 1)
                    hidden_out(n0, k)
                    output_out(n0, k - 1)

            TURNS = SORTED // UNROLL
            group_out(0, 0)
            hidden_out(0, 0)
            with dve.Fori(0, TURNS - 1) as n0:
                tiles(n0, UNROLL)
            tiles(TURNS - 1, UNROLL - 1)
            output_out(TURNS - 1, UNROLL - 1)

            dve.wait_ge(s["coef_ready"], 1)
            for n in range(TILES):
                y, x = y_back[:, 4 * n:4 * n + 4, :], xs[:, 4 * n:4 * n + 4, :]
                dve.wait_ge(s[f"y_part{n}"], 64)
                v.tensor_tensor(y, y, coef[:, 4 * n:4 * n + 4].unsqueeze(2).to_broadcast([128, 4, D]), ALU.mult)\
                    .then_inc(s["y_times"], 1)
                dve.wait_ge(s["y_times"], n + 1)
                v.tensor_tensor(x, x, y, ALU.add).then_inc(s["tile_done"], 1)


INPUTS = ["x", "ctx_1024", "mask_BxS2_bk0", "g_xattn", "g_ffn", "L0_xattn_g1", "L0_xattn_b1", "L0_xattn_g2",
          "L0_xattn_b2", "L0_xattn_Wq", "L0_xattn_Wkv", "L0_xattn_Wout", "L0_ffn_W_exp", "L0_ffn_b_exp",
          "L0_ffn_up_weights", "L0_ffn_up_bias", "L0_ffn_down_weights", "L0_ffn_W_con", "L0_ffn_b_con",
          "L0_ffn_down_bias", "L1_xattn_Wq", "L1_xattn_bq", "L1_xattn_Wk", "L1_xattn_bk", "L1_xattn_Wv",
          "L1_xattn_bv", "L1_xattn_Wo", "L1_xattn_bo", "L1_ffn_Wr", "L1_ffn_br", "L1_ffn_W1", "L1_ffn_W2"]


def kernel(**inputs):
    import numpy as _np
    import concourse.bacc as _bacc
    from concourse.bass_utils import run_bass_kernel_spmd as _run

    nc = _bacc.Bacc("TRN2", target_bir_lowering=False, num_devices=1)
    arrays, t = {}, {}
    for name in INPUTS:
        a = _np.ascontiguousarray(inputs[name])
        arrays[f"in_{name}"] = a
        t[name] = nc.dram_tensor(f"in_{name}", a.shape, mybir.dt.from_np(a.dtype), kind="ExternalInput").ap()
    out = nc.dram_tensor("out_x", t["x"].shape, F32, kind="ExternalOutput").ap()
    flamingo_kernel(nc, t, out)
    r = _run(nc, [arrays], core_ids=[0])
    return r.results[0]["out_x"]
```
